# Optimizing a Trainium2 kernel written in Bass

```python
import numpy as np
import jax
import jax.numpy as jnp

def _softmax(x, axis=-1):
    return jax.nn.softmax(x, axis=axis)

def _gelu(x):
    return jax.nn.gelu(x, approximate=True)

def _silu(x):
    return jax.nn.silu(x)

def _sigmoid(x):
    return jax.nn.sigmoid(x)

def _layernorm(x, axis=-1, eps=1e-05):
    m = jnp.mean(x, axis=axis, keepdims=True)
    v = jnp.var(x, axis=axis, keepdims=True)
    return (x - m) / jnp.sqrt(v + eps)

def _scatter_add(tgt, idx, src, axis=0):
    return tgt.at[idx].add(src)

def _segment_sum(src, seg, n):
    return jax.ops.segment_sum(src, seg, n)
kernel_name = 'mk_flamingo_gated_d2_seqx_r8_a2e4cd'

def setup_inputs(seed: int=0):
    np.random.seed(seed)
    _w = jnp.asarray

    def _rec_inputs():
        import jax
        import jax.numpy as jnp
        _rk = jax.random.key(seed)
        x = -0.0002928 + 1 * jax.random.normal(jax.random.fold_in(_rk, 1), (32, 56, 128), jnp.float32)
        _lenS = 56 - jax.random.randint(jax.random.fold_in(_rk, 7), (32,), 0, max(1, 56 // 4) + 1, jnp.int32)
        _lenS2 = 1500 - jax.random.randint(jax.random.fold_in(_rk, 8), (32,), 0, max(1, 1500 // 4) + 1, jnp.int32)
        _ctx_1024P = jax.random.normal(jax.random.fold_in(_rk, 11), (32, 16, 128), jnp.float32)
        _ctx_1024c = jax.random.dirichlet(jax.random.fold_in(_rk, 511), 0.3 * jnp.ones((16,), jnp.float32), (32, 1500))
        _ctx_1024t = jnp.einsum('bsk,bkd->bsd', _ctx_1024c, _ctx_1024P)
        _ctx_1024t = _ctx_1024t * jax.lax.rsqrt(jnp.mean(jnp.square(_ctx_1024t)) + 1e-12) * 0.953939
        ctx_1024 = -1.39393e-06 + 0.999914 * (_ctx_1024t + 0.3 * jax.random.normal(jax.random.fold_in(_rk, 611), (32, 1500, 128), jnp.float32))
        _validS = jnp.arange(56)[None, :] < _lenS[:, None]
        _validS2 = jnp.arange(1500)[None, :] < _lenS2[:, None]
        _causal = jnp.tril(jnp.ones((56, 56), dtype=bool))
        mask_BxS2_ik0 = jnp.where(jnp.broadcast_to(_validS2[:, :], (32, 1500)), 0, 1).astype(jnp.int32)
        _g = jax.random.normal(jax.random.fold_in(_rk, 9001), (2, 2), jnp.float32)
        _g = jnp.sign(_g) * jnp.maximum(jnp.abs(_g), 1.0) + (_g == 0) * 1.0
        g_xattn = _g[0]
        g_ffn = _g[1]
        return (x, ctx_1024, mask_BxS2_ik0, g_xattn, g_ffn)
    x, ctx_1024, mask_BxS2_ik0, g_xattn, g_ffn = _rec_inputs()

    def _L0_xattn_setup():
        import jax, jax.numpy as jnp
        import numpy as np
        EMBED = 128
        HEADS = 16
        HEAD_DIM = EMBED // HEADS
        B, S = (2, 256)

        def _split_heads(x):
            b, s, _ = x.shape
            return x.reshape(b, s, HEADS, HEAD_DIM).transpose(0, 2, 1, 3)
        key = jax.random.key(seed)
        ks = jax.random.split(key, 11)
        sc = 1.0 / np.sqrt(EMBED)
        d = {'query': jax.random.normal(ks[0], (B, S, EMBED), jnp.float32), 'key': jax.random.normal(ks[1], (B, S, EMBED), jnp.float32), 'value': jax.random.normal(ks[2], (B, S, EMBED), jnp.float32), 'Wq': jax.random.normal(ks[3], (EMBED, EMBED), jnp.float32) * sc, 'bq': jnp.zeros((EMBED,), jnp.float32), 'Wk': jax.random.normal(ks[4], (EMBED, EMBED), jnp.float32) * sc, 'bk': jnp.zeros((EMBED,), jnp.float32), 'Wv': jax.random.normal(ks[5], (EMBED, EMBED), jnp.float32) * sc, 'bv': jnp.zeros((EMBED,), jnp.float32), 'Wo': jax.random.normal(ks[6], (EMBED, EMBED), jnp.float32) * sc, 'bo': jnp.zeros((EMBED,), jnp.float32)}
        return d
    _L0_xattn_all = _L0_xattn_setup()
    _L0_xattn_in = {k: v for k, v in _L0_xattn_all.items() if k in ('Wq', 'bq', 'Wk', 'bk', 'Wv', 'bv', 'Wo', 'bo')}
    del _L0_xattn_all

    def _L0_ffn_setup():
        import jax, jax.numpy as jnp
        import numpy as np
        EPS = 1e-05

        def rmsnorm(x):
            return x * jax.lax.rsqrt(jnp.mean(x * x, axis=-1, keepdims=True) + EPS)

        def act_quant(x):
            scale = 127.0 / jnp.clip(jnp.max(jnp.abs(x), axis=-1, keepdims=True), 1e-05)
            q = jnp.clip(jnp.round(x * scale), -128.0, 127.0) / scale
            return x + jax.lax.stop_gradient(q - x)

        def weight_quant(w):
            scale = 1.0 / jnp.clip(jnp.mean(jnp.abs(w)), 1e-05)
            q = jnp.clip(jnp.round(w * scale), -1.0, 1.0) / scale
            return w + jax.lax.stop_gradient(q - w)

        def bitlinear(x, w, b):
            xq = act_quant(rmsnorm(x))
            wq = weight_quant(w)
            return jnp.einsum('bsd,fd->bsf', xq, wq) + b
        key = jax.random.key(seed)
        k0, k1, k2 = jax.random.split(key, 3)
        B, S, D, F = (2, 1024, 128, 512)
        x = jax.random.normal(k0, (B, S, D), dtype=jnp.float32)
        w1 = jax.random.normal(k1, (F, D), dtype=jnp.float32) * (1.0 / np.sqrt(D))
        b1 = jnp.zeros((F,), dtype=jnp.float32)
        w2 = jax.random.normal(k2, (D, F), dtype=jnp.float32) * (1.0 / np.sqrt(F))
        b2 = jnp.zeros((D,), dtype=jnp.float32)
        return {'x': x, 'w1': w1, 'b1': b1, 'w2': w2, 'b2': b2}
    _L0_ffn_all = _L0_ffn_setup()
    _L0_ffn_in = {k: v for k, v in _L0_ffn_all.items() if k in ('w1', 'b1', 'w2', 'b2')}
    del _L0_ffn_all

    def _L1_xattn_setup():
        import jax, jax.numpy as jnp
        import numpy as np
        DIM = 128
        HEADS = 16
        HEAD_DIM = DIM // HEADS
        SCALE = HEAD_DIM ** (-0.5)
        MASK_FILL = -1000000000.0

        def layer_norm(x, gamma, beta, eps=1e-05):
            mu = jnp.mean(x, axis=-1, keepdims=True)
            var = jnp.var(x, axis=-1, keepdims=True)
            return (x - mu) * jax.lax.rsqrt(var + eps) * gamma + beta
        key = jax.random.key(seed)
        ks = jax.random.split(key, 10)
        B, N1, N2, C = (8, 32, 512, DIM)
        s = C ** (-0.5)
        return {'x': jax.random.normal(ks[0], (B, N1, C), jnp.float32), 'kv': jax.random.normal(ks[1], (B, N2, C), jnp.float32), 'padding_mask': jax.random.randint(ks[2], (B, N2), 0, 2, jnp.int32), 'w_q': jax.random.normal(ks[3], (C, C), jnp.float32) * s, 'w_kv': jax.random.normal(ks[4], (C, 2 * C), jnp.float32) * s, 'w_proj': jax.random.normal(ks[5], (C, C), jnp.float32) * s, 'b_proj': jnp.zeros((C,), jnp.float32), 'g_x': jnp.ones((C,), jnp.float32), 'b_x': jnp.zeros((C,), jnp.float32), 'g_kv': jnp.ones((C,), jnp.float32), 'b_kv': jnp.zeros((C,), jnp.float32)}
    _L1_xattn_all = _L1_xattn_setup()
    _L1_xattn_in = {k: v for k, v in _L1_xattn_all.items() if k in ('w_q', 'w_kv', 'w_proj', 'b_proj', 'g_x', 'b_x', 'g_kv', 'b_kv')}
    del _L1_xattn_all

    def _L1_ffn_setup():
        import jax, jax.numpy as jnp
        import numpy as np
        TOP_K = 2
        EPS = 1e-05

        def layer_norm(x, g, b):
            mu = jnp.mean(x, axis=-1, keepdims=True)
            var = jnp.mean(jnp.square(x - mu), axis=-1, keepdims=True)
            return (x - mu) * jax.lax.rsqrt(var + EPS) * g + b
        key = jax.random.key(seed)
        ks = jax.random.split(key, 12)
        B, S, D, F, E = (2, 256, 128, 512, 8)
        std = 0.02
        return {'x': jax.random.normal(ks[0], (B, S, D), jnp.float32), 'g1': jnp.ones((D,), jnp.float32), 'be1': jnp.zeros((D,), jnp.float32), 'mix_w': jax.random.normal(ks[1], (D, D), jnp.float32) * std, 'mix_b': jnp.zeros((D,), jnp.float32), 'g2': jnp.ones((D,), jnp.float32), 'be2': jnp.zeros((D,), jnp.float32), 'router_w': jax.random.normal(ks[2], (D, E), jnp.float32) * std, 'w1': jax.random.normal(ks[3], (E, D, F), jnp.float32) * std, 'b1': jnp.zeros((E, F), jnp.float32), 'w2': jax.random.normal(ks[4], (E, F, D), jnp.float32) * std, 'b2': jnp.zeros((E, D), jnp.float32)}
    _L1_ffn_all = _L1_ffn_setup()
    _L1_ffn_in = {k: v for k, v in _L1_ffn_all.items() if k in ('g1', 'be1', 'mix_w', 'mix_b', 'g2', 'be2', 'router_w', 'w1', 'b1', 'w2', 'b2')}
    del _L1_ffn_all
    return {'x': x, 'ctx_1024': ctx_1024, 'mask_BxS2_ik0': mask_BxS2_ik0, 'g_xattn': g_xattn, 'g_ffn': g_ffn, 'L0_xattn_Wq': _L0_xattn_in['Wq'], 'L0_xattn_bq': _L0_xattn_in['bq'], 'L0_xattn_Wk': _L0_xattn_in['Wk'], 'L0_xattn_bk': _L0_xattn_in['bk'], 'L0_xattn_Wv': _L0_xattn_in['Wv'], 'L0_xattn_bv': _L0_xattn_in['bv'], 'L0_xattn_Wo': _L0_xattn_in['Wo'], 'L0_xattn_bo': _L0_xattn_in['bo'], 'L0_ffn_w1': _L0_ffn_in['w1'], 'L0_ffn_b1': _L0_ffn_in['b1'], 'L0_ffn_w2': _L0_ffn_in['w2'], 'L0_ffn_b2': _L0_ffn_in['b2'], 'L1_xattn_w_q': _L1_xattn_in['w_q'], 'L1_xattn_w_kv': _L1_xattn_in['w_kv'], 'L1_xattn_w_proj': _L1_xattn_in['w_proj'], 'L1_xattn_b_proj': _L1_xattn_in['b_proj'], 'L1_xattn_g_x': _L1_xattn_in['g_x'], 'L1_xattn_b_x': _L1_xattn_in['b_x'], 'L1_xattn_g_kv': _L1_xattn_in['g_kv'], 'L1_xattn_b_kv': _L1_xattn_in['b_kv'], 'L1_ffn_g1': _L1_ffn_in['g1'], 'L1_ffn_be1': _L1_ffn_in['be1'], 'L1_ffn_mix_w': _L1_ffn_in['mix_w'], 'L1_ffn_mix_b': _L1_ffn_in['mix_b'], 'L1_ffn_g2': _L1_ffn_in['g2'], 'L1_ffn_be2': _L1_ffn_in['be2'], 'L1_ffn_router_w': _L1_ffn_in['router_w'], 'L1_ffn_w1': _L1_ffn_in['w1'], 'L1_ffn_b1': _L1_ffn_in['b1'], 'L1_ffn_w2': _L1_ffn_in['w2'], 'L1_ffn_b2': _L1_ffn_in['b2']}

def reference(x, ctx_1024, mask_BxS2_ik0, g_xattn, g_ffn, L0_xattn_Wq, L0_xattn_bq, L0_xattn_Wk, L0_xattn_bk, L0_xattn_Wv, L0_xattn_bv, L0_xattn_Wo, L0_xattn_bo, L0_ffn_w1, L0_ffn_b1, L0_ffn_w2, L0_ffn_b2, L1_xattn_w_q, L1_xattn_w_kv, L1_xattn_w_proj, L1_xattn_b_proj, L1_xattn_g_x, L1_xattn_b_x, L1_xattn_g_kv, L1_xattn_b_kv, L1_ffn_g1, L1_ffn_be1, L1_ffn_mix_w, L1_ffn_mix_b, L1_ffn_g2, L1_ffn_be2, L1_ffn_router_w, L1_ffn_w1, L1_ffn_b1, L1_ffn_w2, L1_ffn_b2):
    import jax
    import jax.numpy as jnp

    def _L0_xattn_ref(query, key, value, Wq, bq, Wk, bk, Wv, bv, Wo, bo):
        import jax, jax.numpy as jnp
        import numpy as np
        EMBED = 128
        HEADS = 16
        HEAD_DIM = EMBED // HEADS
        B, S = (2, 256)

        def _split_heads(x):
            b, s, _ = x.shape
            return x.reshape(b, s, HEADS, HEAD_DIM).transpose(0, 2, 1, 3)
        q = _split_heads(query @ Wq.T + bq)
        k = _split_heads(key @ Wk.T + bk)
        v = _split_heads(value @ Wv.T + bv)
        scale = 1.0 / np.sqrt(HEAD_DIM).astype(np.float32)
        attn = jnp.einsum('bhqd,bhkd->bhqk', q, k) * scale
        attn = jax.nn.softmax(attn, axis=-1)
        out = jnp.einsum('bhqk,bhkd->bhqd', attn, v)
        out = out.transpose(0, 2, 1, 3).reshape(query.shape[0], -1, EMBED)
        return out @ Wo.T + bo

    def _L0_ffn_ref(x, w1, b1, w2, b2):
        import jax, jax.numpy as jnp
        import numpy as np
        EPS = 1e-05

        def rmsnorm(x):
            return x * jax.lax.rsqrt(jnp.mean(x * x, axis=-1, keepdims=True) + EPS)

        def act_quant(x):
            scale = 127.0 / jnp.clip(jnp.max(jnp.abs(x), axis=-1, keepdims=True), 1e-05)
            q = jnp.clip(jnp.round(x * scale), -128.0, 127.0) / scale
            return x + jax.lax.stop_gradient(q - x)

        def weight_quant(w):
            scale = 1.0 / jnp.clip(jnp.mean(jnp.abs(w)), 1e-05)
            q = jnp.clip(jnp.round(w * scale), -1.0, 1.0) / scale
            return w + jax.lax.stop_gradient(q - w)

        def bitlinear(x, w, b):
            xq = act_quant(rmsnorm(x))
            wq = weight_quant(w)
            return jnp.einsum('bsd,fd->bsf', xq, wq) + b
        h = bitlinear(x, w1, b1)
        h = jax.nn.gelu(h, approximate=False)
        return bitlinear(h, w2, b2)

    def _L1_xattn_ref(x, kv, padding_mask, w_q, w_kv, w_proj, b_proj, g_x, b_x, g_kv, b_kv):
        import jax, jax.numpy as jnp
        import numpy as np
        DIM = 128
        HEADS = 16
        HEAD_DIM = DIM // HEADS
        SCALE = HEAD_DIM ** (-0.5)
        MASK_FILL = -1000000000.0

        def layer_norm(x, gamma, beta, eps=1e-05):
            mu = jnp.mean(x, axis=-1, keepdims=True)
            var = jnp.var(x, axis=-1, keepdims=True)
            return (x - mu) * jax.lax.rsqrt(var + eps) * gamma + beta
        B, N1, C = x.shape
        N2 = kv.shape[1]
        xn = layer_norm(x, g_x, b_x)
        kvn = layer_norm(kv, g_kv, b_kv)
        q = (xn @ w_q).reshape(B, N1, HEADS, HEAD_DIM).transpose(0, 2, 1, 3)
        kv_proj = (kvn @ w_kv).reshape(B, N2, 2, HEADS, HEAD_DIM).transpose(2, 0, 3, 1, 4)
        k, v = (kv_proj[0], kv_proj[1])
        attn = jnp.einsum('bhqd,bhkd->bhqk', q, k) * SCALE
        mask = padding_mask[:, None, None, :]
        attn = jnp.where(mask == 0, MASK_FILL, attn)
        attn = jax.nn.softmax(attn, axis=-1)
        out = jnp.einsum('bhqk,bhkd->bhqd', attn, v)
        out = out.transpose(0, 2, 1, 3).reshape(B, N1, C)
        return out @ w_proj + b_proj

    def _L1_ffn_ref(x, g1, be1, mix_w, mix_b, g2, be2, router_w, w1, b1, w2, b2):
        import jax, jax.numpy as jnp
        import numpy as np
        TOP_K = 2
        EPS = 1e-05

        def layer_norm(x, g, b):
            mu = jnp.mean(x, axis=-1, keepdims=True)
            var = jnp.mean(jnp.square(x - mu), axis=-1, keepdims=True)
            return (x - mu) * jax.lax.rsqrt(var + EPS) * g + b
        res = x
        n = layer_norm(x, g1, be1)
        x = res + n + (n @ mix_w + mix_b)
        res = x
        n = layer_norm(x, g2, be2)
        B, S, D = n.shape
        E = w1.shape[0]
        flat = n.reshape(-1, D)
        probs = jax.nn.softmax(flat @ router_w, axis=-1)
        topw, topi = jax.lax.top_k(probs, TOP_K)
        combine = jnp.sum(jax.nn.one_hot(topi, E, dtype=flat.dtype) * topw[..., None], axis=1)
        h = jax.nn.silu(jnp.einsum('td,edf->tef', flat, w1) + b1)
        y = jnp.einsum('tef,efd->ted', h, w2) + b2
        out = jnp.einsum('te,ted->td', combine, y)
        return res + out.reshape(B, S, D)
    x = x + jnp.tanh(g_xattn[0]) * _L0_xattn_ref(_layernorm(x, axis=-1), ctx_1024, ctx_1024, L0_xattn_Wq, L0_xattn_bq, L0_xattn_Wk, L0_xattn_bk, L0_xattn_Wv, L0_xattn_bv, L0_xattn_Wo, L0_xattn_bo)
    x = x + jnp.tanh(g_ffn[0]) * _L0_ffn_ref(_layernorm(x, axis=-1), L0_ffn_w1, L0_ffn_b1, L0_ffn_w2, L0_ffn_b2)
    x = x + jnp.tanh(g_xattn[1]) * _L1_xattn_ref(_layernorm(x, axis=-1), ctx_1024, mask_BxS2_ik0, L1_xattn_w_q, L1_xattn_w_kv, L1_xattn_w_proj, L1_xattn_b_proj, L1_xattn_g_x, L1_xattn_b_x, L1_xattn_g_kv, L1_xattn_b_kv)
    x = x + jnp.tanh(g_ffn[1]) * _L1_ffn_ref(_layernorm(x, axis=-1), L1_ffn_g1, L1_ffn_be1, L1_ffn_mix_w, L1_ffn_mix_b, L1_ffn_g2, L1_ffn_be2, L1_ffn_router_w, L1_ffn_w1, L1_ffn_b1, L1_ffn_w2, L1_ffn_b2)
    return x

_drawn_inputs = setup_inputs


def setup_inputs(seed=0):
    import zlib

    import numpy as np

    out = dict(_drawn_inputs(seed))
    spreads = {'g_ffn': (-1.0, 0.2),
     'L0_xattn_bq': (0.0, 0.437),
     'L0_xattn_bk': (0.0, 0.8),
     'L0_xattn_bv': (0.0, 0.1),
     'L0_xattn_bo': (0.0, 0.1),
     'L0_ffn_b1': (0.0, 0.1),
     'L0_ffn_b2': (0.0, 0.1),
     'L1_xattn_b_proj': (0.0, 0.1),
     'L1_xattn_g_x': (1.0, 0.2),
     'L1_xattn_b_x': (0.0, 0.504),
     'L1_xattn_g_kv': (1.0, 0.2),
     'L1_xattn_b_kv': (0.0, 0.1),
     'L1_ffn_g1': (1.0, 0.2),
     'L1_ffn_be1': (0.0, 0.1),
     'L1_ffn_mix_b': (0.0, 0.1),
     'L1_ffn_g2': (1.0, 0.6),
     'L1_ffn_be2': (0.0, 0.456),
     'L1_ffn_b1': (0.0, 0.8),
     'L1_ffn_b2': (0.0, 0.1)}
    factors = {}
    for name, (base, spread) in spreads.items():
        noise = np.random.default_rng([zlib.crc32(name.encode()), seed]).standard_normal(out[name].shape)
        drawn = base * np.exp(spread * noise) if base else spread * noise
        out[name] = jnp.asarray(drawn.astype(out[name].dtype))
    for name, factor in factors.items():
        out[name] = (out[name] * factor).astype(out[name].dtype)
    return out
```

```python
from contextlib import ExitStack

import concourse.bass as bass
from concourse import mybir

F32 = mybir.dt.float32
BF16 = mybir.dt.bfloat16
I32 = mybir.dt.int32
ACT = mybir.ActivationFunctionType
ALU = mybir.AluOpType
AX = mybir.AxisListType

D = 128
HEADS = 16
HD = D // HEADS
S = 56
CTX = 1500
P = 128
KT = -(-CTX // P)
LAST = CTX - (KT - 1) * P
PAIRS = HEADS // 2
PR = 2 * HD
PQ = 2 * S
PARTS_K = (0, 1, 2, 0, 1, 0)
PARTS_Q = (0, 0, 0, 1, 1, 2)
TERMS = len(PARTS_K)
SPLIT = TERMS * PR
FILLED = SPLIT + 3
STACK = FILLED + 3
CH = 500
NCH = CTX // CH
VW = PR + 1
TOK = 2 * S
EPS = 1e-5
SCALE = float(HD) ** -0.5
FILL = (998244352.0, 1753088.0, 2560.0)
MAGIC = 12582912.0
F0 = 512
FT = F0 // P
E = 8
GT = 4
GC = GT * TOK

MATS = ("wq0", "wk0", "wv0", "wo0", "wq1", "wk1", "wv1", "wo1", "mix", "ident", "pick",
        "woh0a", "woh0b", "woh0c", "woh0d", "woh1a", "woh1b", "woh1c", "woh1d",
        "fa", "fb", "fc", "fd", "ga", "gb", "gc", "gd")
COLS = ("bq0", "bk0", "bv0", "g_x", "b_x", "g_kv", "b_kv", "g2", "be2", "even", "odd")
ROWS = (("bo0", D), ("b2", D), ("b1", F0), ("bo1", D), ("g1", D), ("be1", D), ("mix_b", D), ("gates", 4))
ROW_AT = {}
for _name, _width in ROWS:
    ROW_AT[_name] = sum(w for _, w in ROWS[:len(ROW_AT)])
ROW_W = sum(w for _, w in ROWS)
RING = 3


class Shared:
    pass


class Step:

    def __init__(self, lap, u, first, laps, make, peak, mix):
        self.lap, self.u, self.first, self.laps = lap, u, first, laps
        self.make, self.peak, self.mix = make, peak, mix

    def batch(self, ahead):
        return 3 * self.lap + (self.u + ahead)

    def buf(self, ahead):
        return (self.u + ahead) % 3

    def use(self, ahead):
        return self.lap + (self.u + ahead) // 3

    def items(self):
        out = []
        for kt in range(KT):
            if self.mix:
                out.append(("score", kt, 0))
            if self.peak and kt < PAIRS:
                out += [("peak", kt, j) for j in range(NCH)]
            if self.peak and kt == PAIRS + 1:
                out += [("shift", 0, 0), ("shift", 1, 0)]
            if self.make:
                out += {3: [("turn", 0, 0)], 4: [("turn", 1, 0)], 5: [("turn", 2, 0), ("key", 0, 0)],
                        6: [("key", 1, 0)], 7: [("key", 2, 0)]}.get(kt, [])
            if self.mix and kt:
                out.append(("mix", kt - 1, 0))
        if self.mix:
            out.append(("mix", KT - 1, 0))
        if self.make:
            out += [("value", 0, 0), ("value", 1, 0)]
        if self.mix:
            out.append(("total", 0, 0))
        if self.make:
            out.append(("value", 2, 0))
        if self.mix:
            out.append(("project", 0, 0))
        return out

    def slots(self):
        n, out = 0, []
        for kind, a, b in self.items():
            if kind in ("score", "mix"):
                out.append((kind, a, b, 0, 0))
            else:
                at = self.first + n
                out.append((kind, a, b, at % RING, at // RING + self.laps))
                n += 1
        return out

    def width(self):
        return sum(kind not in ("score", "mix") for kind, _, _ in self.items())


def run_steps(eng, nb, body):
    first = 0
    for s in (-2, -1):
        step = Step(-1, s + 3, first, 0, True, s == -1, False)
        body(step)
        first += step.width()
    steady = Step(0, 0, 0, 0, True, True, True).width()
    with eng.Fori(0, (nb - 2) // 3) as lap:
        for u in range(3):
            body(Step(lap, u, first + u * steady, lap * steady, True, True, True))
    first += (nb - 2) * steady
    for s in (nb - 2, nb - 1):
        step = Step(s // 3, s % 3, first, 0, False, s == nb - 2, True)
        body(step)
        first += step.width()


def rows_of(kt):
    return P if kt < KT - 1 else LAST


def setup(nc, m):
    with ExitStack() as ctx:
        mask = ctx.enter_context(nc.sbuf_tensor("mask", [m.nb, CTX], I32))
        keep = ctx.enter_context(nc.sbuf_tensor("keep", [m.nb, CTX], BF16))
        fill = ctx.enter_context(nc.sbuf_tensor("fill", [m.nb, 3, CTX], BF16))
        loaded = ctx.enter_context(nc.semaphore("setup_loaded"))
        mask_loaded = ctx.enter_context(nc.semaphore("mask_loaded"))
        made = ctx.enter_context(nc.semaphore("masks_made"))
        saved = ctx.enter_context(nc.semaphore("masks_saved"))
        tanhs = ctx.enter_context(nc.semaphore("tanhs"))
        block = ctx.enter_context(nc.Block())

        @block.sync
        def _(sp):
            sp.dma_start(mask[:, :], m.mask_dram).then_inc(mask_loaded, 16)
            sp.dma_start(m.x[:, :, :], m.x_dram.rearrange("b s d -> (b s) d").rearrange(
                "(n p) d -> p n d", p=TOK)).then_inc(loaded, 16)
            sp.dma_start(m.mats[:, :], m.mats_dram).then_inc(loaded, 16)
            sp.dma_start(m.cols[:, :], m.cols_dram).then_inc(loaded, 16)
            sp.dma_start(m.rows[:, :], m.rows_dram.partition_broadcast(P)).then_inc(loaded, 16)
            sp.dma_start(m.router[:, :], m.router_dram).then_inc(loaded, 16)
            sp.dma_start(m.b2e[:, :], m.b2e_dram).then_inc(loaded, 16)
            sp.wait_ge(made, 4)
            sp.dma_start(m.keep_dram, keep[:, :]).then_inc(saved, 16)
            sp.dma_start(m.fill_dram, fill[:, :, :]).then_inc(saved, 16)
            sp.wait_ge(loaded, 16 * 6)
            sp.wait_ge(saved, 32)

        @block.vector
        def _(dve):
            dve.wait_ge(mask_loaded, 16)
            nc.vector.tensor_scalar(keep[:, :], mask[:, :], 0.0, None, ALU.not_equal).then_inc(made, 1)
            dve.wait_ge(made, 1)
            for n in range(3):
                nc.vector.tensor_scalar(fill[:, n, :], keep[:, :], 1.0, FILL[n], ALU.subtract, ALU.mult)\
                    .then_inc(made, 1)

        @block.scalar
        def _(act):
            act.wait_ge(loaded, 16 * 6)
            nc.scalar.activation(m.identb[:, :], mat(m, "ident"), ACT.Copy).then_inc(tanhs, 1)
            nc.scalar.activation(m.gates[:, :], m.rows[:, ROW_AT["gates"]:ROW_AT["gates"] + 4], ACT.Tanh)\
                .then_inc(tanhs, 1)
            act.wait_ge(tanhs, 2)


def mat(m, name):
    at = MATS.index(name) * P
    return m.mats[:, at:at + P]


def col(m, name):
    at = COLS.index(name)
    return m.cols[:, at:at + 1]


def row(m, name, p=P):
    at = ROW_AT[name]
    return m.rows[0:p, at:at + dict(ROWS)[name]]


def per_token(ap, nt, width=D):
    return ap.unsqueeze(2).to_broadcast([TOK, nt, width])


def per_channel(ap, nt, width=D):
    return ap.unsqueeze(1).to_broadcast([TOK, nt, width])


class Chain:

    def __init__(self, eng, sem):
        self.eng, self.sem, self.n = eng, sem, 0

    def then(self, ins):
        self.n += 1
        ins.then_inc(self.sem, 1)
        self.eng.wait_ge(self.sem, self.n)

    def mark(self, ins):
        self.n += 1
        ins.then_inc(self.sem, 1)
        return self.n


def norm_vector(nc, dve, chain, roots, src, dst, tmp, st, nt, turn):
    chain.then(nc.vector.tensor_reduce(st[:, 0, :], src, AX.X, ALU.add))
    chain.then(nc.vector.tensor_scalar(st[:, 1, :], st[:, 0, :], 1.0 / D, None, ALU.mult))
    chain.then(nc.vector.tensor_tensor(dst, src, per_token(st[:, 1, :], nt), ALU.subtract))
    chain.then(nc.vector.tensor_tensor(tmp, dst, dst, ALU.mult))
    chain.then(nc.vector.tensor_reduce(st[:, 2, :], tmp, AX.X, ALU.add))
    dve.wait_ge(roots, turn)
    chain.then(nc.vector.reciprocal(st[:, 4, :], st[:, 3, :]))
    chain.then(nc.vector.tensor_tensor(dst, dst, per_token(st[:, 4, :], nt), ALU.mult))


NORM_LINKS = 7
NORM_SUM = 5


def norm_scalar(nc, act, m, chain_sem, at, roots, st):
    act.wait_ge(chain_sem, at)
    nc.scalar.activation(st[:, 3, :], st[:, 2, :], ACT.Sqrt, bias=m.eps[0:TOK, 0:1], scale=1.0 / D)\
        .then_inc(roots, 1)


def queries(nc, m, layer):
    nt, ng = m.nt, m.nt // GT if m.nt >= GT else 1
    gt = min(GT, m.nt)
    gc = gt * TOK
    L = str(layer)
    norms = 1 + layer
    cols = nt * TOK
    with ExitStack() as ctx:
        def sb(name, shape, dt):
            return ctx.enter_context(nc.sbuf_tensor(f"q{L}_{name}", shape, dt))

        def sem(name):
            return ctx.enter_context(nc.semaphore(f"q{L}_{name}"))

        z = sb("z", [TOK, nt, D], F32)
        sq = sb("sq", [TOK, nt, D], F32)
        st = sb("st", [TOK, 5, nt], F32)
        zT = sb("zT", [P, cols], F32)
        qf = sb("qf", [P, cols], F32)
        rest = sb("rest", [P, cols], F32)
        part = sb("part", [P, 3, cols], BF16)
        block_q = sb("block_q", [P, 3, m.nb, PQ], BF16)
        wq = sb("wq", [P, P], F32)
        bq = sb("bq", [P, 1], F32)
        bvb = sb("bvb", [P, TOK], F32)
        turned = [ctx.enter_context(nc.psum_tensor(f"q{L}_turned{g}", [P, 512], F32)) for g in range(ng)]
        qps = ctx.enter_context(nc.psum_tensor(f"q{L}_qps", [P, 2, 512], F32))
        small = ctx.enter_context(nc.psum_tensor(f"q{L}_small", [P, 512], F32))
        normed, roots, turns, turns_out = sem("normed"), sem("roots"), sem("turns"), sem("turns_out")
        folded, biases = sem("folded"), sem("biases")
        projected, steps, blocks, saved = sem("projected"), sem("steps"), sem("blocks"), sem("saved")
        eps_set = sem("eps_set")
        block = ctx.enter_context(nc.Block())
        last_norm = NORM_LINKS * norms

        @block.vector
        def _(dve):
            if layer == 0:
                nc.vector.memset(m.eps[:, :], EPS).then_inc(eps_set, 1)
            chain = Chain(dve, normed)
            src = m.x
            for n in range(norms):
                norm_vector(nc, dve, chain, roots, src[:, :, :], z[:, :, :], sq[:, :, :], st, nt, n + 1)
                src = z
            if layer == 0:
                nc.vector.tensor_copy(wq[:, :], mat(m, "wq0")).then_inc(folded, 1)
                nc.vector.tensor_copy(m.wk[0][:, :], mat(m, "wk0")).then_inc(folded, 1)
                nc.vector.tensor_copy(m.wv[0][:, :], mat(m, "wv0")).then_inc(folded, 1)
                nc.vector.tensor_copy(bq[:, :], col(m, "bq0")).then_inc(folded, 1)
                nc.vector.tensor_copy(m.bk[0][:, :], col(m, "bk0")).then_inc(folded, 1)
                nc.vector.tensor_copy(bvb[:, :], col(m, "bv0").to_broadcast([P, TOK])).then_inc(folded, 1)
            else:
                nc.vector.tensor_scalar(wq[:, :], mat(m, "wq1"), col(m, "g_x"), None, ALU.mult).then_inc(folded, 1)
                nc.vector.tensor_scalar(m.wk[1][:, :], mat(m, "wk1"), col(m, "g_kv"), None, ALU.mult).then_inc(folded, 1)
                nc.vector.tensor_scalar(m.wv[1][:, :], mat(m, "wv1"), col(m, "g_kv"), None, ALU.mult).then_inc(folded, 1)
                dve.wait_ge(biases, 1)
                nc.vector.tensor_copy(bq[:, :], small[:, 0:1]).then_inc(folded, 1)
                nc.vector.tensor_copy(m.bk[1][:, :], small[:, 1:2]).then_inc(folded, 1)
                nc.vector.tensor_copy(bvb[:, :], small[:, 2:3].to_broadcast([P, TOK])).then_inc(folded, 1)
            dve.wait_ge(biases, 2)
            nc.vector.tensor_tensor(m.yb[layer][:, :], small[0:TOK, 128:256], row(m, "bo" + L, TOK), ALU.add)\
                .then_inc(folded, 1)
            done = Chain(dve, steps)
            for g in range(ng):
                dve.wait_ge(projected, g + 1)
                dve.wait_ge(folded, 4)
                nc.vector.tensor_scalar(qf[:, g * gc:(g + 1) * gc], qps[:, g % 2, 0:gc], bq[:, 0:1], SCALE,
                                        ALU.add, ALU.mult).then_inc(steps, 1)
            done.n = ng
            dve.wait_ge(steps, ng)
            done.then(nc.vector.tensor_copy(part[:, 0, :], qf[:, :]))
            done.then(nc.vector.tensor_tensor(rest[:, :], qf[:, :], part[:, 0, :], ALU.subtract))
            done.then(nc.vector.tensor_copy(part[:, 1, :], rest[:, :]))
            done.then(nc.vector.tensor_tensor(part[:, 2, :], rest[:, :], part[:, 1, :], ALU.subtract))
            for n in range(3):
                for h, name in enumerate(("even", "odd")):
                    nc.vector.tensor_scalar(
                        block_q[:, n, :, h * S:(h + 1) * S], part[:, n, :].rearrange("p (b q) -> p b q", q=S),
                        col(m, name), None, ALU.mult).then_inc(blocks, 1)

        @block.scalar
        def _(act):
            if layer == 0:
                act.wait_ge(eps_set, 1)
            for n in range(norms):
                norm_scalar(nc, act, m, normed, NORM_LINKS * n + NORM_SUM, roots, st)
            for g in range(ng):
                act.wait_ge(turns, g + 1)
                nc.scalar.activation(zT[:, g * gc:(g + 1) * gc], turned[g][:, 0:gc], ACT.Copy)\
                    .then_inc(turns_out, 1)

        @block.tensor
        def _(pe):
            if layer == 1:
                for n, (w, b) in enumerate((("wq1", "b_x"), ("wk1", "b_kv"), ("wv1", "b_kv"))):
                    last = nc.tensor.matmul(small[:, n:n + 1], mat(m, w), col(m, b), start=True, stop=True)
                last.then_inc(biases, 1)
            else:
                pe.sem_inc(biases, 1)
            pe.wait_ge(folded, 6)
            nc.tensor.matmul(small[0:TOK, 128:256], bvb[:, :], mat(m, "wo" + L), start=True, stop=True)\
                .then_inc(biases, 1)
            pe.wait_ge(normed, last_norm)
            for g in range(ng):
                for i in range(gt):
                    last = nc.tensor.transpose(turned[g][:, i * TOK:(i + 1) * TOK], z[:, g * gt + i, :],
                                               mat(m, "ident")[0:TOK, 0:TOK])
                last.then_inc(turns, 1)
            for g in range(ng):
                pe.wait_ge(turns_out, g + 1)
                if g >= 2:
                    pe.wait_ge(steps, g - 1)
                nc.tensor.matmul(qps[:, g % 2, 0:gc], wq[:, :], zT[:, g * gc:(g + 1) * gc], start=True, stop=True)\
                    .then_inc(projected, 1)

        @block.sync
        def _(sp):
            for t in range(TERMS):
                n = PARTS_Q[t]
                sp.wait_ge(blocks, 2 * n + 2)
                sp.dma_start(m.q_dram[t].rearrange("r p b c -> p r (b c)"),
                             block_q[:, n, :, :].rearrange("p b c -> p (b c)")).then_inc(saved, 16)
            sp.wait_ge(saved, 16 * TERMS)


def context_norm(nc, m):
    with ExitStack() as ctx:
        def sb(name, shape, dt):
            return ctx.enter_context(nc.sbuf_tensor("cn_" + name, shape, dt))

        def sem(name):
            return ctx.enter_context(nc.semaphore("cn_" + name))

        raw = sb("raw", [P, 2, KT, D], F32)
        zed = sb("zed", [P, 2, KT, D], F32)
        st = sb("st", [P, 2, KT, 6], F32)
        tmp = sb("tmp", [P, 2, 5, KT], F32)
        power = sb("power", [P, KT], F32)
        loaded = [sem("loaded0"), sem("loaded1")]
        saved = [sem("saved0"), sem("saved1")]
        stats, small, scaled, ready = sem("stats"), sem("small"), sem("scaled"), sem("ready")
        block = ctx.enter_context(nc.Block())
        SMALL = 8

        @block.sync
        def _(sp):
            sp.wait_ge(ready, 3)
            with sp.Fori(0, m.nb // 2) as lap:
                for u in range(2):
                    b = 2 * lap + u
                    sp.wait_ge(scaled, 2 * lap + (u + 1))
                    sp.dma_start(raw[:, u, 0:KT - 1, :], m.ctx_dram[b, 0:(KT - 1) * P, :].rearrange(
                        "(c p) d -> p c d", p=P)).then_inc(loaded[u], 16)
                    sp.dma_start(raw[0:LAST, u, KT - 1, :], m.ctx_dram[b, (KT - 1) * P:CTX, :])\
                        .then_inc(loaded[u], 16)
            for u in range(2):
                sp.wait_ge(saved[u], 32 * (m.nb // 2))

        @block.vector
        def _(dve):
            nc.vector.memset(power[:, :], -0.5).then_inc(ready, 1)
            nc.vector.memset(raw[:, :, KT - 1, :], 0.0).then_inc(ready, 1)
            nc.vector.memset(st[:, :, :, :], 0.0).then_inc(ready, 1)
            dve.wait_ge(ready, 3)
            dve.sem_inc(scaled, 2)
            with dve.Fori(0, m.nb // 2) as lap:
                for u in range(2):
                    at = 2 * lap + u
                    dve.wait_ge(loaded[u], 32 * lap + 32)
                    dve.wait_ge(scaled, at + 1)
                    for c in range(KT):
                        last = nc.vector.bn_stats(st[0:rows_of(c), u, c, :], raw[0:rows_of(c), u, c, :])
                    last.then_inc(small, 1)
                    total, apart, var, inv, off = (tmp[:, u, n, :] for n in range(5))
                    even, odd = st[:, u, :, 1], st[:, u, :, 4]
                    dve.wait_ge(small, SMALL * at + 1)
                    nc.vector.tensor_tensor(total, even, odd, ALU.add).then_inc(small, 1)
                    dve.wait_ge(small, SMALL * at + 2)
                    nc.vector.tensor_tensor(apart, even, odd, ALU.subtract).then_inc(small, 1)
                    dve.wait_ge(small, SMALL * at + 3)
                    nc.vector.tensor_tensor(apart, apart, apart, ALU.mult).then_inc(small, 1)
                    dve.wait_ge(small, SMALL * at + 4)
                    nc.vector.tensor_scalar(apart, apart, 0.25, EPS, ALU.mult, ALU.add).then_inc(small, 1)
                    dve.wait_ge(small, SMALL * at + 5)
                    nc.vector.tensor_tensor(var, st[:, u, :, 2], st[:, u, :, 5], ALU.add).then_inc(small, 1)
                    dve.wait_ge(small, SMALL * at + 6)
                    nc.vector.scalar_tensor_tensor(out=var, in0=var, scalar=1.0 / D, in1=apart,
                                                   op0=ALU.mult, op1=ALU.add).then_inc(small, 1)
                    dve.wait_ge(stats, at + 1)
                    nc.vector.scalar_tensor_tensor(out=off, in0=total, scalar=-0.5, in1=inv,
                                                   op0=ALU.mult, op1=ALU.mult).then_inc(small, 1)

        @block.gpsimd
        def _(pool):
            pool.wait_ge(ready, 3)
            with pool.Fori(0, m.nb // 2) as lap:
                for u in range(2):
                    at = 2 * lap + u
                    pool.wait_ge(small, SMALL * at + SMALL - 1)
                    nc.gpsimd.tensor_tensor(tmp[:, u, 3, :], tmp[:, u, 2, :], power[:, :], ALU.pow)\
                        .then_inc(stats, 1)

        @block.scalar
        def _(act):
            with act.Fori(0, m.nb // 2) as lap:
                for u in range(2):
                    at = 2 * lap + u
                    act.wait_ge(small, SMALL * at + SMALL)
                    act.wait_ge(saved[u], 32 * lap)
                    for c in range(KT):
                        r = rows_of(c)
                        last = nc.scalar.activation(zed[0:r, u, c, :], raw[0:r, u, c, :], ACT.Identity,
                                                    bias=tmp[0:r, u, 4, c:c + 1], scale=tmp[0:r, u, 3, c:c + 1])
                    last.then_inc(scaled, 1)
                    act.wait_ge(scaled, at + 3)
                    act.dma_start(m.z_dram[at, 0:(KT - 1) * P, :].rearrange("(c p) d -> p c d", p=P),
                                  zed[:, u, 0:KT - 1, :]).then_inc(saved[u], 16)
                    act.dma_start(m.z_dram[at, (KT - 1) * P:CTX, :], zed[0:LAST, u, KT - 1, :])\
                        .then_inc(saved[u], 16)


def attention(nc, m, layer):
    nb = m.nb
    src = m.ctx_dram if layer == 0 else m.z_dram
    rows_a = SPLIT if layer == 0 else FILLED
    loads = 4 if layer == 0 else 5
    L = str(layer)
    with ExitStack() as ctx:
        def sb(name, shape, dt):
            return ctx.enter_context(nc.sbuf_tensor(f"a{L}_{name}", shape, dt))

        def sem(name):
            return ctx.enter_context(nc.semaphore(f"a{L}_{name}"))

        kstack = sb("kstack", [STACK, 3, PAIRS, CTX], BF16)
        qstack = sb("qstack", [STACK, 3, PAIRS, PQ], BF16)
        raw = sb("raw", [P, 3, KT, D], F32)
        rawT = sb("rawT", [P, CTX], F32)
        kf = sb("kf", [P, CTX], F32)
        rest = sb("rest", [P, CTX], F32)
        part = sb("part", [P, 3, CTX], BF16)
        keep = sb("keep", [P, CTX], BF16) if layer else None
        vals = sb("vals", [P, 3, KT, PAIRS, VW], F32)
        probs = sb("probs", [P, 2, 2, GC], F32)
        mixed_sb = sb("mixed_sb", [P, 2 * PQ], F32)
        inverse = sb("inverse", [P, 2 * PQ], F32)
        heads = sb("heads", [P, 2, 2, S], F32)
        out_sb = sb("out_sb", [S, D], F32)
        peaks = sb("peaks", [PQ, PAIRS, NCH], F32)
        low = sb("low", [PQ, 3, PAIRS], F32)
        shift = sb("shift", [PQ, PAIRS, 6], BF16)
        scores = [ctx.enter_context(nc.psum_tensor(f"a{L}_scores{i}", [P, 2, 512], F32)) for i in range(2)]
        ring = [ctx.enter_context(nc.psum_tensor(f"a{L}_ring{i}", [P, 512], F32)) for i in range(RING)]
        mix_ps = ctx.enter_context(nc.psum_tensor(f"a{L}_mix", [P, 512], F32))

        ready = sem("ready")
        raw_loaded = [sem(f"raw_loaded{i}") for i in range(3)]
        keep_loaded = sem("keep_loaded")
        filled = [sem(f"ring_filled{i}") for i in range(RING)]
        drained = [sem(f"ring_drained{i}") for i in range(RING)]
        high_made, rest_made, mid_made, low_made = sem("high_made"), sem("rest_made"), sem("mid_made"), sem("low_made")
        part_saved = [sem(f"part_saved{i}") for i in range(3)]
        stack_loaded = [sem(f"stack_loaded{i}") for i in range(3)]
        scored, exped, mixed, mix_read = sem("scored"), sem("exped"), sem("mixed"), sem("mix_read")
        shift_steps, normalised, out_saved = sem("shift_steps"), sem("normalised"), sem("out_saved")
        READY = 7
        SHIFTS = 6
        block = ctx.enter_context(nc.Block())

        @block.sync
        def _(sp):
            sp.wait_ge(ready, READY)

            def step(s):
                if not s.make:
                    return
                k, batch = s.buf(2), s.batch(2)
                if s.mix:
                    sp.wait_ge(scored, 12 * s.batch(0))
                sp.dma_start(qstack[0:SPLIT, k, :, :],
                             m.q_dram[:, :, :, batch, :].rearrange("t r p c -> (t r) p c"))\
                    .then_inc(stack_loaded[k], 16)
                if layer:
                    sp.dma_start(kstack[SPLIT:FILLED, k, :, :],
                                 m.fill_dram[batch].unsqueeze(1).to_broadcast([3, PAIRS, CTX]))\
                        .then_inc(stack_loaded[k], 16)
                for n, made in enumerate((high_made, mid_made, low_made)):
                    sp.wait_ge(made, NCH * (batch + 1))
                    sp.dma_start(m.k_dram[k, n].rearrange("r p n -> p r n"), part[:, n, :])\
                        .then_inc(part_saved[n], 16)
                for n in range(3):
                    sp.wait_ge(part_saved[n], 16 * (batch + 1))
                at = 0
                for n in (3, 2, 1):
                    sp.dma_start(kstack[at:at + n * PR, k, :, :],
                                 m.k_dram[k, 0:n].rearrange("t r p n -> (t r) p n"))\
                        .then_inc(stack_loaded[k], 16)
                    at += n * PR

            run_steps(sp, nb, step)
            for k in range(3):
                sp.wait_ge(stack_loaded[k], 16 * loads * len(range(k, nb, 3)))

        @block.scalar
        def _(act):
            act.wait_ge(ready, READY)
            act.sem_inc(exped, 2)

            def step(s):
                if s.make:
                    k, batch = s.buf(2), s.batch(2)
                    act.dma_start(raw[:, k, 0:KT - 1, :], src[batch, 0:(KT - 1) * P, :].rearrange(
                        "(c p) d -> p c d", p=P)).then_inc(raw_loaded[k], 16)
                    act.dma_start(raw[0:LAST, k, KT - 1, :], src[batch, (KT - 1) * P:CTX, :])\
                        .then_inc(raw_loaded[k], 16)
                    if layer:
                        if s.peak:
                            act.wait_ge(high_made, NCH * batch)
                        act.dma_start(keep[:, :], m.keep_dram[batch].partition_broadcast(P))\
                            .then_inc(keep_loaded, 16)
                for kind, a, j, bank, before in s.slots():
                    if kind == "score":
                        rows, n = rows_of(a), 12 * s.batch(0) + a + 1
                        act.wait_ge(scored, n)
                        act.wait_ge(mixed, n)
                        nc.scalar.activation(probs[0:rows, a % 2, :, :], scores[a % 2][0:rows, :, 0:GC], ACT.Exp)\
                            .then_inc(exped, 1)
                    elif kind == "turn":
                        act.wait_ge(filled[bank], before + 1)
                        width = min(512, CTX - 512 * a)
                        nc.scalar.activation(rawT[:, 512 * a:512 * a + width], ring[bank][:, 0:width], ACT.Copy)\
                            .then_inc(drained[bank], 1)
                    elif kind == "key" and layer == 0:
                        act.wait_ge(filled[bank], before + 1)
                        if s.peak:
                            act.wait_ge(rest_made, NCH * s.batch(1) + a + 1)
                        nc.scalar.activation(kf[:, CH * a:CH * (a + 1)], ring[bank][:, 0:CH], ACT.Identity,
                                             bias=m.bk[0][:, 0:1]).then_inc(drained[bank], 1)
                    elif kind == "value":
                        act.wait_ge(filled[bank], before + 1)
                        tiles = ring[bank][:, :].rearrange("p (c h e) -> p c h e", c=4, h=PAIRS)
                        k = s.buf(2)
                        if a < NCH - 1:
                            nc.scalar.activation(vals[:, k, 4 * a:4 * a + 4, :, 0:PR], tiles, ACT.Copy)\
                                .then_inc(drained[bank], 1)
                        else:
                            nc.scalar.activation(vals[:, k, 4 * a:4 * a + 3, :, 0:PR], tiles[:, 0:3], ACT.Copy)
                            nc.scalar.activation(vals[0:LAST, k, KT - 1, :, 0:PR], tiles[0:LAST, 3], ACT.Copy)\
                                .then_inc(drained[bank], 1)
                    elif kind == "mix" and a == KT - 1:
                        act.wait_ge(mixed, 12 * s.batch(1) + 2)
                        act.wait_ge(normalised, s.batch(0))
                        nc.scalar.activation(mixed_sb[:, :], mix_ps[:, 0:2 * PQ], ACT.Copy).then_inc(mix_read, 1)
                    elif kind == "project":
                        act.wait_ge(filled[bank], before + 1)
                        act.wait_ge(out_saved, 16 * s.batch(0))
                        nc.scalar.activation(out_sb[:, :], ring[bank][0:S, 0:D], ACT.Copy)\
                            .then_inc(drained[bank], 1)
                        act.wait_ge(drained[bank], before + 1)
                        act.dma_start(m.y_dram[s.batch(0)], out_sb[:, :]).then_inc(out_saved, 16)

            run_steps(act, nb, step)
            act.wait_ge(out_saved, 16 * nb)

        @block.vector
        def _(dve):
            nc.vector.memset(kstack[SPLIT:STACK, :, :, :], 1.0).then_inc(ready, 1)
            nc.vector.memset(qstack[SPLIT:STACK, :, :, :], 1.0).then_inc(ready, 1)
            nc.vector.memset(vals[:, :, :, :, :], 1.0).then_inc(ready, 1)
            nc.vector.memset(shift[:, :, :], 1.0).then_inc(ready, 1)
            nc.vector.memset(mix_ps[:, :], 0.0).then_inc(ready, 1)
            nc.vector.memset(raw[:, :, KT - 1, :], 0.0).then_inc(ready, 1)
            dve.wait_ge(ready, 1)
            if layer == 0:
                nc.vector.memset(kstack[SPLIT:FILLED, :, :, :], 0.0).then_inc(ready, 1)
            else:
                nc.vector.memset(low[:, :, :], 0.0).then_inc(ready, 1)
            dve.wait_ge(ready, READY)

            def mids(s, chunks):
                batch = s.batch(2)
                for a in chunks:
                    dve.wait_ge(rest_made, NCH * batch + a + 1)
                    if s.peak:
                        dve.wait_ge(part_saved[1], 16 * batch)
                        dve.wait_ge(low_made, NCH * s.batch(1) + a + 1)
                    nc.vector.tensor_copy(part[:, 1, CH * a:CH * (a + 1)], rest[:, CH * a:CH * (a + 1)])\
                        .then_inc(mid_made, 1)

            def step(s):
                for kind, a, j, bank, before in s.slots():
                    if kind == "peak":
                        dve.wait_ge(filled[bank], before + 1)
                        nc.vector.tensor_reduce(peaks[:, a, j:j + 1], ring[bank][0:PQ, 0:CH], AX.X, ALU.max)\
                            .then_inc(drained[bank], 1)
                        if (a, j) == (PAIRS - 1, NCH - 1):
                            n = SHIFTS * s.batch(1)
                            dve.wait_ge(drained[bank], before + 1)
                            nc.vector.tensor_reduce(low[:, 0, :], peaks[:, :, :], AX.X, ALU.max, negate=True)\
                                .then_inc(shift_steps, 1)
                            dve.wait_ge(shift_steps, n + 1)
                            nc.vector.tensor_copy(shift[:, :, 3], low[:, 0, :]).then_inc(shift_steps, 1)
                            dve.wait_ge(shift_steps, n + 2)
                            nc.vector.tensor_tensor(low[:, 1, :], low[:, 0, :], shift[:, :, 3], ALU.subtract)\
                                .then_inc(shift_steps, 1)
                            dve.wait_ge(shift_steps, n + 3)
                            nc.vector.tensor_copy(shift[:, :, 4], low[:, 1, :]).then_inc(shift_steps, 1)
                            dve.wait_ge(shift_steps, n + 4)
                            nc.vector.tensor_tensor(low[:, 2, :], low[:, 1, :], shift[:, :, 4], ALU.subtract)\
                                .then_inc(shift_steps, 1)
                            dve.wait_ge(shift_steps, n + 5)
                            nc.vector.tensor_copy(shift[:, :, 5], low[:, 2, :]).then_inc(shift_steps, 1)
                    elif kind == "shift":
                        dve.wait_ge(filled[bank], before + 1)
                        nc.vector.tensor_copy(qstack[SPLIT:STACK, s.buf(1), 4 * a:4 * a + 4, :],
                                              ring[bank][SPLIT:STACK, 0:GC].rearrange("r (p c) -> r p c", p=4))\
                            .then_inc(drained[bank], 1)
                    elif kind == "key":
                        batch = s.batch(2)
                        if layer:
                            dve.wait_ge(filled[bank], before + 1)
                            dve.wait_ge(keep_loaded, 16 * (batch + 1))
                            if s.peak:
                                dve.wait_ge(rest_made, NCH * s.batch(1) + a + 1)
                            nc.vector.scalar_tensor_tensor(
                                out=kf[:, CH * a:CH * (a + 1)], in0=ring[bank][:, 0:CH], scalar=m.bk[1][:, 0:1],
                                in1=keep[:, CH * a:CH * (a + 1)], op0=ALU.add, op1=ALU.mult)\
                                .then_inc(drained[bank], 1)
                        dve.wait_ge(drained[bank], before + 1)
                        if s.peak:
                            dve.wait_ge(part_saved[0], 16 * batch)
                            dve.wait_ge(rest_made, NCH * s.batch(1) + a + 1)
                        nc.vector.tensor_copy(part[:, 0, CH * a:CH * (a + 1)], kf[:, CH * a:CH * (a + 1)])\
                            .then_inc(high_made, 1)
                        if a:
                            mids(s, [a - 1])
                        if a == NCH - 1:
                            mids(s, [a])
                    elif kind == "total":
                        dve.wait_ge(filled[bank], before + 1)
                        nc.vector.reciprocal(inverse[:, :], ring[bank][:, 0:2 * PQ]).then_inc(drained[bank], 1)
                        dve.wait_ge(drained[bank], before + 1)
                        nc.vector.tensor_tensor(heads[:, :, :, :].rearrange("p r x q -> p (r x q)"),
                                                mixed_sb[:, :], inverse[:, :], ALU.mult).then_inc(normalised, 1)

            run_steps(dve, nb, step)

        @block.gpsimd
        def _(pool):
            def step(s):
                if not s.make:
                    return
                batch = s.batch(2)
                for a in range(NCH):
                    pool.wait_ge(high_made, NCH * batch + a + 1)
                    if s.peak:
                        pool.wait_ge(low_made, NCH * s.batch(1) + a + 1)
                    nc.gpsimd.tensor_tensor(rest[:, CH * a:CH * (a + 1)], kf[:, CH * a:CH * (a + 1)],
                                            part[:, 0, CH * a:CH * (a + 1)], ALU.subtract).then_inc(rest_made, 1)
                for a in range(NCH):
                    pool.wait_ge(mid_made, NCH * batch + a + 1)
                    if s.peak:
                        pool.wait_ge(part_saved[2], 16 * batch)
                    nc.gpsimd.tensor_tensor(part[:, 2, CH * a:CH * (a + 1)], rest[:, CH * a:CH * (a + 1)],
                                            part[:, 1, CH * a:CH * (a + 1)], ALU.subtract).then_inc(low_made, 1)

            run_steps(pool, nb, step)

        @block.tensor
        def _(pe):
            pe.wait_ge(ready, READY)
            pe.sem_inc(mixed, 2)
            ident = mat(m, "ident")

            def step(s):
                shifts = []
                for kind, a, j, bank, before in s.slots():
                    if kind not in ("score", "mix"):
                        pe.wait_ge(drained[bank], before)
                    if kind == "score":
                        rows, k = rows_of(a), s.buf(0)
                        pe.wait_ge(exped, 12 * s.batch(0) + a + 1)
                        for p in range(PAIRS):
                            last = nc.tensor.matmul(
                                scores[a % 2][0:rows, p // 4, (p % 4) * PQ:(p % 4 + 1) * PQ],
                                kstack[:, k, p, P * a:P * a + rows], qstack[:, k, p, :], start=True, stop=True)
                        last.then_inc(scored, 1)
                    elif kind == "mix":
                        rows, k = rows_of(a), s.buf(0)
                        pe.wait_ge(exped, 12 * s.batch(0) + a + 3)
                        if a == 0:
                            pe.wait_ge(mix_read, s.batch(0))
                        for p in range(PAIRS):
                            r, q = p // 4, p % 4
                            last = nc.tensor.matmul(
                                mix_ps[32 * q:32 * q + VW, r * PQ:(r + 1) * PQ], vals[0:rows, k, a, p, :],
                                probs[0:rows, a % 2, r, q * PQ:(q + 1) * PQ],
                                start=(a == 0 and r == 0), stop=(a == KT - 1), skip_group_check=True)
                        last.then_inc(mixed, 1)
                    elif kind == "peak":
                        k = s.buf(1)
                        if (a, j) == (0, 0):
                            pe.wait_ge(stack_loaded[k], 16 * loads * (s.use(1) + 1))
                        nc.tensor.matmul(ring[bank][0:PQ, 0:CH], qstack[0:rows_a, k, a, :],
                                         kstack[0:rows_a, k, a, CH * j:CH * (j + 1)], start=True, stop=True)\
                            .then_inc(filled[bank], 1)
                    elif kind == "shift":
                        pe.wait_ge(shift_steps, SHIFTS * (s.batch(1) + 1))
                        for p in range(4):
                            last = nc.tensor.matmul(ring[bank][SPLIT:STACK, p * PQ:(p + 1) * PQ],
                                                    shift[:, 4 * a + p, :], m.identb[0:PQ, 0:PQ],
                                                    start=True, stop=True)
                        last.then_inc(filled[bank], 1)
                        shifts.append((bank, before + 1))
                    elif kind == "turn":
                        k = s.buf(2)
                        if a == 0:
                            pe.wait_ge(raw_loaded[k], 32 * (s.use(2) + 1))
                        for c in range(4 * a, 4 * a + 4):
                            rows = rows_of(c)
                            last = nc.tensor.transpose(ring[bank][:, P * (c - 4 * a):P * (c - 4 * a) + rows],
                                                       raw[0:rows, k, c, :], ident[0:rows, 0:rows])
                        last.then_inc(filled[bank], 1)
                        turned = (bank, before + 1)
                    elif kind == "key":
                        if a == 0:
                            pe.wait_ge(drained[turned[0]], turned[1])
                        nc.tensor.matmul(ring[bank][:, 0:CH], m.wk[layer][:, :], rawT[:, CH * a:CH * (a + 1)],
                                         start=True, stop=True).then_inc(filled[bank], 1)
                    elif kind == "value":
                        for c in range(4 * a, 4 * a + 4):
                            rows = rows_of(c)
                            last = nc.tensor.matmul(ring[bank][0:rows, P * (c - 4 * a):P * (c - 4 * a + 1)],
                                                    rawT[:, P * c:P * c + rows], m.wv[layer][:, :],
                                                    start=True, stop=True)
                        last.then_inc(filled[bank], 1)
                    elif kind == "total":
                        pe.wait_ge(mix_read, s.batch(1))
                        nc.tensor.matmul(ring[bank][:, 0:2 * PQ], mat(m, "pick"), mixed_sb[:, :],
                                         start=True, stop=True).then_inc(filled[bank], 1)
                    elif kind == "project":
                        pe.wait_ge(normalised, s.batch(1))
                        for n in range(4):
                            last = nc.tensor.matmul(ring[bank][0:S, 0:D], heads[:, n // 2, n % 2, :],
                                                    mat(m, f"woh{layer}{'abcd'[n]}"), start=(n == 0), stop=(n == 3))
                        last.then_inc(filled[bank], 1)
                for bank, n in shifts:
                    pe.wait_ge(drained[bank], n)

            run_steps(pe, nb, step)


def ffn_ternary(nc, m):
    nt = m.nt
    gt = min(GT, nt)
    ng = nt // gt
    gc = gt * TOK
    cols = nt * TOK
    with ExitStack() as ctx:
        def sb(name, shape, dt):
            return ctx.enter_context(nc.sbuf_tensor("t_" + name, shape, dt))

        def sem(name):
            return ctx.enter_context(nc.semaphore("t_" + name))

        y = sb("y", [TOK, nt, D], F32)
        z = sb("z", [TOK, nt, D], F32)
        sq = sb("sq", [TOK, nt, D], F32)
        st = sb("st", [TOK, 12, nt], F32)
        qz = sb("qz", [TOK, nt, D], BF16)
        qzT = sb("qzT", [P, cols], BF16)
        w1 = sb("w1", [P, F0], BF16)
        w2 = sb("w2", [P, F0], BF16)
        wr = sb("wr", [P, F0], F32)
        wst = sb("wst", [P, 8], F32)
        ones = sb("ones", [P, P], F32)
        h = sb("h", [TOK, nt, F0], F32)
        hq = sb("hq", [TOK, 2, F0], F32)
        hb = sb("hb", [TOK, 2, F0], BF16)
        hT = sb("hT", [P, 2, FT, TOK], BF16)
        junk = sb("junk", [TOK, F0], F32)
        sums = ctx.enter_context(nc.psum_tensor("t_sums", [P, 512], F32))
        turned = [ctx.enter_context(nc.psum_tensor(f"t_turned{i}", [P, 1024], BF16)) for i in range(2)]
        hps = [ctx.enter_context(nc.psum_tensor(f"t_hps{i}", [TOK, F0], F32)) for i in range(2)]
        ops = [ctx.enter_context(nc.psum_tensor(f"t_ops{i}", [TOK, 512], F32)) for i in range(2)]
        y_loaded, chain_sem, roots = sem("y_loaded"), sem("chain"), sem("roots")
        wsum, wready, zturned, zcopied = sem("wsum"), sem("wready"), sem("zturned"), sem("zcopied")
        hid, hid_read, gelus, squares = sem("hid"), sem("hid_read"), sem("gelus"), sem("squares")
        quant, hturned, hcopied, outs, outs_read = sem("quant"), sem("hturned"), sem("hcopied"), sem("outs"), sem("outs_read")
        tok_quant = sem("tok_quant")
        block = ctx.enter_context(nc.Block())
        A = mybir.AxisListType.X

        @block.sync
        def _(sp):
            sp.dma_start(y[:, :, :], m.y_dram.rearrange("b s d -> (b s) d").rearrange("(n p) d -> p n d", p=TOK))\
                .then_inc(y_loaded, 16)

        @block.vector
        def _(dve):
            def out_tile(i):
                dve.wait_ge(outs, i + 1)
                nc.vector.scalar_tensor_tensor(out=y[:, i, :], in0=ops[i % 2][:, 0:D], scalar=st[:, 7, i:i + 1],
                                               in1=row(m, "b2", TOK), op0=ALU.mult, op1=ALU.add).then_inc(outs_read, 1)

            chain = Chain(dve, chain_sem)
            nc.vector.memset(ones[:, :], 1.0).then_inc(wready, 1)
            for n, (a, b) in enumerate((("fa", "fd"), ("ga", "gd"))):
                at = MATS.index(a) * P
                nc.vector.tensor_reduce(wst[:, n:n + 1], m.mats[:, at:at + F0], AX.X, ALU.add,
                                        apply_absolute_value=True).then_inc(wready, 1)
            dve.wait_ge(wsum, 1)
            chain.then(nc.vector.tensor_scalar(wst[:, 2:4], sums[:, 0:2], 1.0 / (D * F0), 1e-5, ALU.mult, ALU.max))
            chain.then(nc.vector.reciprocal(wst[:, 4:6], wst[:, 2:4]))
            for n, (w, a) in enumerate(((w1, "fa"), (w2, "ga"))):
                at = MATS.index(a) * P
                chain.then(nc.vector.tensor_scalar(wr[:, :], m.mats[:, at:at + F0], wst[:, 4 + n:5 + n], 1.0,
                                                   ALU.mult, ALU.min))
                chain.then(nc.vector.tensor_scalar(wr[:, :], wr[:, :], -1.0, MAGIC, ALU.max, ALU.add))
                chain.then(nc.vector.tensor_scalar(w[:, :], wr[:, :], MAGIC, None, ALU.subtract))
            dve.wait_ge(y_loaded, 16)
            chain.then(nc.vector.tensor_tensor(y[:, :, :], y[:, :, :], per_channel(m.yb[0][:, :], nt), ALU.add))
            chain.then(nc.vector.scalar_tensor_tensor(out=m.x[:, :, :], in0=y[:, :, :], scalar=m.gates[0:TOK, 0:1],
                                                      in1=m.x[:, :, :], op0=ALU.mult, op1=ALU.add))
            norm_vector(nc, dve, chain, roots, m.x[:, :, :], z[:, :, :], sq[:, :, :], st, nt, 1)
            chain.then(nc.vector.tensor_tensor(sq[:, :, :], z[:, :, :], z[:, :, :], ALU.mult))
            chain.then(nc.vector.tensor_reduce(st[:, 2, :], sq[:, :, :], AX.X, ALU.add))
            dve.wait_ge(roots, 2)
            chain.then(nc.vector.reciprocal(st[:, 4, :], st[:, 3, :]))
            chain.then(nc.vector.tensor_tensor(z[:, :, :], z[:, :, :], per_token(st[:, 4, :], nt), ALU.mult))
            chain.then(nc.vector.tensor_reduce(st[:, 5, :], z[:, :, :], AX.X, ALU.max, apply_absolute_value=True))
            chain.then(nc.vector.tensor_scalar(st[:, 5, :], st[:, 5, :], 1e-5, 1.0 / 127.0, ALU.max, ALU.mult))
            chain.then(nc.vector.reciprocal(st[:, 6, :], st[:, 5, :]))
            chain.then(nc.vector.tensor_tensor(z[:, :, :], z[:, :, :], per_token(st[:, 6, :], nt), ALU.mult))
            chain.then(nc.vector.tensor_scalar(z[:, :, :], z[:, :, :], 127.0, -128.0, ALU.min, ALU.max))
            chain.then(nc.vector.tensor_scalar(z[:, :, :], z[:, :, :], MAGIC, MAGIC, ALU.add, ALU.subtract))
            nc.vector.tensor_copy(qz[:, :, :], z[:, :, :]).then_inc(tok_quant, 1)
            chain.then(nc.vector.tensor_scalar(st[:, 7, :], st[:, 5, :], wst[0:TOK, 2:3], None, ALU.mult))
            for g in range(ng):
                dve.wait_ge(zturned, g + 1)
                nc.vector.tensor_copy(qzT[:, g * gc:(g + 1) * gc], turned[g % 2][:, 0:gc]).then_inc(zcopied, 1)
            for i in range(nt):
                dve.wait_ge(hid, i + 1)
                nc.vector.scalar_tensor_tensor(out=h[:, i, :], in0=hps[i % 2][:, :], scalar=st[:, 7, i:i + 1],
                                               in1=row(m, "b1", TOK), op0=ALU.mult, op1=ALU.add).then_inc(hid_read, 1)
            for i in range(nt):
                dve.wait_ge(gelus, i + 1)
                last = nc.vector.tensor_reduce(st[:, 8, i:i + 1], h[:, i, :], AX.X, ALU.max,
                                               apply_absolute_value=True)
            chain.then(last)
            dve.wait_ge(roots, 3)
            chain.then(nc.vector.reciprocal(st[:, 4, :], st[:, 3, :]))
            chain.then(nc.vector.tensor_tensor(st[:, 8, :], st[:, 8, :], st[:, 4, :], ALU.mult))
            chain.then(nc.vector.tensor_scalar(st[:, 5, :], st[:, 8, :], 1e-5, 1.0 / 127.0, ALU.max, ALU.mult))
            chain.then(nc.vector.reciprocal(st[:, 6, :], st[:, 5, :]))
            chain.then(nc.vector.tensor_tensor(st[:, 6, :], st[:, 6, :], st[:, 4, :], ALU.mult))
            chain.then(nc.vector.tensor_scalar(st[:, 7, :], st[:, 5, :], wst[0:TOK, 3:4], None, ALU.mult))
            for i in range(nt):
                u = i % 2
                chain.then(nc.vector.tensor_scalar(hq[:, u, :], h[:, i, :], st[:, 6, i:i + 1], 127.0, ALU.mult, ALU.min))
                chain.then(nc.vector.tensor_scalar(hq[:, u, :], hq[:, u, :], -128.0, MAGIC, ALU.max, ALU.add))
                if i >= 2:
                    dve.wait_ge(hturned, i - 1)
                nc.vector.tensor_scalar(hb[:, u, :], hq[:, u, :], MAGIC, None, ALU.subtract).then_inc(quant, 1)
                if i:
                    out_tile(i - 1)
            out_tile(nt - 1)
            dve.wait_ge(outs_read, nt)
            chain.then(nc.vector.scalar_tensor_tensor(out=m.x[:, :, :], in0=y[:, :, :], scalar=m.gates[0:TOK, 2:3],
                                                      in1=m.x[:, :, :], op0=ALU.mult, op1=ALU.add))

        links_before = 2 + 6 + 2

        @block.scalar
        def _(act):
            norm_scalar(nc, act, m, chain_sem, links_before + NORM_SUM, roots, st)
            norm_scalar(nc, act, m, chain_sem, links_before + NORM_LINKS + 2, roots, st)
            for i in range(nt):
                act.wait_ge(hid_read, i + 1)
                nc.scalar.activation(h[:, i, :], h[:, i, :], ACT.Gelu).then_inc(gelus, 1)
            act.wait_ge(gelus, nt)
            for i in range(nt):
                nc.scalar.activation(junk[:, :], h[:, i, :], ACT.Square, accum_out=st[:, 9, i:i + 1])\
                    .then_inc(squares, 1)
                act.wait_ge(squares, i + 1)
            nc.scalar.activation(st[:, 3, :], st[:, 9, :], ACT.Sqrt, bias=m.eps[0:TOK, 0:1], scale=1.0 / F0)\
                .then_inc(roots, 1)
            for i in range(nt):
                act.wait_ge(hturned, i + 1)
                if i >= 2:
                    act.wait_ge(outs, i - 1)
                nc.scalar.activation(hT[:, i % 2, :, :].rearrange("p f t -> p (f t)"), turned[i % 2][:, 0:FT * TOK],
                                     ACT.Copy).then_inc(hcopied, 1)

        @block.tensor
        def _(pe):
            def second(i):
                pe.wait_ge(hcopied, i + 1)
                if i >= 2:
                    pe.wait_ge(outs_read, i - 1)
                for f in range(FT):
                    last = nc.tensor.matmul(ops[i % 2][:, 0:D], hT[:, i % 2, f, :], w2[:, f * P:(f + 1) * P],
                                            start=(f == 0), stop=(f == FT - 1))
                last.then_inc(outs, 1)

            pe.wait_ge(wready, 3)
            nc.tensor.matmul(sums[:, 0:2], ones[:, :], wst[:, 0:2], start=True, stop=True).then_inc(wsum, 1)
            pe.wait_ge(tok_quant, 1)
            for g in range(ng):
                if g >= 2:
                    pe.wait_ge(zcopied, g - 1)
                for i in range(gt):
                    last = nc.tensor.transpose(turned[g % 2][:, i * TOK:(i + 1) * TOK], qz[:, g * gt + i, :],
                                               m.identb[0:TOK, 0:TOK])
                last.then_inc(zturned, 1)
            pe.wait_ge(chain_sem, 8)
            for i in range(nt):
                pe.wait_ge(zcopied, i // gt + 1)
                if i >= 2:
                    pe.wait_ge(hid_read, i - 1)
                nc.tensor.matmul(hps[i % 2][:, :], qzT[:, i * TOK:(i + 1) * TOK], w1[:, :], start=True, stop=True)\
                    .then_inc(hid, 1)
            for i in range(nt):
                pe.wait_ge(quant, i + 1)
                pe.wait_ge(zcopied, ng)
                if i >= 2:
                    pe.wait_ge(hcopied, i - 1)
                for f in range(FT):
                    last = nc.tensor.transpose(turned[i % 2][:, f * TOK:(f + 1) * TOK], hb[:, i % 2, f * P:(f + 1) * P],
                                               m.identb[0:TOK, 0:TOK])
                last.then_inc(hturned, 1)
                if i:
                    second(i - 1)
            second(nt - 1)


def ffn_experts(nc, m):
    nt = m.nt
    gt = min(GT, nt)
    ng = nt // gt
    gc = gt * TOK
    cols = nt * TOK
    with ExitStack() as ctx:
        def sb(name, shape, dt):
            return ctx.enter_context(nc.sbuf_tensor("e_" + name, shape, dt))

        def sem(name):
            return ctx.enter_context(nc.semaphore("e_" + name))

        y = sb("y", [TOK, nt, D], F32)
        n1 = sb("n1", [TOK, nt, D], F32)
        sq = sb("sq", [TOK, nt, D], F32)
        st = sb("st", [TOK, 5, nt], F32)
        x1 = sb("x1", [TOK, nt, D], F32)
        nT = sb("nT", [P, cols], F32)
        pr = sb("pr", [TOK, 6, nt, E], F32)
        top = sb("top", [TOK, 3, nt], F32)
        order = sb("order", [TOK, E], F32)
        ind = sb("ind", [E, cols], F32)
        w1 = sb("w1", [P, 2, F0], F32)
        w2 = sb("w2", [P, 2, F0], F32)
        b1 = sb("b1", [P, 2, FT], F32)
        comb = sb("comb", [P, 2, cols], F32)
        hid = sb("hid", [P, 2, GC], F32)
        hw = sb("hw", [P, 2, GC], F32)
        oT = sb("oT", [P, cols], F32)
        acc = [ctx.enter_context(nc.psum_tensor(f"e_acc{g}", [P, 512], F32)) for g in range(ng)]
        ps = [ctx.enter_context(nc.psum_tensor(f"e_ps{i}", [P, 512], F32)) for i in range(2)]
        pl = ctx.enter_context(nc.psum_tensor("e_pl", [P, 512], F32))
        y_loaded, chain_sem, roots = sem("y_loaded"), sem("chain"), sem("roots")
        n1_done, turned, copied, mixed, mixed_read = sem("n1_done"), sem("turned"), sem("copied"), sem("mixed"), sem("mixed_read")
        n2_done, routed, chosen, comb_saved, comb_turned = sem("n2_done"), sem("routed"), sem("chosen"), sem("comb_saved"), sem("comb_turned")
        comb_copied, acc_set = sem("comb_copied"), sem("acc_set")
        loaded = [sem("loaded0"), sem("loaded1")]
        hidden, silus, weighted, added = sem("hidden"), sem("silus"), sem("weighted"), sem("added")
        acc_read, back, outed, out_saved = sem("acc_read"), sem("back"), sem("outed"), sem("out_saved")
        ex, chosen_ex = sem("ex"), sem("chosen_ex")
        block = ctx.enter_context(nc.Block())
        PER = FT * ng

        @block.sync
        def _(sp):
            sp.dma_start(y[:, :, :], m.y_dram.rearrange("b s d -> (b s) d").rearrange("(n p) d -> p n d", p=TOK))\
                .then_inc(y_loaded, 16)
            sp.wait_ge(comb_copied, ng)
            sp.dma_start(m.comb_dram, ind[:, :]).then_inc(comb_saved, 16)
            sp.wait_ge(comb_saved, 16)
            with sp.Fori(0, E // 2) as lap:
                for u in range(2):
                    e = 2 * lap + u
                    sp.wait_ge(added, 2 * PER * lap + PER * u)
                    sp.dma_start(w1[:, u, :], m.w1_dram[e]).then_inc(loaded[u], 16)
                    sp.dma_start(w2[:, u, :], m.w2_dram[e]).then_inc(loaded[u], 16)
                    sp.dma_start(b1[:, u, :], m.b1_dram[e]).then_inc(loaded[u], 16)
                    sp.dma_start(comb[:, u, :], m.comb_dram[e].partition_broadcast(P)).then_inc(loaded[u], 16)
            sp.wait_ge(outed, ng + 1)
            sp.dma_start(m.out_dram.rearrange("b s d -> (b s) d").rearrange("(n p) d -> p n d", p=TOK), m.x[:, :, :])\
                .then_inc(out_saved, 16)
            sp.wait_ge(out_saved, 16)

        @block.vector
        def _(dve):
            chain = Chain(dve, chain_sem)
            for e in range(E):
                last = nc.vector.memset(order[:, e:e + 1], float(E - e))
            dve.wait_ge(y_loaded, 16)
            chain.then(nc.vector.tensor_tensor(y[:, :, :], y[:, :, :], per_channel(m.yb[1][:, :], nt), ALU.add))
            chain.then(nc.vector.scalar_tensor_tensor(out=m.x[:, :, :], in0=y[:, :, :], scalar=m.gates[0:TOK, 1:2],
                                                      in1=m.x[:, :, :], op0=ALU.mult, op1=ALU.add))
            norm_vector(nc, dve, chain, roots, m.x[:, :, :], x1[:, :, :], sq[:, :, :], st, nt, 1)
            norm_vector(nc, dve, chain, roots, x1[:, :, :], n1[:, :, :], sq[:, :, :], st, nt, 2)
            chain.then(nc.vector.tensor_tensor(n1[:, :, :], n1[:, :, :], per_channel(row(m, "g1", TOK), nt), ALU.mult))
            nc.vector.tensor_tensor(n1[:, :, :], n1[:, :, :], per_channel(row(m, "be1", TOK), nt), ALU.add)\
                .then_inc(n1_done, 1)
            dve.wait_ge(n1_done, 1)
            chain.then(nc.vector.tensor_tensor(x1[:, :, :], x1[:, :, :], n1[:, :, :], ALU.add))
            chain.then(nc.vector.tensor_tensor(x1[:, :, :], x1[:, :, :], per_channel(row(m, "mix_b", TOK), nt), ALU.add))
            for g in range(ng):
                dve.wait_ge(mixed, g + 1)
                nc.vector.tensor_tensor(x1[:, g * gt:(g + 1) * gt, :], x1[:, g * gt:(g + 1) * gt, :],
                                        acc[g][0:TOK, 0:gt * D].rearrange("p (i d) -> p i d", i=gt), ALU.add)\
                    .then_inc(mixed_read, 1)
            dve.wait_ge(mixed_read, ng)
            norm_vector(nc, dve, chain, roots, x1[:, :, :], n1[:, :, :], sq[:, :, :], st, nt, 3)
            dve.wait_ge(routed, 1)
            logits = pl[0:TOK, 0:nt * E].rearrange("p (i e) -> p i e", e=E)

            def spread(ap):
                return per_token(ap, nt, E)

            chain.then(nc.vector.tensor_reduce(top[:, 0, :], logits, AX.X, ALU.max))
            nc.vector.tensor_tensor(pr[:, 0, :, :], logits, spread(top[:, 0, :]), ALU.subtract).then_inc(ex, 1)
            dve.wait_ge(ex, 2)
            chain.then(nc.vector.tensor_reduce(top[:, 1, :], pr[:, 1, :, :], AX.X, ALU.add))
            chain.then(nc.vector.reciprocal(top[:, 2, :], top[:, 1, :]))
            chain.then(nc.vector.tensor_tensor(pr[:, 0, :, :], pr[:, 1, :, :], spread(top[:, 2, :]), ALU.mult))
            chain.then(nc.vector.tensor_copy(pr[:, 5, :, :], pr[:, 0, :, :]))
            for n in (3, 4):
                chain.then(nc.vector.tensor_reduce(top[:, 0, :], pr[:, 5, :, :], AX.X, ALU.max))
                chain.then(nc.vector.tensor_tensor(pr[:, 2, :, :], pr[:, 5, :, :], spread(top[:, 0, :]), ALU.is_equal))
                chain.then(nc.vector.tensor_tensor(pr[:, 2, :, :], pr[:, 2, :, :],
                                                   order[:, :].unsqueeze(1).to_broadcast([TOK, nt, E]), ALU.mult))
                chain.then(nc.vector.tensor_reduce(top[:, 1, :], pr[:, 2, :, :], AX.X, ALU.max))
                chain.then(nc.vector.tensor_tensor(pr[:, n, :, :], pr[:, 2, :, :], spread(top[:, 1, :]), ALU.is_equal))
                if n == 3:
                    chain.then(nc.vector.scalar_tensor_tensor(
                        out=pr[:, 5, :, :], in0=pr[:, 3, :, :], scalar=-2.0, in1=pr[:, 5, :, :],
                        op0=ALU.mult, op1=ALU.add))
            chain.then(nc.vector.tensor_tensor(pr[:, 3, :, :], pr[:, 3, :, :], pr[:, 4, :, :], ALU.add))
            nc.vector.tensor_tensor(pr[:, 2, :, :], pr[:, 3, :, :], pr[:, 0, :, :], ALU.mult).then_inc(chosen, 1)
            dve.sem_inc(weighted, 2)
            with dve.Fori(0, E // 2) as lap:
                for u in range(2):
                    dve.wait_ge(loaded[u], 64 * lap + 64)
                    for f in range(FT):
                        for g in range(ng):
                            n = PER * u + f * ng + g
                            at = 2 * PER * lap + n
                            dve.wait_ge(silus, at + 3)
                            dve.wait_ge(added, at - 1 + PER)
                            nc.vector.tensor_tensor(hw[:, n % 2, 0:gc], hid[:, n % 2, 0:gc],
                                                    comb[:, u, g * gc:(g + 1) * gc], ALU.mult).then_inc(weighted, 1)
            for g in range(ng):
                dve.wait_ge(back, g + 1)
                nc.vector.tensor_tensor(x1[:, g * gt:(g + 1) * gt, :], x1[:, g * gt:(g + 1) * gt, :],
                                        ps[g % 2][0:TOK, 0:gt * D].rearrange("p (i d) -> p i d", i=gt), ALU.add)\
                    .then_inc(outed, 1)
            dve.wait_ge(outed, ng)
            nc.vector.scalar_tensor_tensor(out=m.x[:, :, :], in0=x1[:, :, :], scalar=m.gates[0:TOK, 3:4],
                                           in1=m.x[:, :, :], op0=ALU.mult, op1=ALU.add).then_inc(outed, 1)

        first_norm = 2
        second_norm = first_norm + 2 * NORM_LINKS + 1 + 2

        @block.scalar
        def _(act):
            norm_scalar(nc, act, m, chain_sem, first_norm + NORM_SUM, roots, st)
            norm_scalar(nc, act, m, chain_sem, first_norm + NORM_LINKS + NORM_SUM, roots, st)
            for g in range(ng):
                act.wait_ge(turned, g + 1)
                nc.scalar.activation(nT[:, g * gc:(g + 1) * gc], ps[g % 2][:, 0:gc], ACT.Copy).then_inc(copied, 1)
            norm_scalar(nc, act, m, chain_sem, second_norm + NORM_SUM, roots, st)
            for g in range(ng):
                act.wait_ge(turned, ng + g + 1)
                nc.scalar.activation(nT[:, g * gc:(g + 1) * gc], ps[g % 2][:, 0:gc], ACT.Identity,
                                     bias=col(m, "be2"), scale=col(m, "g2")).then_inc(copied, 1)
            act.wait_ge(ex, 1)
            nc.scalar.activation(pr[:, 1, :, :], pr[:, 0, :, :], ACT.Exp).then_inc(ex, 1)
            for g in range(ng):
                act.wait_ge(comb_turned, g + 1)
                nc.scalar.activation(ind[:, g * gc:(g + 1) * gc], ps[g % 2][0:E, 0:gc], ACT.Copy).then_inc(comb_copied, 1)
            act.sem_inc(silus, 2)
            with act.Fori(0, E // 2) as lap:
                for u in range(2):
                    act.wait_ge(loaded[u], 64 * lap + 64)
                    for f in range(FT):
                        for g in range(ng):
                            n = PER * u + f * ng + g
                            at = 2 * PER * lap + n
                            act.wait_ge(hidden, at + 1)
                            act.wait_ge(weighted, at + 1)
                            nc.scalar.activation(hid[:, n % 2, 0:gc], ps[n % 2][:, 0:gc], ACT.Silu,
                                                 bias=b1[:, u, f:f + 1]).then_inc(silus, 1)
            act.wait_ge(added, PER + E * PER)
            for g in range(ng):
                nc.scalar.activation(oT[:, g * gc:(g + 1) * gc], acc[g][:, 0:gc], ACT.Copy).then_inc(acc_read, 1)

        @block.tensor
        def _(pe):
            ident = mat(m, "ident")

            def turn(base):
                for g in range(ng):
                    if g >= 2:
                        pe.wait_ge(copied, base + g - 1)
                    for i in range(gt):
                        last = nc.tensor.transpose(ps[g % 2][:, i * TOK:(i + 1) * TOK], n1[:, g * gt + i, :],
                                                   ident[0:TOK, 0:TOK])
                    last.then_inc(turned, 1)

            pe.wait_ge(n1_done, 1)
            turn(0)
            for g in range(ng):
                pe.wait_ge(copied, g + 1)
                for i in range(gt):
                    at = (g * gt + i) * TOK
                    last = nc.tensor.matmul(acc[g][0:TOK, i * D:(i + 1) * D], nT[:, at:at + TOK], mat(m, "mix"),
                                            start=True, stop=True)
                last.then_inc(mixed, 1)
            pe.wait_ge(chain_sem, second_norm + NORM_LINKS)
            pe.wait_ge(copied, ng)
            turn(ng)
            pe.wait_ge(copied, 2 * ng)
            for i in range(nt):
                last = nc.tensor.matmul(pl[0:TOK, i * E:(i + 1) * E], nT[:, i * TOK:(i + 1) * TOK], m.router[:, :],
                                        start=True, stop=True)
            last.then_inc(routed, 1)
            pe.wait_ge(chosen, 1)
            for g in range(ng):
                if g >= 2:
                    pe.wait_ge(comb_copied, g - 1)
                for i in range(gt):
                    last = nc.tensor.transpose(ps[g % 2][0:E, i * TOK:(i + 1) * TOK], pr[:, 2, g * gt + i, :],
                                               ident[0:TOK, 0:TOK])
                last.then_inc(comb_turned, 1)
            pe.wait_ge(comb_copied, ng)
            pe.wait_ge(mixed_read, ng)
            for g in range(ng):
                nc.tensor.matmul(acc[g][:, 0:gc], m.b2e[:, :], ind[:, g * gc:(g + 1) * gc], start=True, stop=False,
                                 skip_group_check=True)

            pe.sem_inc(added, PER)

            def first(lap, u, n):
                f, g = (n // ng) % FT, n % ng
                pe.wait_ge(silus, 2 * PER * lap + n + 1)
                nc.tensor.matmul(ps[n % 2][:, 0:gc], w1[:, u, f * P:(f + 1) * P], nT[:, g * gc:(g + 1) * gc],
                                 start=True, stop=True).then_inc(hidden, 1)

            def second(lap, u, n):
                f, g = (n // ng) % FT, n % ng
                pe.wait_ge(weighted, 2 * PER * lap + n + 3)
                nc.tensor.matmul(acc[g][:, 0:gc], w2[:, u, f * P:(f + 1) * P], hw[:, n % 2, 0:gc],
                                 start=False, stop=True, skip_group_check=True).then_inc(added, 1)

            with pe.Fori(0, E // 2) as lap:
                for u in range(2):
                    pe.wait_ge(loaded[u], 64 * lap + 64)
                    for n in range(PER * u, PER * u + PER):
                        if n == PER * u:
                            first(lap, u, n)
                        if n + 1 < PER * u + PER:
                            first(lap, u, n + 1)
                        second(lap, u, n)
            for g in range(ng):
                pe.wait_ge(acc_read, g + 1)
                if g >= 2:
                    pe.wait_ge(outed, g - 1)
                for i in range(gt):
                    at = (g * gt + i) * TOK
                    last = nc.tensor.transpose(ps[g % 2][0:TOK, i * D:(i + 1) * D], oT[:, at:at + TOK], ident)
                last.then_inc(back, 1)


def program(nc, nb, x_dram, ctx_dram, mask_dram, mats_dram, cols_dram, rows_dram, router_dram, b2e_dram,
            w1_dram, w2_dram, b1_dram, out_dram):
    nt = nb // 2
    with ExitStack() as ctx:
        def sb(name, shape, dt):
            return ctx.enter_context(nc.sbuf_tensor(name, shape, dt))

        def dram(name, shape, dt):
            return nc.dram_tensor(name, shape, dt, kind="Internal").ap()

        m = Shared()
        m.nb = nb
        m.nt = nt
        m.x_dram = x_dram
        m.ctx_dram = ctx_dram
        m.mask_dram = mask_dram
        m.mats_dram = mats_dram
        m.cols_dram = cols_dram
        m.rows_dram = rows_dram
        m.router_dram = router_dram
        m.b2e_dram = b2e_dram
        m.w1_dram = w1_dram
        m.w2_dram = w2_dram
        m.b1_dram = b1_dram
        m.out_dram = out_dram
        m.z_dram = dram("z_scratch", [nb, CTX, D], F32)
        m.keep_dram = dram("keep_scratch", [nb, CTX], BF16)
        m.fill_dram = dram("fill_scratch", [nb, 3, CTX], BF16)
        m.q_dram = dram("q_scratch", [TERMS, PR, PAIRS, nb, PQ], BF16)
        m.k_dram = dram("k_scratch", [3, 3, PR, PAIRS, CTX], BF16)
        m.y_dram = dram("y_scratch", [nb, S, D], F32)
        m.comb_dram = dram("comb_scratch", [E, nb * S], F32)
        m.x = sb("x", [TOK, nt, D], F32)
        m.mats = sb("mats", [P, len(MATS) * P], F32)
        m.cols = sb("cols", [P, len(COLS)], F32)
        m.rows = sb("rows", [P, ROW_W], F32)
        m.router = sb("router", [P, E], F32)
        m.b2e = sb("b2e", [E, D], F32)
        m.identb = sb("identb", [P, P], BF16)
        m.gates = sb("gates", [P, 4], F32)
        m.eps = sb("eps", [P, 1], F32)
        m.wk = [sb("wk_0", [P, P], F32), sb("wk_1", [P, P], F32)]
        m.wv = [sb("wv_0", [P, P], F32), sb("wv_1", [P, P], F32)]
        m.bk = [sb("bk_0", [P, 1], F32), sb("bk_1", [P, 1], F32)]
        m.yb = [sb("yb_0", [TOK, D], F32), sb("yb_1", [TOK, D], F32)]
        setup(nc, m)
        queries(nc, m, 0)
        attention(nc, m, 0)
        ffn_ternary(nc, m)
        context_norm(nc, m)
        queries(nc, m, 1)
        attention(nc, m, 1)
        ffn_experts(nc, m)


def layouts(inputs):
    import numpy as np

    a = {k: np.asarray(v) for k, v in inputs.items()}
    f = np.float32
    mats = {
        "wq0": a["L0_xattn_Wq"].T, "wk0": a["L0_xattn_Wk"].T, "wv0": a["L0_xattn_Wv"].T, "wo0": a["L0_xattn_Wo"].T,
        "wq1": a["L1_xattn_w_q"], "wk1": a["L1_xattn_w_kv"][:, :D], "wv1": a["L1_xattn_w_kv"][:, D:],
        "wo1": a["L1_xattn_w_proj"], "mix": a["L1_ffn_mix_w"], "ident": np.eye(P, dtype=f),
    }
    pick = np.zeros((P, P), f)
    for i in range(P):
        pick[i // 32 * 32 + PR, i] = 1.0
    mats["pick"] = pick
    for layer in range(2):
        wo = mats[f"wo{layer}"]
        for n in range(4):
            r, odd = n // 2, n % 2
            w = np.zeros((P, P), f)
            for q in range(4):
                h = 2 * (4 * r + q) + odd
                w[32 * q + HD * odd:32 * q + HD * odd + HD] = wo[h * HD:(h + 1) * HD]
            mats[f"woh{layer}{'abcd'[n]}"] = w
    w1 = a["L0_ffn_w1"].T
    w2 = a["L0_ffn_w2"].T
    for n in range(4):
        mats["f" + "abcd"[n]] = w1[:, n * P:(n + 1) * P]
        mats["g" + "abcd"[n]] = w2[n * P:(n + 1) * P, :]
    parity = (np.arange(P) // HD) % 2
    cols = {
        "bq0": a["L0_xattn_bq"], "bk0": a["L0_xattn_bk"], "bv0": a["L0_xattn_bv"], "g_x": a["L1_xattn_g_x"],
        "b_x": a["L1_xattn_b_x"], "g_kv": a["L1_xattn_g_kv"], "b_kv": a["L1_xattn_b_kv"], "g2": a["L1_ffn_g2"],
        "be2": a["L1_ffn_be2"], "even": (1 - parity).astype(f), "odd": parity.astype(f),
    }
    rows = {
        "bo0": a["L0_xattn_bo"], "b2": a["L0_ffn_b2"], "b1": a["L0_ffn_b1"], "bo1": a["L1_xattn_b_proj"],
        "g1": a["L1_ffn_g1"], "be1": a["L1_ffn_be1"], "mix_b": a["L1_ffn_mix_b"],
        "gates": np.concatenate([a["g_xattn"], a["g_ffn"]]),
    }
    out = {
        "x": a["x"], "ctx": a["ctx_1024"], "mask": a["mask_BxS2_ik0"],
        "mats": np.concatenate([mats[k] for k in MATS], axis=1),
        "cols": np.stack([cols[k] for k in COLS], axis=1),
        "rows": np.concatenate([rows[k] for k, _ in ROWS]),
        "router": a["L1_ffn_router_w"], "b2e": a["L1_ffn_b2"],
        "w1": a["L1_ffn_w1"],
        "w2": a["L1_ffn_w2"].reshape(E, FT, P, D).transpose(0, 2, 1, 3).reshape(E, P, FT * D),
        "b1": a["L1_ffn_b1"].reshape(E, FT, P).transpose(0, 2, 1),
    }
    return {k: np.ascontiguousarray(v) for k, v in out.items()}


def kernel(**inputs):
    import concourse.bacc as bacc
    from concourse.bass_utils import run_bass_kernel_spmd

    arrays = layouts(inputs)
    nb = arrays["x"].shape[0]
    nc = bacc.Bacc("TRN2", target_bir_lowering=False, num_devices=1)
    args = {f"{k}_dram": nc.dram_tensor(f"in_{k}", v.shape, mybir.dt.from_np(v.dtype), kind="ExternalInput").ap()
            for k, v in arrays.items()}
    out = nc.dram_tensor("out_x", (nb, S, D), F32, kind="ExternalOutput").ap()
    program(nc, nb, out_dram=out, **args)
    r = run_bass_kernel_spmd(nc, [{f"in_{k}": v for k, v in arrays.items()}], core_ids=[0])
    return r.results[0]["out_x"]
```

```python
from contextlib import ExitStack

import concourse.bass as bass
from concourse import mybir

F32 = mybir.dt.float32
BF16 = mybir.dt.bfloat16
I32 = mybir.dt.int32
ACT = mybir.ActivationFunctionType
ALU = mybir.AluOpType
AX = mybir.AxisListType

D = 128
HEADS = 16
HD = D // HEADS
S = 56
CTX = 1500
P = 128
KT = -(-CTX // P)
LAST = CTX - (KT - 1) * P
PAIRS = HEADS // 2
PR = 2 * HD
PQ = 2 * S
PARTS_K = (0, 0, 0, 1, 1, 2)
PARTS_Q = (0, 1, 2, 0, 1, 0)
TERMS = len(PARTS_K)
SPLIT = TERMS * PR
FILLED = SPLIT + 3
STACK = FILLED + 3
CH = 500
NCH = CTX // CH
VW = PR + 1
TOK = 2 * S
EPS = 1e-5
SCALE = float(HD) ** -0.5
FILL = (998244352.0, 1753088.0, 2560.0)
MAGIC = 12582912.0
F0 = 512
FT = F0 // P
E = 8
GT = 4
GC = GT * TOK

MATS = ("wq0", "wk0", "wv0", "wo0", "wq1", "wk1", "wv1", "wo1", "mix", "ident", "pick",
        "woh0a", "woh0b", "woh0c", "woh0d", "woh1a", "woh1b", "woh1c", "woh1d",
        "fa", "fb", "fc", "fd", "ga", "gb", "gc", "gd")
COLS = ("g1", "be1", "bq0", "bk0", "bv0", "g_x", "b_x", "g_kv", "b_kv", "g2", "be2", "even", "odd")
ROWS = (("bo0", D), ("b2", D), ("b1", F0), ("bo1", D), ("g1", D), ("be1", D), ("mix_b", D), ("gates", 4))
ROW_AT = {}
for _name, _width in ROWS:
    ROW_AT[_name] = sum(w for _, w in ROWS[:len(ROW_AT)])
ROW_W = sum(w for _, w in ROWS)
STATS_FROM = 5
KEYS = ("turn", "key")
VALUES_AT = (6, 8, 10)
LOOSE = ("score", "mix", "mid", "stat")
PEAKS_BY = (0, 3, 6, 9, 12, 14, 16, 18, 20, 22, 24, 24, 24)
RING = 3


class Shared:
    pass


class Step:

    def __init__(self, lap, u, first, laps, make, peak, mix, finish):
        self.lap, self.u, self.first, self.laps = lap, u, first, laps
        self.make, self.peak, self.mix, self.finish = make, peak, mix, finish

    def batch(self, ahead):
        return 3 * self.lap + (self.u + ahead)

    def buf(self, ahead):
        return (self.u + ahead) % 3

    def use(self, ahead):
        return self.lap + (self.u + ahead) // 3

    def items(self):
        order = [("peak", p, j) for p in range(PAIRS) for j in range(NCH)]
        peaks = [order[PEAKS_BY[kt]:PEAKS_BY[kt + 1]] for kt in range(KT)]
        out = []
        for kt in range(KT):
            if self.mix:
                out.append(("score", kt, 0))
            if self.finish:
                out += {1: [("total", 0, 0)], 6: [("project", 0, 0)]}.get(kt, [])
            made = [(KEYS[kt], n, 0) for n in range(3)] if self.make and kt < len(KEYS) else []
            found = peaks[kt] if self.peak else []
            for n in range(max(len(made), len(found))):
                out += made[n:n + 1] + found[n:n + 1]
            if self.make:
                out += {3: [("mid", 0, 0)], 4: [("mid", 1, 0)], 5: [("mid", 2, 0)],
                        VALUES_AT[0]: [("value", 0, 0)], VALUES_AT[1]: [("value", 1, 0)],
                        VALUES_AT[2]: [("value", 2, 0)]}.get(kt, [])
            if self.make and STATS_FROM <= kt < STATS_FROM + KT // 2:
                out += [("stat", 2 * (kt - STATS_FROM) + n, 0) for n in range(2)]
            if self.mix and kt:
                out.append(("mix", kt - 1, 0))
        if self.peak:
            out += [("shift", 0, 0), ("shift", 1, 0)]
        if self.mix:
            out.append(("mix", KT - 1, 0))
        return out

    def slots(self):
        n, out = 0, []
        for kind, a, b in self.items():
            if kind in LOOSE:
                out.append((kind, a, b, 0, 0))
            else:
                at = self.first + n
                out.append((kind, a, b, at % RING, at // RING + self.laps))
                n += 1
        return out

    def width(self):
        return sum(kind not in LOOSE for kind, _, _ in self.items())


def run_steps(eng, nb, body):
    first = 0
    for s in range(-2, 3):
        step = Step(s // 3, s % 3, first, 0, True, s >= -1, s >= 0, s >= 1)
        body(step)
        first += step.width()
    steady = Step(1, 0, 0, 0, True, True, True, True).width()
    with eng.Fori(1, (nb - 2) // 3) as lap:
        for u in range(3):
            body(Step(lap, u, first + (u - 3) * steady, lap * steady, True, True, True, True))
    first += (nb - 5) * steady
    for s in (nb - 2, nb - 1, nb):
        step = Step(s // 3, s % 3, first, 0, False, s == nb - 2, s < nb, True)
        body(step)
        first += step.width()


def rows_of(kt):
    return P if kt < KT - 1 else LAST


def setup(nc, m):
    with ExitStack() as ctx:
        mask = ctx.enter_context(nc.sbuf_tensor("mask", [m.nb, CTX], I32))
        keep = ctx.enter_context(nc.sbuf_tensor("keep", [m.nb, CTX], BF16))
        fill = ctx.enter_context(nc.sbuf_tensor("fill", [m.nb, 3, CTX], BF16))
        loaded = ctx.enter_context(nc.semaphore("setup_loaded"))
        mask_loaded = ctx.enter_context(nc.semaphore("mask_loaded"))
        made = ctx.enter_context(nc.semaphore("masks_made"))
        saved = ctx.enter_context(nc.semaphore("masks_saved"))
        tanhs = ctx.enter_context(nc.semaphore("tanhs"))
        block = ctx.enter_context(nc.Block())

        @block.sync
        def _(sp):
            sp.dma_start(mask[:, :], m.mask_dram).then_inc(mask_loaded, 16)
            sp.dma_start(m.x[:, :, :], m.x_dram.rearrange("b s d -> (b s) d").rearrange(
                "(n p) d -> p n d", p=TOK)).then_inc(loaded, 16)
            sp.dma_start(m.mats[:, :], m.mats_dram).then_inc(loaded, 16)
            sp.dma_start(m.cols[:, :], m.cols_dram).then_inc(loaded, 16)
            sp.dma_start(m.rows[:, :], m.rows_dram.partition_broadcast(P)).then_inc(loaded, 16)
            sp.dma_start(m.router[:, :], m.router_dram).then_inc(loaded, 16)
            sp.dma_start(m.b2e[:, :], m.b2e_dram).then_inc(loaded, 16)
            sp.wait_ge(made, 4)
            sp.dma_start(m.keep_dram, keep[:, :]).then_inc(saved, 16)
            sp.dma_start(m.fill_dram, fill[:, :, :]).then_inc(saved, 16)
            sp.wait_ge(loaded, 16 * 6)
            sp.wait_ge(saved, 32)

        @block.vector
        def _(dve):
            dve.wait_ge(mask_loaded, 16)
            nc.vector.tensor_scalar(keep[:, :], mask[:, :], 0.0, None, ALU.not_equal).then_inc(made, 1)
            dve.wait_ge(made, 1)
            for n in range(3):
                nc.vector.tensor_scalar(fill[:, n, :], keep[:, :], 1.0, FILL[n], ALU.subtract, ALU.mult)\
                    .then_inc(made, 1)

        @block.scalar
        def _(act):
            act.wait_ge(loaded, 16 * 6)
            nc.scalar.activation(m.identb[:, :], mat(m, "ident"), ACT.Copy).then_inc(tanhs, 1)
            nc.scalar.activation(m.gates[:, :], m.rows[:, ROW_AT["gates"]:ROW_AT["gates"] + 4], ACT.Tanh)\
                .then_inc(tanhs, 1)
            act.wait_ge(tanhs, 2)


def mat(m, name):
    at = MATS.index(name) * P
    return m.mats[:, at:at + P]


def col(m, name):
    at = COLS.index(name)
    return m.cols[:, at:at + 1]


def row(m, name, p=P):
    at = ROW_AT[name]
    return m.rows[0:p, at:at + dict(ROWS)[name]]


def per_token(ap, nt, width=D):
    return ap.unsqueeze(2).to_broadcast([TOK, nt, width])


def per_channel(ap, nt, width=D):
    return ap.unsqueeze(1).to_broadcast([TOK, nt, width])


class Chain:

    def __init__(self, eng, sem):
        self.eng, self.sem, self.n = eng, sem, 0

    def then(self, ins):
        self.n += 1
        ins.then_inc(self.sem, 1)
        self.eng.wait_ge(self.sem, self.n)

    def mark(self, ins):
        self.n += 1
        ins.then_inc(self.sem, 1)
        return self.n


def norm_vector(nc, dve, chain, roots, src, dst, tmp, st, nt, turn):
    for i in range(nt):
        last = nc.vector.bn_stats(tmp[:, i, 0:6], src[:, i, :])
    chain.then(last)
    even, odd, apart, squares = tmp[:, :, 1], tmp[:, :, 4], tmp[:, :, 6], tmp[:, :, 7]
    chain.mark(nc.vector.tensor_tensor(apart, even, odd, ALU.subtract))
    chain.mark(nc.vector.tensor_tensor(squares, tmp[:, :, 2], tmp[:, :, 5], ALU.add))
    chain.then(nc.vector.tensor_tensor(st[:, 0, :], even, odd, ALU.add))
    chain.then(nc.vector.scalar_tensor_tensor(out=apart, in0=apart, scalar=D / 4.0, in1=apart,
                                              op0=ALU.mult, op1=ALU.mult))
    chain.then(nc.vector.tensor_tensor(st[:, 2, :], squares, apart, ALU.add))
    chain.mark(nc.vector.tensor_scalar(st[:, 1, :], st[:, 0, :], 0.5, None, ALU.mult))
    dve.wait_ge(roots, turn)
    chain.then(nc.vector.reciprocal(st[:, 4, :], st[:, 3, :]))
    for i in range(nt):
        last = nc.vector.tensor_scalar(dst[:, i, :], src[:, i, :], st[:, 1, i:i + 1], st[:, 4, i:i + 1],
                                       ALU.subtract, ALU.mult)
    chain.then(last)


NORM_LINKS = 9
NORM_SUM = 6


def norm_scalar(nc, act, m, chain_sem, at, roots, st):
    act.wait_ge(chain_sem, at)
    nc.scalar.activation(st[:, 3, :], st[:, 2, :], ACT.Sqrt, bias=m.eps[0:TOK, 0:1], scale=1.0 / D)\
        .then_inc(roots, 1)


def queries(nc, m, layer):
    nt, ng = m.nt, m.nt // GT if m.nt >= GT else 1
    gt = min(GT, m.nt)
    gc = gt * TOK
    L = str(layer)
    norms = 1 + layer
    cols = nt * TOK
    with ExitStack() as ctx:
        def sb(name, shape, dt):
            return ctx.enter_context(nc.sbuf_tensor(f"q{L}_{name}", shape, dt))

        def sem(name):
            return ctx.enter_context(nc.semaphore(f"q{L}_{name}"))

        z = sb("z", [TOK, nt, D], F32)
        sq = sb("sq", [TOK, nt, D], F32)
        st = sb("st", [TOK, 5, nt], F32)
        zT = sb("zT", [P, cols], F32)
        qf = sb("qf", [P, cols], F32)
        rest = sb("rest", [P, cols], F32)
        part = sb("part", [P, 3, cols], BF16)
        block_q = sb("block_q", [P, 3, m.nb, PQ], BF16)
        wq = sb("wq", [P, P], F32)
        bq = sb("bq", [P, 1], F32)
        bvb = sb("bvb", [P, TOK], F32)
        turned = [ctx.enter_context(nc.psum_tensor(f"q{L}_turned{g}", [P, 512], F32)) for g in range(ng)]
        qps = ctx.enter_context(nc.psum_tensor(f"q{L}_qps", [P, 2, 512], F32))
        small = ctx.enter_context(nc.psum_tensor(f"q{L}_small", [P, 512], F32))
        normed, roots, turns, turns_out = sem("normed"), sem("roots"), sem("turns"), sem("turns_out")
        folded, biases = sem("folded"), sem("biases")
        projected, steps, blocks, saved = sem("projected"), sem("steps"), sem("blocks"), sem("saved")
        eps_set = sem("eps_set")
        block = ctx.enter_context(nc.Block())
        last_norm = NORM_LINKS * norms

        @block.vector
        def _(dve):
            if layer == 0:
                nc.vector.memset(m.eps[:, :], EPS).then_inc(eps_set, 1)
            chain = Chain(dve, normed)
            src = m.x
            for n in range(norms):
                norm_vector(nc, dve, chain, roots, src[:, :, :], z[:, :, :], sq[:, :, :], st, nt, n + 1)
                src = z
            if layer == 0:
                nc.vector.tensor_copy(wq[:, :], mat(m, "wq0")).then_inc(folded, 1)
                nc.vector.tensor_copy(m.wk[0][:, :], mat(m, "wk0")).then_inc(folded, 1)
                nc.vector.tensor_copy(m.wv[0][:, :], mat(m, "wv0")).then_inc(folded, 1)
                nc.vector.tensor_copy(bq[:, :], col(m, "bq0")).then_inc(folded, 1)
                nc.vector.tensor_copy(m.bk[0][:, :], col(m, "bk0")).then_inc(folded, 1)
                nc.vector.tensor_copy(bvb[:, :], col(m, "bv0").to_broadcast([P, TOK])).then_inc(folded, 1)
            else:
                nc.vector.tensor_scalar(wq[:, :], mat(m, "wq1"), col(m, "g_x"), None, ALU.mult).then_inc(folded, 1)
                nc.vector.tensor_scalar(m.wk[1][:, :], mat(m, "wk1"), col(m, "g_kv"), None, ALU.mult).then_inc(folded, 1)
                nc.vector.tensor_scalar(m.wv[1][:, :], mat(m, "wv1"), col(m, "g_kv"), None, ALU.mult).then_inc(folded, 1)
                dve.wait_ge(biases, 1)
                nc.vector.tensor_copy(bq[:, :], small[:, 0:1]).then_inc(folded, 1)
                nc.vector.tensor_copy(m.bk[1][:, :], small[:, 1:2]).then_inc(folded, 1)
                nc.vector.tensor_copy(bvb[:, :], small[:, 2:3].to_broadcast([P, TOK])).then_inc(folded, 1)
            dve.wait_ge(biases, 2)
            nc.vector.tensor_tensor(m.yb[layer][:, :], small[0:TOK, 128:256], row(m, "bo" + L, TOK), ALU.add)\
                .then_inc(folded, 1)
            done = Chain(dve, steps)
            for g in range(ng):
                dve.wait_ge(projected, g + 1)
                dve.wait_ge(folded, 4)
                nc.vector.tensor_scalar(qf[:, g * gc:(g + 1) * gc], qps[:, g % 2, 0:gc], bq[:, 0:1], SCALE,
                                        ALU.add, ALU.mult).then_inc(steps, 1)
            done.n = ng
            dve.wait_ge(steps, ng)
            done.then(nc.vector.tensor_copy(part[:, 0, :], qf[:, :]))
            done.then(nc.vector.tensor_tensor(rest[:, :], qf[:, :], part[:, 0, :], ALU.subtract))
            done.then(nc.vector.tensor_copy(part[:, 1, :], rest[:, :]))
            done.then(nc.vector.tensor_tensor(part[:, 2, :], rest[:, :], part[:, 1, :], ALU.subtract))
            for n in range(3):
                for h, name in enumerate(("even", "odd")):
                    nc.vector.tensor_scalar(
                        block_q[:, n, :, h * S:(h + 1) * S], part[:, n, :].rearrange("p (b q) -> p b q", q=S),
                        col(m, name), None, ALU.mult).then_inc(blocks, 1)

        @block.scalar
        def _(act):
            if layer == 0:
                act.wait_ge(eps_set, 1)
            for n in range(norms):
                norm_scalar(nc, act, m, normed, NORM_LINKS * n + NORM_SUM, roots, st)
            for g in range(ng):
                act.wait_ge(turns, g + 1)
                nc.scalar.activation(zT[:, g * gc:(g + 1) * gc], turned[g][:, 0:gc], ACT.Copy)\
                    .then_inc(turns_out, 1)

        @block.tensor
        def _(pe):
            if layer == 1:
                for n, (w, b) in enumerate((("wq1", "b_x"), ("wk1", "b_kv"), ("wv1", "b_kv"))):
                    last = nc.tensor.matmul(small[:, n:n + 1], mat(m, w), col(m, b), start=True, stop=True)
                last.then_inc(biases, 1)
            else:
                pe.sem_inc(biases, 1)
            pe.wait_ge(folded, 6)
            nc.tensor.matmul(small[0:TOK, 128:256], bvb[:, :], mat(m, "wo" + L), start=True, stop=True)\
                .then_inc(biases, 1)
            pe.wait_ge(normed, last_norm)
            for g in range(ng):
                for i in range(gt):
                    last = nc.tensor.transpose(turned[g][:, i * TOK:(i + 1) * TOK], z[:, g * gt + i, :],
                                               mat(m, "ident")[0:TOK, 0:TOK])
                last.then_inc(turns, 1)
            for g in range(ng):
                pe.wait_ge(turns_out, g + 1)
                if g >= 2:
                    pe.wait_ge(steps, g - 1)
                nc.tensor.matmul(qps[:, g % 2, 0:gc], wq[:, :], zT[:, g * gc:(g + 1) * gc], start=True, stop=True)\
                    .then_inc(projected, 1)

        @block.sync
        def _(sp):
            for t in range(TERMS):
                n = PARTS_Q[t]
                sp.wait_ge(blocks, 2 * n + 2)
                sp.dma_start(m.q_dram[t].rearrange("r p b c -> p r (b c)"),
                             block_q[:, n, :, :].rearrange("p b c -> p (b c)")).then_inc(saved, 16)
            sp.wait_ge(saved, 16 * TERMS)


def key_norms(nc, m):
    nk = m.nb * KT
    with ExitStack() as ctx:
        def sb(name, shape, dt):
            return ctx.enter_context(nc.sbuf_tensor("kn_" + name, shape, dt))

        def sem(name):
            return ctx.enter_context(nc.semaphore("kn_" + name))

        st = sb("st", [P, nk, 6], F32)
        apart = sb("apart", [P, nk], F32)
        var = sb("var", [P, nk], F32)
        half = sb("half", [P, nk], F32)
        norms = sb("norms", [P, m.nb, 2, KT], F32)
        root = sb("root", [P, nk], F32)
        loaded, links, rooted, saved = sem("loaded"), sem("links"), sem("rooted"), sem("saved")
        block = ctx.enter_context(nc.Block())

        def by_batch(ap):
            return ap.rearrange("p (b c) -> p b c", c=KT)

        @block.sync
        def _(sp):
            sp.dma_start(st[:, :, :].rearrange("p k n -> p (k n)"), m.stats_dram.rearrange("p b n -> p (b n)"))\
                .then_inc(loaded, 16)
            sp.wait_ge(links, 8)
            sp.dma_start(m.norms_dram.rearrange("p b n -> p (b n)"), norms[:, :, :, :].rearrange("p b n c -> p (b n c)"))\
                .then_inc(saved, 16)
            sp.wait_ge(saved, 16)

        @block.vector
        def _(dve):
            chain = Chain(dve, links)
            even, odd = st[:, :, 1], st[:, :, 4]
            dve.wait_ge(loaded, 16)
            chain.then(nc.vector.tensor_scalar(half[:, :], odd, 0.5, None, ALU.mult))
            chain.then(nc.vector.tensor_tensor(apart[:, :], even, odd, ALU.subtract))
            chain.then(nc.vector.tensor_tensor(apart[:, :], apart[:, :], apart[:, :], ALU.mult))
            chain.then(nc.vector.tensor_scalar(apart[:, :], apart[:, :], 0.25, None, ALU.mult))
            chain.then(nc.vector.tensor_tensor(var[:, :], st[:, :, 2], st[:, :, 5], ALU.add))
            chain.mark(nc.vector.scalar_tensor_tensor(out=var[:, :], in0=var[:, :], scalar=1.0 / D, in1=apart[:, :],
                                                      op0=ALU.mult, op1=ALU.add))
            chain.mark(nc.vector.scalar_tensor_tensor(out=norms[:, :, 0, :], in0=by_batch(even), scalar=0.5,
                                                      in1=by_batch(half[:, :]), op0=ALU.mult, op1=ALU.add))
            dve.wait_ge(rooted, 1)
            chain.mark(nc.vector.reciprocal(norms[:, :, 1, :], by_batch(root[:, :])))

        @block.scalar
        def _(act):
            act.wait_ge(links, 6)
            nc.scalar.activation(root[:, :], var[:, :], ACT.Sqrt, bias=m.eps[:, 0:1]).then_inc(rooted, 1)


def attention(nc, m, layer):
    nb = m.nb
    raw_loads = 2 if layer == 0 else 3
    rows_a = SPLIT if layer == 0 else FILLED
    loads = 4 if layer == 0 else 5
    L = str(layer)
    with ExitStack() as ctx:
        def sb(name, shape, dt):
            return ctx.enter_context(nc.sbuf_tensor(f"a{L}_{name}", shape, dt))

        def sem(name):
            return ctx.enter_context(nc.semaphore(f"a{L}_{name}"))

        ones = sb("ones", [STACK, CTX], BF16)
        kstack = sb("kstack", [STACK, 3, PAIRS, CTX], BF16)
        qstack = sb("qstack", [STACK, 3, PAIRS, PQ], BF16)
        raw = sb("raw", [P, 3, KT, D], F32)
        stats = sb("stats", [P, KT, 6], F32) if layer == 0 else None
        norms = sb("norms", [P, 3, 2, KT], F32) if layer else None
        rawT = sb("rawT", [P, CTX], F32)
        kf = sb("kf", [P, CTX], F32)
        rest = sb("rest", [P, CTX], F32)
        part = sb("part", [P, 3, CTX], BF16)
        keep = sb("keep", [P, CTX], BF16) if layer else None
        vals = sb("vals", [P, 3, KT, PAIRS, VW], F32)
        probs = sb("probs", [P, 2, 2, GC], F32)
        mixed_sb = sb("mixed_sb", [P, 2 * PQ], F32)
        inverse = sb("inverse", [P, 2 * PQ], F32)
        heads = sb("heads", [P, 2, 2, S], F32)
        out_sb = sb("out_sb", [S, D], F32)
        peaks = sb("peaks", [PQ, PAIRS, NCH], F32)
        low = sb("low", [PQ, 3, PAIRS], F32)
        shift = sb("shift", [PQ, PAIRS, 6], BF16)
        scores = [ctx.enter_context(nc.psum_tensor(f"a{L}_scores{i}", [P, 2, 512], F32)) for i in range(2)]
        ring = [ctx.enter_context(nc.psum_tensor(f"a{L}_ring{i}", [P, 512], F32)) for i in range(RING)]
        mix_ps = ctx.enter_context(nc.psum_tensor(f"a{L}_mix", [P, 512], F32))

        ones_made, ones_spread, shift_set = sem("ones_made"), sem("ones_spread"), sem("shift_set")
        ready = sem("ready")
        raw_loaded = [sem(f"raw_loaded{i}") for i in range(3)]
        stats_made, stats_saved = sem("stats_made"), sem("stats_saved")
        centred, normed = sem("centred"), sem("normed")
        keep_loaded = sem("keep_loaded")
        filled = [sem(f"ring_filled{i}") for i in range(RING)]
        drained = [sem(f"ring_drained{i}") for i in range(RING)]
        high_made, rest_made, mid_made, low_made = sem("high_made"), sem("rest_made"), sem("mid_made"), sem("low_made")
        part_saved = [sem(f"part_saved{i}") for i in range(3)]
        stack_loaded = [sem(f"stack_loaded{i}") for i in range(3)]
        scored, exped, mixed, mix_read = sem("scored"), sem("exped"), sem("mixed"), sem("mix_read")
        shift_steps, normalised, out_saved = sem("shift_steps"), sem("normalised"), sem("out_saved")
        READY = 6
        SHIFTS = 6
        block = ctx.enter_context(nc.Block())

        @block.sync
        def _(sp):
            sp.wait_ge(ones_made, 1)
            for k in range(3):
                sp.dma_start(kstack[SPLIT:STACK, k, :, :],
                             ones[SPLIT:STACK, :].unsqueeze(1).to_broadcast([STACK - SPLIT, PAIRS, CTX]))\
                    .then_inc(ones_spread, 16)
            sp.wait_ge(ready, READY - 1)
            sp.wait_ge(ones_spread, 48)
            sp.sem_inc(ready, 1)

            def load_context(k, batch):
                sp.dma_start(raw[:, k, 0:KT - 1, :], m.ctx_dram[batch, 0:(KT - 1) * P, :].rearrange(
                    "(c p) d -> p c d", p=P)).then_inc(raw_loaded[k], 16)
                sp.dma_start(raw[0:LAST, k, KT - 1, :], m.ctx_dram[batch, (KT - 1) * P:CTX, :])\
                    .then_inc(raw_loaded[k], 16)
                if layer:
                    sp.dma_start(norms[:, k, :, :].rearrange("p n c -> p (n c)"), m.norms_dram[:, batch, :])\
                        .then_inc(raw_loaded[k], 16)

            load_context(0, 0)

            def step(s):
                if not s.make:
                    return
                load_context(s.buf(3), s.batch(3) % nb)
                if layer:
                    if s.peak:
                        sp.wait_ge(high_made, NCH * s.batch(2))
                    sp.dma_start(keep[:, :], m.keep_dram[s.batch(2)].partition_broadcast(P)).then_inc(keep_loaded, 16)
                k, batch = s.buf(2), s.batch(2)
                if s.mix:
                    sp.wait_ge(scored, 12 * s.batch(0))
                sp.dma_start(qstack[0:SPLIT, k, :, :],
                             m.q_dram[:, :, :, batch, :].rearrange("t r p c -> (t r) p c"))\
                    .then_inc(stack_loaded[k], 16)
                if layer:
                    sp.dma_start(kstack[SPLIT:FILLED, k, :, :],
                                 m.fill_dram[batch].unsqueeze(1).to_broadcast([3, PAIRS, CTX]))\
                        .then_inc(stack_loaded[k], 16)
                def save(n, made):
                    sp.wait_ge(made, NCH * (batch + 1))
                    sp.dma_start(m.k_dram[k, n].rearrange("r p n -> p r n"), part[:, n, :])\
                        .then_inc(part_saved[n], 16)

                def stack(n):
                    at, rows = PARTS_K.index(n) * PR, PARTS_K.count(n)
                    sp.wait_ge(part_saved[n], 16 * (batch + 1))
                    sp.dma_start(kstack[at:at + rows * PR, k, :, :],
                                 m.k_dram[k, n].unsqueeze(0).to_broadcast([rows, PR, PAIRS, CTX]))\
                        .then_inc(stack_loaded[k], 16)

                save(0, high_made)
                save(1, mid_made)
                stack(0)
                save(2, low_made)
                stack(1)
                stack(2)
                if layer == 0:
                    sp.wait_ge(stats_made, batch + 1)
                    sp.dma_start(m.stats_dram[:, batch, :], stats[:, :, :].rearrange("p c n -> p (c n)"))\
                        .then_inc(stats_saved, 16)

            run_steps(sp, nb, step)
            for k in range(3):
                sp.wait_ge(stack_loaded[k], 16 * loads * len(range(k, nb, 3)))
                sp.wait_ge(raw_loaded[k], 16 * raw_loads * len(range(k, nb + 1, 3)))
            if layer == 0:
                sp.wait_ge(stats_saved, 16 * nb)

        @block.scalar
        def _(act):
            act.wait_ge(ready, READY)
            act.sem_inc(exped, 2)

            def step(s):
                for kind, a, j, bank, before in s.slots():
                    if kind == "score":
                        rows, n = rows_of(a), 12 * s.batch(0) + a + 1
                        act.wait_ge(scored, n)
                        act.wait_ge(mixed, n)
                        nc.scalar.activation(probs[0:rows, a % 2, :, :], scores[a % 2][0:rows, :, 0:GC], ACT.Exp)\
                            .then_inc(exped, 1)
                    elif kind == "turn":
                        act.wait_ge(filled[bank], before + 1)
                        width = min(512, CTX - 512 * a)
                        nc.scalar.activation(rawT[:, 512 * a:512 * a + width], ring[bank][:, 0:width], ACT.Copy)\
                            .then_inc(drained[bank], 1)
                    elif kind == "key":
                        if layer == 0:
                            act.wait_ge(filled[bank], before + 1)
                            if s.peak:
                                act.wait_ge(rest_made, NCH * s.batch(1) + a + 1)
                            nc.scalar.activation(kf[:, CH * a:CH * (a + 1)], ring[bank][:, 0:CH], ACT.Identity,
                                                 bias=m.bk[0][:, 0:1]).then_inc(drained[bank], 1)
                        act.wait_ge(drained[bank], before + 1)
                        if s.peak:
                            act.wait_ge(part_saved[0], 16 * s.batch(2))
                            act.wait_ge(rest_made, NCH * s.batch(1) + a + 1)
                        nc.scalar.activation(part[:, 0, CH * a:CH * (a + 1)], kf[:, CH * a:CH * (a + 1)], ACT.Copy)\
                            .then_inc(high_made, 1)
                    elif kind == "value":
                        act.wait_ge(filled[bank], before + 1)
                        tiles = ring[bank][:, :].rearrange("p (c h e) -> p c h e", c=4, h=PAIRS)
                        k = s.buf(2)
                        if a < NCH - 1:
                            nc.scalar.activation(vals[:, k, 4 * a:4 * a + 4, :, 0:PR], tiles, ACT.Copy)\
                                .then_inc(drained[bank], 1)
                        else:
                            nc.scalar.activation(vals[:, k, 4 * a:4 * a + 3, :, 0:PR], tiles[:, 0:3], ACT.Copy)
                            nc.scalar.activation(vals[0:LAST, k, KT - 1, :, 0:PR], tiles[0:LAST, 3], ACT.Copy)\
                                .then_inc(drained[bank], 1)
                    elif kind == "mix" and a == KT - 1:
                        act.wait_ge(mixed, 12 * s.batch(1) + 2)
                        nc.scalar.activation(mixed_sb[:, :], mix_ps[:, 0:2 * PQ], ACT.Copy).then_inc(mix_read, 1)
                    elif kind == "project":
                        act.wait_ge(filled[bank], before + 1)
                        act.wait_ge(out_saved, 16 * s.batch(-1))
                        nc.scalar.activation(out_sb[:, :], ring[bank][0:S, 0:D], ACT.Copy)\
                            .then_inc(drained[bank], 1)
                        act.wait_ge(drained[bank], before + 1)
                        act.dma_start(m.y_dram[s.batch(-1)], out_sb[:, :]).then_inc(out_saved, 16)

            run_steps(act, nb, step)
            act.wait_ge(out_saved, 16 * nb)

        @block.vector
        def _(dve):
            nc.vector.memset(ones[SPLIT:STACK, :], 1.0).then_inc(ones_made, 1)
            nc.vector.memset(qstack[SPLIT:STACK, :, :, :], 1.0).then_inc(ready, 1)
            nc.vector.memset(vals[:, :, :, :, PR:VW], 1.0).then_inc(ready, 1)
            nc.vector.memset(shift[:, :, :], 1.0).then_inc(shift_set, 1)
            nc.vector.memset(mix_ps[:, :], 0.0).then_inc(ready, 1)
            nc.vector.memset(raw[:, :, KT - 1, :], 0.0).then_inc(ready, 1)
            if layer == 0:
                dve.wait_ge(shift_set, 1)
                nc.vector.memset(shift[:, :, 0:3], 0.0).then_inc(ready, 1)
            else:
                nc.vector.memset(low[:, :, :], 0.0).then_inc(ready, 1)
            dve.wait_ge(ready, READY)

            def mids(s, chunks):
                batch = s.batch(2)
                for a in chunks:
                    dve.wait_ge(rest_made, NCH * batch + a + 1)
                    if s.peak:
                        dve.wait_ge(part_saved[1], 16 * batch)
                        dve.wait_ge(low_made, NCH * s.batch(1) + a + 1)
                    nc.vector.tensor_copy(part[:, 1, CH * a:CH * (a + 1)], rest[:, CH * a:CH * (a + 1)])\
                        .then_inc(mid_made, 1)

            def step(s):
                for kind, a, j, bank, before in s.slots():
                    if kind == "peak":
                        dve.wait_ge(filled[bank], before + 1)
                        nc.vector.tensor_reduce(peaks[:, a, j:j + 1], ring[bank][0:PQ, 0:CH], AX.X, ALU.max)\
                            .then_inc(drained[bank], 1)
                        if (a, j) == (PAIRS - 1, NCH - 1):
                            n = SHIFTS * s.batch(1)
                            dve.wait_ge(drained[bank], before + 1)
                            nc.vector.tensor_reduce(low[:, 0, :], peaks[:, :, :], AX.X, ALU.max, negate=True)\
                                .then_inc(shift_steps, 1)
                            dve.wait_ge(shift_steps, n + 1)
                            nc.vector.tensor_copy(shift[:, :, 3], low[:, 0, :]).then_inc(shift_steps, 1)
                            dve.wait_ge(shift_steps, n + 2)
                            nc.vector.tensor_tensor(low[:, 1, :], low[:, 0, :], shift[:, :, 3], ALU.subtract)\
                                .then_inc(shift_steps, 1)
                            dve.wait_ge(shift_steps, n + 3)
                            nc.vector.tensor_copy(shift[:, :, 4], low[:, 1, :]).then_inc(shift_steps, 1)
                            dve.wait_ge(shift_steps, n + 4)
                            nc.vector.tensor_tensor(low[:, 2, :], low[:, 1, :], shift[:, :, 4], ALU.subtract)\
                                .then_inc(shift_steps, 1)
                            dve.wait_ge(shift_steps, n + 5)
                            nc.vector.tensor_copy(shift[:, :, 5], low[:, 2, :]).then_inc(shift_steps, 1)
                    elif kind == "shift":
                        dve.wait_ge(filled[bank], before + 1)
                        nc.vector.tensor_copy(qstack[SPLIT:STACK, s.buf(1), 4 * a:4 * a + 4, :],
                                              ring[bank][SPLIT:STACK, 0:GC].rearrange("r (p c) -> r p c", p=4))\
                            .then_inc(drained[bank], 1)
                    elif kind == "key" and layer:
                        dve.wait_ge(filled[bank], before + 1)
                        dve.wait_ge(keep_loaded, 16 * (s.batch(2) + 1))
                        if s.peak:
                            dve.wait_ge(rest_made, NCH * s.batch(1) + a + 1)
                        nc.vector.scalar_tensor_tensor(
                            out=kf[:, CH * a:CH * (a + 1)], in0=ring[bank][:, 0:CH], scalar=m.bk[1][:, 0:1],
                            in1=keep[:, CH * a:CH * (a + 1)], op0=ALU.add, op1=ALU.mult)\
                            .then_inc(drained[bank], 1)
                    elif kind == "mid":
                        mids(s, [a])
                    elif kind == "stat" and layer == 0:
                        if a == 0:
                            dve.wait_ge(raw_loaded[s.buf(2)], 32 * (s.use(2) + 1))
                            if s.peak:
                                dve.wait_ge(stats_saved, 16 * s.batch(2))
                        last = nc.vector.bn_stats(stats[:, a, :], raw[:, s.buf(2), a, :])
                        if a == KT - 1:
                            last.then_inc(stats_made, 1)
                    elif kind == "total":
                        dve.wait_ge(filled[bank], before + 1)
                        nc.vector.reciprocal(inverse[:, :], ring[bank][:, 0:2 * PQ]).then_inc(drained[bank], 1)
                        dve.wait_ge(drained[bank], before + 1)
                        nc.vector.tensor_tensor(heads[:, :, :, :].rearrange("p r x q -> p (r x q)"),
                                                mixed_sb[:, :], inverse[:, :], ALU.mult).then_inc(normalised, 1)

            run_steps(dve, nb, step)

        @block.gpsimd
        def _(pool):
            def normalise(k, batch, use):
                def per_key(n):
                    return norms[:, k, n, :].unsqueeze(2).to_broadcast([P, KT, D])

                pool.wait_ge(raw_loaded[k], 16 * raw_loads * (use + 1))
                nc.gpsimd.tensor_tensor(raw[:, k, :, :], raw[:, k, :, :], per_key(0), ALU.subtract)\
                    .then_inc(centred, 1)
                pool.wait_ge(centred, batch + 1)
                nc.gpsimd.tensor_tensor(raw[:, k, :, :], raw[:, k, :, :], per_key(1), ALU.mult)\
                    .then_inc(normed, 1)

            pool.wait_ge(ready, READY)
            if layer:
                normalise(0, 0, 0)

            def step(s):
                if not s.make:
                    return
                batch = s.batch(2)
                for a in range(NCH):
                    pool.wait_ge(high_made, NCH * batch + a + 1)
                    if s.peak:
                        pool.wait_ge(low_made, NCH * s.batch(1) + a + 1)
                    nc.gpsimd.tensor_tensor(rest[:, CH * a:CH * (a + 1)], kf[:, CH * a:CH * (a + 1)],
                                            part[:, 0, CH * a:CH * (a + 1)], ALU.subtract).then_inc(rest_made, 1)
                for a in range(NCH):
                    pool.wait_ge(mid_made, NCH * batch + a + 1)
                    if s.peak:
                        pool.wait_ge(part_saved[2], 16 * batch)
                    nc.gpsimd.tensor_tensor(part[:, 2, CH * a:CH * (a + 1)], rest[:, CH * a:CH * (a + 1)],
                                            part[:, 1, CH * a:CH * (a + 1)], ALU.subtract).then_inc(low_made, 1)
                if layer:
                    normalise(s.buf(3), s.batch(3), s.use(3))

            run_steps(pool, nb, step)

        @block.tensor
        def _(pe):
            pe.wait_ge(ready, READY)
            pe.sem_inc(mixed, 2)
            ident = mat(m, "ident")

            def step(s):
                shifts = []
                for kind, a, j, bank, before in s.slots():
                    if kind not in LOOSE:
                        pe.wait_ge(drained[bank], before)
                    if kind == "score":
                        rows, k = rows_of(a), s.buf(0)
                        pe.wait_ge(exped, 12 * s.batch(0) + a + 1)
                        for p in range(PAIRS):
                            last = nc.tensor.matmul(
                                scores[a % 2][0:rows, p // 4, (p % 4) * PQ:(p % 4 + 1) * PQ],
                                kstack[:, k, p, P * a:P * a + rows], qstack[:, k, p, :], start=True, stop=True)
                        last.then_inc(scored, 1)
                    elif kind == "mix":
                        rows, k = rows_of(a), s.buf(0)
                        pe.wait_ge(exped, 12 * s.batch(0) + a + 3)
                        if a == 0:
                            pe.wait_ge(mix_read, s.batch(0))
                        for p in range(PAIRS):
                            r, q = p // 4, p % 4
                            last = nc.tensor.matmul(
                                mix_ps[32 * q:32 * q + VW, r * PQ:(r + 1) * PQ], vals[0:rows, k, a, p, :],
                                probs[0:rows, a % 2, r, q * PQ:(q + 1) * PQ],
                                start=(a == 0 and r == 0), stop=(a == KT - 1), skip_group_check=True)
                        last.then_inc(mixed, 1)
                    elif kind == "peak":
                        k = s.buf(1)
                        if (a, j) == (0, 0):
                            pe.wait_ge(stack_loaded[k], 16 * loads * (s.use(1) + 1))
                        nc.tensor.matmul(ring[bank][0:PQ, 0:CH], qstack[0:rows_a, k, a, :],
                                         kstack[0:rows_a, k, a, CH * j:CH * (j + 1)], start=True, stop=True)\
                            .then_inc(filled[bank], 1)
                    elif kind == "shift":
                        pe.wait_ge(shift_steps, SHIFTS * (s.batch(1) + 1))
                        for p in range(4):
                            last = nc.tensor.matmul(ring[bank][SPLIT:STACK, p * PQ:(p + 1) * PQ],
                                                    shift[:, 4 * a + p, :], m.identb[0:PQ, 0:PQ],
                                                    start=True, stop=True)
                        last.then_inc(filled[bank], 1)
                        shifts.append((bank, before + 1))
                    elif kind == "turn":
                        k = s.buf(2)
                        if a == 0:
                            if layer:
                                pe.wait_ge(normed, s.batch(2) + 1)
                            else:
                                pe.wait_ge(raw_loaded[k], 32 * (s.use(2) + 1))
                        for c in range(4 * a, 4 * a + 4):
                            rows = rows_of(c)
                            last = nc.tensor.transpose(ring[bank][:, P * (c - 4 * a):P * (c - 4 * a) + rows],
                                                       raw[0:rows, k, c, :], ident[0:rows, 0:rows])
                        last.then_inc(filled[bank], 1)
                        turned = (bank, before + 1)
                    elif kind == "key":
                        if a == 0:
                            pe.wait_ge(drained[turned[0]], turned[1])
                        nc.tensor.matmul(ring[bank][:, 0:CH], m.wk[layer][:, :], rawT[:, CH * a:CH * (a + 1)],
                                         start=True, stop=True).then_inc(filled[bank], 1)
                    elif kind == "value":
                        for c in range(4 * a, 4 * a + 4):
                            rows = rows_of(c)
                            last = nc.tensor.matmul(ring[bank][0:rows, P * (c - 4 * a):P * (c - 4 * a + 1)],
                                                    rawT[:, P * c:P * c + rows], m.wv[layer][:, :],
                                                    start=True, stop=True)
                        last.then_inc(filled[bank], 1)
                    elif kind == "total":
                        pe.wait_ge(mix_read, s.batch(0))
                        nc.tensor.matmul(ring[bank][:, 0:2 * PQ], mat(m, "pick"), mixed_sb[:, :],
                                         start=True, stop=True).then_inc(filled[bank], 1)
                    elif kind == "project":
                        pe.wait_ge(normalised, s.batch(0))
                        for n in range(4):
                            last = nc.tensor.matmul(ring[bank][0:S, 0:D], heads[:, n // 2, n % 2, :],
                                                    mat(m, f"woh{layer}{'abcd'[n]}"), start=(n == 0), stop=(n == 3))
                        last.then_inc(filled[bank], 1)
                for bank, n in shifts:
                    pe.wait_ge(drained[bank], n)

            run_steps(pe, nb, step)


def ffn_ternary(nc, m):
    nt = m.nt
    gt = min(GT, nt)
    ng = nt // gt
    gc = gt * TOK
    cols = nt * TOK
    with ExitStack() as ctx:
        def sb(name, shape, dt):
            return ctx.enter_context(nc.sbuf_tensor("t_" + name, shape, dt))

        def sem(name):
            return ctx.enter_context(nc.semaphore("t_" + name))

        y = sb("y", [TOK, nt, D], F32)
        z = sb("z", [TOK, nt, D], F32)
        sq = sb("sq", [TOK, nt, D], F32)
        st = sb("st", [TOK, 12, nt], F32)
        qz = sb("qz", [TOK, nt, D], BF16)
        qzT = sb("qzT", [P, cols], BF16)
        w1 = sb("w1", [P, F0], BF16)
        w2 = sb("w2", [P, F0], BF16)
        wr = sb("wr", [P, F0], F32)
        wst = sb("wst", [P, 8], F32)
        ones = sb("ones", [P, P], F32)
        h = sb("h", [TOK, nt, F0], F32)
        hq = sb("hq", [TOK, 2, F0], F32)
        hb = sb("hb", [TOK, 2, F0], BF16)
        hT = sb("hT", [P, 2, FT, TOK], BF16)
        junk = sb("junk", [TOK, F0], F32)
        sums = ctx.enter_context(nc.psum_tensor("t_sums", [P, 512], F32))
        turned = [ctx.enter_context(nc.psum_tensor(f"t_turned{i}", [P, 1024], BF16)) for i in range(2)]
        hps = [ctx.enter_context(nc.psum_tensor(f"t_hps{i}", [TOK, F0], F32)) for i in range(2)]
        ops = [ctx.enter_context(nc.psum_tensor(f"t_ops{i}", [TOK, 512], F32)) for i in range(2)]
        y_loaded, chain_sem, roots = sem("y_loaded"), sem("chain"), sem("roots")
        wsum, wready, zturned, zcopied = sem("wsum"), sem("wready"), sem("zturned"), sem("zcopied")
        hid, hid_read, gelus, squares = sem("hid"), sem("hid_read"), sem("gelus"), sem("squares")
        quant, hturned, hcopied, outs, outs_read = sem("quant"), sem("hturned"), sem("hcopied"), sem("outs"), sem("outs_read")
        tok_quant = sem("tok_quant")
        block = ctx.enter_context(nc.Block())
        A = mybir.AxisListType.X

        @block.sync
        def _(sp):
            sp.dma_start(y[:, :, :], m.y_dram.rearrange("b s d -> (b s) d").rearrange("(n p) d -> p n d", p=TOK))\
                .then_inc(y_loaded, 16)

        @block.vector
        def _(dve):
            def out_tile(i):
                dve.wait_ge(outs, i + 1)
                nc.vector.scalar_tensor_tensor(out=y[:, i, :], in0=ops[i % 2][:, 0:D], scalar=st[:, 7, i:i + 1],
                                               in1=row(m, "b2", TOK), op0=ALU.mult, op1=ALU.add).then_inc(outs_read, 1)

            chain = Chain(dve, chain_sem)
            nc.vector.memset(ones[:, :], 1.0).then_inc(wready, 1)
            for n, (a, b) in enumerate((("fa", "fd"), ("ga", "gd"))):
                at = MATS.index(a) * P
                nc.vector.tensor_reduce(wst[:, n:n + 1], m.mats[:, at:at + F0], AX.X, ALU.add,
                                        apply_absolute_value=True).then_inc(wready, 1)
            dve.wait_ge(wsum, 1)
            chain.then(nc.vector.tensor_scalar(wst[:, 2:4], sums[:, 0:2], 1.0 / (D * F0), 1e-5, ALU.mult, ALU.max))
            chain.then(nc.vector.reciprocal(wst[:, 4:6], wst[:, 2:4]))
            for n, (w, a) in enumerate(((w1, "fa"), (w2, "ga"))):
                at = MATS.index(a) * P
                chain.then(nc.vector.tensor_scalar(wr[:, :], m.mats[:, at:at + F0], wst[:, 4 + n:5 + n], 1.0,
                                                   ALU.mult, ALU.min))
                chain.then(nc.vector.tensor_scalar(wr[:, :], wr[:, :], -1.0, MAGIC, ALU.max, ALU.add))
                chain.then(nc.vector.tensor_scalar(w[:, :], wr[:, :], MAGIC, None, ALU.subtract))
            dve.wait_ge(y_loaded, 16)
            chain.then(nc.vector.tensor_tensor(y[:, :, :], y[:, :, :], per_channel(m.yb[0][:, :], nt), ALU.add))
            chain.then(nc.vector.scalar_tensor_tensor(out=m.x[:, :, :], in0=y[:, :, :], scalar=m.gates[0:TOK, 0:1],
                                                      in1=m.x[:, :, :], op0=ALU.mult, op1=ALU.add))
            norm_vector(nc, dve, chain, roots, m.x[:, :, :], z[:, :, :], sq[:, :, :], st, nt, 1)
            chain.then(nc.vector.tensor_tensor(sq[:, :, :], z[:, :, :], z[:, :, :], ALU.mult))
            chain.then(nc.vector.tensor_reduce(st[:, 2, :], sq[:, :, :], AX.X, ALU.add))
            dve.wait_ge(roots, 2)
            chain.then(nc.vector.reciprocal(st[:, 4, :], st[:, 3, :]))
            chain.then(nc.vector.tensor_tensor(z[:, :, :], z[:, :, :], per_token(st[:, 4, :], nt), ALU.mult))
            chain.then(nc.vector.tensor_reduce(st[:, 5, :], z[:, :, :], AX.X, ALU.max, apply_absolute_value=True))
            chain.then(nc.vector.tensor_scalar(st[:, 5, :], st[:, 5, :], 1e-5, 1.0 / 127.0, ALU.max, ALU.mult))
            chain.then(nc.vector.reciprocal(st[:, 6, :], st[:, 5, :]))
            chain.then(nc.vector.tensor_tensor(z[:, :, :], z[:, :, :], per_token(st[:, 6, :], nt), ALU.mult))
            chain.then(nc.vector.tensor_scalar(z[:, :, :], z[:, :, :], 127.0, -128.0, ALU.min, ALU.max))
            chain.then(nc.vector.tensor_scalar(z[:, :, :], z[:, :, :], MAGIC, MAGIC, ALU.add, ALU.subtract))
            nc.vector.tensor_copy(qz[:, :, :], z[:, :, :]).then_inc(tok_quant, 1)
            chain.then(nc.vector.tensor_scalar(st[:, 7, :], st[:, 5, :], wst[0:TOK, 2:3], None, ALU.mult))
            for g in range(ng):
                dve.wait_ge(zturned, g + 1)
                nc.vector.tensor_copy(qzT[:, g * gc:(g + 1) * gc], turned[g % 2][:, 0:gc]).then_inc(zcopied, 1)
            for i in range(nt):
                dve.wait_ge(hid, i + 1)
                nc.vector.scalar_tensor_tensor(out=h[:, i, :], in0=hps[i % 2][:, :], scalar=st[:, 7, i:i + 1],
                                               in1=row(m, "b1", TOK), op0=ALU.mult, op1=ALU.add).then_inc(hid_read, 1)
            for i in range(nt):
                dve.wait_ge(gelus, i + 1)
                last = nc.vector.tensor_reduce(st[:, 8, i:i + 1], h[:, i, :], AX.X, ALU.max,
                                               apply_absolute_value=True)
            chain.then(last)
            dve.wait_ge(roots, 3)
            chain.then(nc.vector.reciprocal(st[:, 4, :], st[:, 3, :]))
            chain.then(nc.vector.tensor_tensor(st[:, 8, :], st[:, 8, :], st[:, 4, :], ALU.mult))
            chain.then(nc.vector.tensor_scalar(st[:, 5, :], st[:, 8, :], 1e-5, 1.0 / 127.0, ALU.max, ALU.mult))
            chain.then(nc.vector.reciprocal(st[:, 6, :], st[:, 5, :]))
            chain.then(nc.vector.tensor_tensor(st[:, 6, :], st[:, 6, :], st[:, 4, :], ALU.mult))
            chain.then(nc.vector.tensor_scalar(st[:, 7, :], st[:, 5, :], wst[0:TOK, 3:4], None, ALU.mult))
            for i in range(nt):
                u = i % 2
                chain.then(nc.vector.tensor_scalar(hq[:, u, :], h[:, i, :], st[:, 6, i:i + 1], 127.0, ALU.mult, ALU.min))
                chain.then(nc.vector.tensor_scalar(hq[:, u, :], hq[:, u, :], -128.0, MAGIC, ALU.max, ALU.add))
                if i >= 2:
                    dve.wait_ge(hturned, i - 1)
                nc.vector.tensor_scalar(hb[:, u, :], hq[:, u, :], MAGIC, None, ALU.subtract).then_inc(quant, 1)
                if i:
                    out_tile(i - 1)
            out_tile(nt - 1)
            dve.wait_ge(outs_read, nt)
            chain.then(nc.vector.scalar_tensor_tensor(out=m.x[:, :, :], in0=y[:, :, :], scalar=m.gates[0:TOK, 2:3],
                                                      in1=m.x[:, :, :], op0=ALU.mult, op1=ALU.add))

        links_before = 2 + 6 + 2

        @block.scalar
        def _(act):
            norm_scalar(nc, act, m, chain_sem, links_before + NORM_SUM, roots, st)
            norm_scalar(nc, act, m, chain_sem, links_before + NORM_LINKS + 2, roots, st)
            for i in range(nt):
                act.wait_ge(hid_read, i + 1)
                nc.scalar.activation(h[:, i, :], h[:, i, :], ACT.Gelu).then_inc(gelus, 1)
            act.wait_ge(gelus, nt)
            for i in range(nt):
                nc.scalar.activation(junk[:, :], h[:, i, :], ACT.Square, accum_out=st[:, 9, i:i + 1])\
                    .then_inc(squares, 1)
                act.wait_ge(squares, i + 1)
            nc.scalar.activation(st[:, 3, :], st[:, 9, :], ACT.Sqrt, bias=m.eps[0:TOK, 0:1], scale=1.0 / F0)\
                .then_inc(roots, 1)
            for i in range(nt):
                act.wait_ge(hturned, i + 1)
                if i >= 2:
                    act.wait_ge(outs, i - 1)
                nc.scalar.activation(hT[:, i % 2, :, :].rearrange("p f t -> p (f t)"), turned[i % 2][:, 0:FT * TOK],
                                     ACT.Copy).then_inc(hcopied, 1)

        @block.tensor
        def _(pe):
            def second(i):
                pe.wait_ge(hcopied, i + 1)
                if i >= 2:
                    pe.wait_ge(outs_read, i - 1)
                for f in range(FT):
                    last = nc.tensor.matmul(ops[i % 2][:, 0:D], hT[:, i % 2, f, :], w2[:, f * P:(f + 1) * P],
                                            start=(f == 0), stop=(f == FT - 1))
                last.then_inc(outs, 1)

            pe.wait_ge(wready, 3)
            nc.tensor.matmul(sums[:, 0:2], ones[:, :], wst[:, 0:2], start=True, stop=True).then_inc(wsum, 1)
            pe.wait_ge(tok_quant, 1)
            for g in range(ng):
                if g >= 2:
                    pe.wait_ge(zcopied, g - 1)
                for i in range(gt):
                    last = nc.tensor.transpose(turned[g % 2][:, i * TOK:(i + 1) * TOK], qz[:, g * gt + i, :],
                                               m.identb[0:TOK, 0:TOK])
                last.then_inc(zturned, 1)
            pe.wait_ge(chain_sem, 8)
            for i in range(nt):
                pe.wait_ge(zcopied, i // gt + 1)
                if i >= 2:
                    pe.wait_ge(hid_read, i - 1)
                nc.tensor.matmul(hps[i % 2][:, :], qzT[:, i * TOK:(i + 1) * TOK], w1[:, :], start=True, stop=True)\
                    .then_inc(hid, 1)
            for i in range(nt):
                pe.wait_ge(quant, i + 1)
                pe.wait_ge(zcopied, ng)
                if i >= 2:
                    pe.wait_ge(hcopied, i - 1)
                for f in range(FT):
                    last = nc.tensor.transpose(turned[i % 2][:, f * TOK:(f + 1) * TOK], hb[:, i % 2, f * P:(f + 1) * P],
                                               m.identb[0:TOK, 0:TOK])
                last.then_inc(hturned, 1)
                if i:
                    second(i - 1)
            second(nt - 1)


def ffn_experts(nc, m):
    nt = m.nt
    gt = min(GT, nt)
    ng = nt // gt
    gc = gt * TOK
    cols = nt * TOK
    PER = FT * ng
    HB = 4
    AHEAD = 2
    with ExitStack() as ctx:
        def sb(name, shape, dt):
            return ctx.enter_context(nc.sbuf_tensor("e_" + name, shape, dt))

        def sem(name):
            return ctx.enter_context(nc.semaphore("e_" + name))

        y = sb("y", [TOK, nt, D], F32)
        n1 = sb("n1", [TOK, nt, D], F32)
        sq = sb("sq", [TOK, nt, D], F32)
        st = sb("st", [TOK, 5, nt], F32)
        x1 = sb("x1", [TOK, nt, D], F32)
        nT = sb("nT", [P, cols], F32)
        pr = sb("pr", [TOK, 6, nt, E], F32)
        top = sb("top", [TOK, 3, nt], F32)
        order = sb("order", [TOK, E], F32)
        shifts = sb("shifts", [TOK, D], F32)
        ind = sb("ind", [E, cols], F32)
        w1 = sb("w1", [P, 2, F0], F32)
        w2 = sb("w2", [P, 2, F0], F32)
        b1 = sb("b1", [P, 2, FT], F32)
        comb = sb("comb", [P, 2, cols], F32)
        hid = sb("hid", [P, HB, GC], F32)
        hw = sb("hw", [P, HB, GC], F32)
        oT = sb("oT", [P, cols], F32)
        acc = [ctx.enter_context(nc.psum_tensor(f"e_acc{g}", [P, 512], F32)) for g in range(ng)]
        ps = [ctx.enter_context(nc.psum_tensor(f"e_ps{i}", [P, 512], F32)) for i in range(HB)]
        pl = ps[HB - 1]
        y_loaded, chain_sem, roots = sem("y_loaded"), sem("chain"), sem("roots")
        turned, copied, mixed, mixed_read = sem("turned"), sem("copied"), sem("mixed"), sem("mixed_read")
        n2_done, routed, chosen, comb_saved, comb_turned = sem("n2_done"), sem("routed"), sem("chosen"), sem("comb_saved"), sem("comb_turned")
        comb_copied, acc_set = sem("comb_copied"), sem("acc_set")
        loaded = [sem("loaded0"), sem("loaded1")]
        hidden, silus, weighted, added = sem("hidden"), sem("silus"), sem("weighted"), sem("added")
        acc_read, back, outed, out_saved = sem("acc_read"), sem("back"), sem("outed"), sem("out_saved")
        ex, chosen_ex = sem("ex"), sem("chosen_ex")
        block = ctx.enter_context(nc.Block())

        @block.sync
        def _(sp):
            sp.dma_start(y[:, :, :], m.y_dram.rearrange("b s d -> (b s) d").rearrange("(n p) d -> p n d", p=TOK))\
                .then_inc(y_loaded, 16)
            def weights(e, u):
                sp.dma_start(w1[:, u, :], m.w1_dram[e]).then_inc(loaded[u], 16)
                sp.dma_start(w2[:, u, :], m.w2_dram[e]).then_inc(loaded[u], 16)
                sp.dma_start(b1[:, u, :], m.b1_dram[e]).then_inc(loaded[u], 16)

            def shares(e, u):
                sp.dma_start(comb[:, u, :], m.comb_dram[e].partition_broadcast(P)).then_inc(loaded[u], 16)

            weights(0, 0)
            weights(1, 1)
            sp.wait_ge(comb_copied, ng)
            sp.dma_start(m.comb_dram, ind[:, :]).then_inc(comb_saved, 16)
            sp.wait_ge(comb_saved, 16)
            shares(0, 0)
            shares(1, 1)
            with sp.Fori(1, E // 2) as lap:
                for u in range(2):
                    sp.wait_ge(added, 2 * PER * lap + PER * u)
                    weights(2 * lap + u, u)
                    shares(2 * lap + u, u)
            sp.wait_ge(outed, ng + 1)
            sp.dma_start(m.out_dram.rearrange("b s d -> (b s) d").rearrange("(n p) d -> p n d", p=TOK), m.x[:, :, :])\
                .then_inc(out_saved, 16)
            sp.wait_ge(out_saved, 16)

        @block.vector
        def _(dve):
            chain = Chain(dve, chain_sem)
            for e in range(E):
                last = nc.vector.memset(order[:, e:e + 1], float(E - e))
            dve.wait_ge(y_loaded, 16)
            chain.then(nc.vector.tensor_tensor(y[:, :, :], y[:, :, :], per_channel(m.yb[1][:, :], nt), ALU.add))
            chain.then(nc.vector.scalar_tensor_tensor(out=m.x[:, :, :], in0=y[:, :, :], scalar=m.gates[0:TOK, 1:2],
                                                      in1=m.x[:, :, :], op0=ALU.mult, op1=ALU.add))
            norm_vector(nc, dve, chain, roots, m.x[:, :, :], x1[:, :, :], sq[:, :, :], st, nt, 1)
            norm_vector(nc, dve, chain, roots, x1[:, :, :], n1[:, :, :], sq[:, :, :], st, nt, 2)
            chain.mark(nc.vector.tensor_tensor(sq[:, :, :], n1[:, :, :], per_channel(row(m, "g1", TOK), nt), ALU.mult))
            chain.then(nc.vector.tensor_tensor(shifts[:, :], row(m, "be1", TOK), row(m, "mix_b", TOK), ALU.add))
            chain.then(nc.vector.tensor_tensor(x1[:, :, :], x1[:, :, :], sq[:, :, :], ALU.add))
            chain.then(nc.vector.tensor_tensor(x1[:, :, :], x1[:, :, :], per_channel(shifts[:, :], nt), ALU.add))
            for g in range(ng):
                dve.wait_ge(mixed, g + 1)
                nc.vector.tensor_tensor(x1[:, g * gt:(g + 1) * gt, :], x1[:, g * gt:(g + 1) * gt, :],
                                        acc[g][0:TOK, 0:gt * D].rearrange("p (i d) -> p i d", i=gt), ALU.add)\
                    .then_inc(mixed_read, 1)
            dve.wait_ge(mixed_read, ng)
            norm_vector(nc, dve, chain, roots, x1[:, :, :], n1[:, :, :], sq[:, :, :], st, nt, 3)
            dve.wait_ge(routed, 1)
            logits = pl[0:TOK, 0:nt * E].rearrange("p (i e) -> p i e", e=E)

            def spread(ap):
                return per_token(ap, nt, E)

            chain.then(nc.vector.tensor_reduce(top[:, 0, :], logits, AX.X, ALU.max))
            nc.vector.tensor_tensor(pr[:, 0, :, :], logits, spread(top[:, 0, :]), ALU.subtract).then_inc(ex, 1)
            dve.wait_ge(ex, 2)
            chain.then(nc.vector.tensor_reduce(top[:, 1, :], pr[:, 1, :, :], AX.X, ALU.add))
            chain.then(nc.vector.reciprocal(top[:, 2, :], top[:, 1, :]))
            chain.then(nc.vector.tensor_tensor(pr[:, 0, :, :], pr[:, 1, :, :], spread(top[:, 2, :]), ALU.mult))
            chain.then(nc.vector.tensor_copy(pr[:, 5, :, :], pr[:, 0, :, :]))
            for n in (3, 4):
                chain.then(nc.vector.tensor_reduce(top[:, 0, :], pr[:, 5, :, :], AX.X, ALU.max))
                chain.then(nc.vector.tensor_tensor(pr[:, 2, :, :], pr[:, 5, :, :], spread(top[:, 0, :]), ALU.is_equal))
                chain.then(nc.vector.tensor_tensor(pr[:, 2, :, :], pr[:, 2, :, :],
                                                   order[:, :].unsqueeze(1).to_broadcast([TOK, nt, E]), ALU.mult))
                chain.then(nc.vector.tensor_reduce(top[:, 1, :], pr[:, 2, :, :], AX.X, ALU.max))
                chain.then(nc.vector.tensor_tensor(pr[:, n, :, :], pr[:, 2, :, :], spread(top[:, 1, :]), ALU.is_equal))
                if n == 3:
                    chain.then(nc.vector.scalar_tensor_tensor(
                        out=pr[:, 5, :, :], in0=pr[:, 3, :, :], scalar=-2.0, in1=pr[:, 5, :, :],
                        op0=ALU.mult, op1=ALU.add))
            chain.then(nc.vector.tensor_tensor(pr[:, 3, :, :], pr[:, 3, :, :], pr[:, 4, :, :], ALU.add))
            nc.vector.tensor_tensor(pr[:, 2, :, :], pr[:, 3, :, :], pr[:, 0, :, :], ALU.mult).then_inc(chosen, 1)
            dve.sem_inc(weighted, HB)
            with dve.Fori(0, E // 2) as lap:
                for u in range(2):
                    dve.wait_ge(loaded[u], 64 * lap + 64)
                    for f in range(FT):
                        for g in range(ng):
                            n = PER * u + f * ng + g
                            at = 2 * PER * lap + n
                            dve.wait_ge(silus, at + 1 + HB)
                            dve.wait_ge(added, at + 1 - HB + PER)
                            nc.vector.tensor_tensor(hw[:, n % HB, 0:gc], hid[:, n % HB, 0:gc],
                                                    comb[:, u, g * gc:(g + 1) * gc], ALU.mult).then_inc(weighted, 1)
            for g in range(ng):
                dve.wait_ge(back, g + 1)
                nc.vector.tensor_tensor(x1[:, g * gt:(g + 1) * gt, :], x1[:, g * gt:(g + 1) * gt, :],
                                        ps[g % 2][0:TOK, 0:gt * D].rearrange("p (i d) -> p i d", i=gt), ALU.add)\
                    .then_inc(outed, 1)
            dve.wait_ge(outed, ng)
            nc.vector.scalar_tensor_tensor(out=m.x[:, :, :], in0=x1[:, :, :], scalar=m.gates[0:TOK, 3:4],
                                           in1=m.x[:, :, :], op0=ALU.mult, op1=ALU.add).then_inc(outed, 1)

        first_norm = 2
        second_norm = first_norm + 2 * NORM_LINKS + 4

        @block.scalar
        def _(act):
            norm_scalar(nc, act, m, chain_sem, first_norm + NORM_SUM, roots, st)
            norm_scalar(nc, act, m, chain_sem, first_norm + NORM_LINKS + NORM_SUM, roots, st)
            for g in range(ng):
                act.wait_ge(turned, g + 1)
                nc.scalar.activation(nT[:, g * gc:(g + 1) * gc], ps[g % 2][:, 0:gc], ACT.Identity,
                                     bias=col(m, "be1"), scale=col(m, "g1")).then_inc(copied, 1)
            norm_scalar(nc, act, m, chain_sem, second_norm + NORM_SUM, roots, st)
            for g in range(ng):
                act.wait_ge(turned, ng + g + 1)
                nc.scalar.activation(nT[:, g * gc:(g + 1) * gc], ps[g % 2][:, 0:gc], ACT.Identity,
                                     bias=col(m, "be2"), scale=col(m, "g2")).then_inc(copied, 1)
            act.wait_ge(ex, 1)
            nc.scalar.activation(pr[:, 1, :, :], pr[:, 0, :, :], ACT.Exp).then_inc(ex, 1)
            for g in range(ng):
                act.wait_ge(comb_turned, g + 1)
                nc.scalar.activation(ind[:, g * gc:(g + 1) * gc], ps[g % 2][0:E, 0:gc], ACT.Copy).then_inc(comb_copied, 1)
            act.sem_inc(silus, HB)
            with act.Fori(0, E // 2) as lap:
                for u in range(2):
                    act.wait_ge(loaded[u], 64 * lap + 64)
                    for f in range(FT):
                        for g in range(ng):
                            n = PER * u + f * ng + g
                            at = 2 * PER * lap + n
                            act.wait_ge(hidden, at + 1)
                            act.wait_ge(weighted, at + 1)
                            nc.scalar.activation(hid[:, n % HB, 0:gc], ps[n % HB][:, 0:gc], ACT.Silu,
                                                 bias=b1[:, u, f:f + 1]).then_inc(silus, 1)
            act.wait_ge(added, PER + E * PER)
            for g in range(ng):
                nc.scalar.activation(oT[:, g * gc:(g + 1) * gc], acc[g][:, 0:gc], ACT.Copy).then_inc(acc_read, 1)

        @block.tensor
        def _(pe):
            ident = mat(m, "ident")

            def turn(base):
                for g in range(ng):
                    if g >= 2:
                        pe.wait_ge(copied, base + g - 1)
                    for i in range(gt):
                        last = nc.tensor.transpose(ps[g % 2][:, i * TOK:(i + 1) * TOK], n1[:, g * gt + i, :],
                                                   ident[0:TOK, 0:TOK])
                    last.then_inc(turned, 1)

            pe.wait_ge(chain_sem, first_norm + 2 * NORM_LINKS)
            turn(0)
            for g in range(ng):
                pe.wait_ge(copied, g + 1)
                for i in range(gt):
                    at = (g * gt + i) * TOK
                    last = nc.tensor.matmul(acc[g][0:TOK, i * D:(i + 1) * D], nT[:, at:at + TOK], mat(m, "mix"),
                                            start=True, stop=True)
                last.then_inc(mixed, 1)
            pe.wait_ge(chain_sem, second_norm + NORM_LINKS)
            pe.wait_ge(copied, ng)
            turn(ng)
            pe.wait_ge(copied, 2 * ng)
            for i in range(nt):
                last = nc.tensor.matmul(pl[0:TOK, i * E:(i + 1) * E], nT[:, i * TOK:(i + 1) * TOK], m.router[:, :],
                                        start=True, stop=True)
            last.then_inc(routed, 1)
            pe.wait_ge(chosen, 1)
            for g in range(ng):
                if g >= 2:
                    pe.wait_ge(comb_copied, g - 1)
                for i in range(gt):
                    last = nc.tensor.transpose(ps[g % 2][0:E, i * TOK:(i + 1) * TOK], pr[:, 2, g * gt + i, :],
                                               ident[0:TOK, 0:TOK])
                last.then_inc(comb_turned, 1)
            pe.wait_ge(comb_copied, ng)
            pe.wait_ge(mixed_read, ng)
            for g in range(ng):
                nc.tensor.matmul(acc[g][:, 0:gc], m.b2e[:, :], ind[:, g * gc:(g + 1) * gc], start=True, stop=False,
                                 skip_group_check=True)

            pe.sem_inc(added, PER)

            def first(lap, n):
                u, f, g = n // PER, (n // ng) % FT, n % ng
                if n == PER * u:
                    pe.wait_ge(loaded[u], 64 * lap + 64)
                pe.wait_ge(silus, 2 * PER * lap + n + 1)
                nc.tensor.matmul(ps[n % HB][:, 0:gc], w1[:, u, f * P:(f + 1) * P], nT[:, g * gc:(g + 1) * gc],
                                 start=True, stop=True).then_inc(hidden, 1)

            def second(lap, n):
                u, f, g = n // PER, (n // ng) % FT, n % ng
                pe.wait_ge(weighted, 2 * PER * lap + n + 1 + HB)
                nc.tensor.matmul(acc[g][:, 0:gc], w2[:, u, f * P:(f + 1) * P], hw[:, n % HB, 0:gc],
                                 start=False, stop=True, skip_group_check=True).then_inc(added, 1)

            def two_experts(lap, more):
                for n in range(2 * PER):
                    if n + AHEAD < 2 * PER:
                        first(lap, n + AHEAD)
                    elif more:
                        first(lap + 1, n + AHEAD - 2 * PER)
                    second(lap, n)

            for n in range(AHEAD):
                first(0, n)
            with pe.Fori(0, E // 2 - 1) as lap:
                two_experts(lap, True)
            two_experts(E // 2 - 1, False)
            for g in range(ng):
                pe.wait_ge(acc_read, g + 1)
                if g >= 2:
                    pe.wait_ge(outed, g - 1)
                for i in range(gt):
                    at = (g * gt + i) * TOK
                    last = nc.tensor.transpose(ps[g % 2][0:TOK, i * D:(i + 1) * D], oT[:, at:at + TOK], ident)
                last.then_inc(back, 1)


def program(nc, nb, x_dram, ctx_dram, mask_dram, mats_dram, cols_dram, rows_dram, router_dram, b2e_dram,
            w1_dram, w2_dram, b1_dram, out_dram):
    nt = nb // 2
    with ExitStack() as ctx:
        def sb(name, shape, dt):
            return ctx.enter_context(nc.sbuf_tensor(name, shape, dt))

        def dram(name, shape, dt):
            return nc.dram_tensor(name, shape, dt, kind="Internal").ap()

        m = Shared()
        m.nb = nb
        m.nt = nt
        m.x_dram = x_dram
        m.ctx_dram = ctx_dram
        m.mask_dram = mask_dram
        m.mats_dram = mats_dram
        m.cols_dram = cols_dram
        m.rows_dram = rows_dram
        m.router_dram = router_dram
        m.b2e_dram = b2e_dram
        m.w1_dram = w1_dram
        m.w2_dram = w2_dram
        m.b1_dram = b1_dram
        m.out_dram = out_dram
        m.stats_dram = dram("stats_scratch", [P, nb, KT * 6], F32)
        m.norms_dram = dram("norms_scratch", [P, nb, 2 * KT], F32)
        m.keep_dram = dram("keep_scratch", [nb, CTX], BF16)
        m.fill_dram = dram("fill_scratch", [nb, 3, CTX], BF16)
        m.q_dram = dram("q_scratch", [TERMS, PR, PAIRS, nb, PQ], BF16)
        m.k_dram = dram("k_scratch", [3, 3, PR, PAIRS, CTX], BF16)
        m.y_dram = dram("y_scratch", [nb, S, D], F32)
        m.comb_dram = dram("comb_scratch", [E, nb * S], F32)
        m.x = sb("x", [TOK, nt, D], F32)
        m.mats = sb("mats", [P, len(MATS) * P], F32)
        m.cols = sb("cols", [P, len(COLS)], F32)
        m.rows = sb("rows", [P, ROW_W], F32)
        m.router = sb("router", [P, E], F32)
        m.b2e = sb("b2e", [E, D], F32)
        m.identb = sb("identb", [P, P], BF16)
        m.gates = sb("gates", [P, 4], F32)
        m.eps = sb("eps", [P, 1], F32)
        m.wk = [sb("wk_0", [P, P], F32), sb("wk_1", [P, P], F32)]
        m.wv = [sb("wv_0", [P, P], F32), sb("wv_1", [P, P], F32)]
        m.bk = [sb("bk_0", [P, 1], F32), sb("bk_1", [P, 1], F32)]
        m.yb = [sb("yb_0", [TOK, D], F32), sb("yb_1", [TOK, D], F32)]
        setup(nc, m)
        queries(nc, m, 0)
        attention(nc, m, 0)
        ffn_ternary(nc, m)
        key_norms(nc, m)
        queries(nc, m, 1)
        attention(nc, m, 1)
        ffn_experts(nc, m)


def layouts(inputs):
    import numpy as np

    a = {k: np.asarray(v) for k, v in inputs.items()}
    f = np.float32
    mats = {
        "wq0": a["L0_xattn_Wq"].T, "wk0": a["L0_xattn_Wk"].T, "wv0": a["L0_xattn_Wv"].T, "wo0": a["L0_xattn_Wo"].T,
        "wq1": a["L1_xattn_w_q"], "wk1": a["L1_xattn_w_kv"][:, :D], "wv1": a["L1_xattn_w_kv"][:, D:],
        "wo1": a["L1_xattn_w_proj"], "mix": a["L1_ffn_mix_w"], "ident": np.eye(P, dtype=f),
    }
    pick = np.zeros((P, P), f)
    for i in range(P):
        pick[i // 32 * 32 + PR, i] = 1.0
    mats["pick"] = pick
    for layer in range(2):
        wo = mats[f"wo{layer}"]
        for n in range(4):
            r, odd = n // 2, n % 2
            w = np.zeros((P, P), f)
            for q in range(4):
                h = 2 * (4 * r + q) + odd
                w[32 * q + HD * odd:32 * q + HD * odd + HD] = wo[h * HD:(h + 1) * HD]
            mats[f"woh{layer}{'abcd'[n]}"] = w
    w1 = a["L0_ffn_w1"].T
    w2 = a["L0_ffn_w2"].T
    for n in range(4):
        mats["f" + "abcd"[n]] = w1[:, n * P:(n + 1) * P]
        mats["g" + "abcd"[n]] = w2[n * P:(n + 1) * P, :]
    parity = (np.arange(P) // HD) % 2
    cols = {
        "g1": a["L1_ffn_g1"], "be1": a["L1_ffn_be1"], "bq0": a["L0_xattn_bq"], "bk0": a["L0_xattn_bk"], "bv0": a["L0_xattn_bv"], "g_x": a["L1_xattn_g_x"],
        "b_x": a["L1_xattn_b_x"], "g_kv": a["L1_xattn_g_kv"], "b_kv": a["L1_xattn_b_kv"], "g2": a["L1_ffn_g2"],
        "be2": a["L1_ffn_be2"], "even": (1 - parity).astype(f), "odd": parity.astype(f),
    }
    rows = {
        "bo0": a["L0_xattn_bo"], "b2": a["L0_ffn_b2"], "b1": a["L0_ffn_b1"], "bo1": a["L1_xattn_b_proj"],
        "g1": a["L1_ffn_g1"], "be1": a["L1_ffn_be1"], "mix_b": a["L1_ffn_mix_b"],
        "gates": np.concatenate([a["g_xattn"], a["g_ffn"]]),
    }
    out = {
        "x": a["x"], "ctx": a["ctx_1024"], "mask": a["mask_BxS2_ik0"],
        "mats": np.concatenate([mats[k] for k in MATS], axis=1),
        "cols": np.stack([cols[k] for k in COLS], axis=1),
        "rows": np.concatenate([rows[k] for k, _ in ROWS]),
        "router": a["L1_ffn_router_w"], "b2e": a["L1_ffn_b2"],
        "w1": a["L1_ffn_w1"],
        "w2": a["L1_ffn_w2"].reshape(E, FT, P, D).transpose(0, 2, 1, 3).reshape(E, P, FT * D),
        "b1": a["L1_ffn_b1"].reshape(E, FT, P).transpose(0, 2, 1),
    }
    return {k: np.ascontiguousarray(v) for k, v in out.items()}


def kernel(**inputs):
    import concourse.bacc as bacc
    from concourse.bass_utils import run_bass_kernel_spmd

    arrays = layouts(inputs)
    nb = arrays["x"].shape[0]
    nc = bacc.Bacc("TRN2", target_bir_lowering=False, num_devices=1)
    args = {f"{k}_dram": nc.dram_tensor(f"in_{k}", v.shape, mybir.dt.from_np(v.dtype), kind="ExternalInput").ap()
            for k, v in arrays.items()}
    out = nc.dram_tensor("out_x", (nb, S, D), F32, kind="ExternalOutput").ap()
    program(nc, nb, out_dram=out, **args)
    r = run_bass_kernel_spmd(nc, [{f"in_{k}": v for k, v in arrays.items()}], core_ids=[0])
    return r.results[0]["out_x"]
```

```python
from contextlib import ExitStack

import concourse.bass as bass
from concourse import mybir

F32 = mybir.dt.float32
BF16 = mybir.dt.bfloat16
I32 = mybir.dt.int32
ACT = mybir.ActivationFunctionType
ALU = mybir.AluOpType
AX = mybir.AxisListType

D = 128
HEADS = 16
HD = D // HEADS
S = 56
CTX = 1500
P = 128
KT = -(-CTX // P)
LAST = CTX - (KT - 1) * P
PAIRS = HEADS // 2
PR = 2 * HD
PQ = 2 * S
PARTS_K = (0, 0, 0, 1, 1, 2)
PARTS_Q = (0, 1, 2, 0, 1, 0)
TERMS = len(PARTS_K)
SPLIT = TERMS * PR
FILLED = SPLIT + 3
STACK = FILLED + 3
CH = 500
NCH = CTX // CH
VW = PR + 1
TOK = 2 * S
EPS = 1e-5
SCALE = float(HD) ** -0.5
FILL = (998244352.0, 1753088.0, 2560.0)
MAGIC = 12582912.0
F0 = 512
FT = F0 // P
E = 8
GT = 4
GC = GT * TOK

MATS = ("wq0", "wk0", "wv0", "wo0", "wq1", "wk1", "wv1", "wo1", "mix", "ident", "pick",
        "woh0a", "woh0b", "woh0c", "woh0d", "woh1a", "woh1b", "woh1c", "woh1d",
        "fa", "fb", "fc", "fd", "ga", "gb", "gc", "gd")
COLS = ("g1", "be1", "bq0", "bk0", "bv0", "g_x", "b_x", "g_kv", "b_kv", "g2", "be2", "even", "odd")
ROWS = (("bo0", D), ("b2", D), ("b1", F0), ("bo1", D), ("g1", D), ("be1", D), ("mix_b", D), ("gates", 4))
ROW_AT = {}
for _name, _width in ROWS:
    ROW_AT[_name] = sum(w for _, w in ROWS[:len(ROW_AT)])
ROW_W = sum(w for _, w in ROWS)
STATS_FROM = 5
MADE = {0: [("key", 0, 0), ("key", 1, 0)], 1: [("key", 2, 0)], 3: [("mid", 0, 0)], 4: [("mid", 1, 0)],
        5: [("mid", 2, 0), ("value", 0, 0)], 7: [("value", 1, 0)], 9: [("value", 2, 0)]}
TURNS = {10: [("turn", 0, 0), ("turn", 1, 0)], 11: [("turn", 2, 0)]}
MIX_EARLY, MIX_LATE = 1, 3
LOOSE = ("score", "mix", "mid", "stat")
PEAKS_BY = (0, 2, 4, 7, 9, 11, 14, 16, 18, 20, 22, 24, 24)
RING = 3


class Shared:
    pass


class Step:

    def __init__(self, lap, u, first, laps, turn, make, peak, mix, finish):
        self.lap, self.u, self.first, self.laps = lap, u, first, laps
        self.turn, self.make, self.peak, self.mix, self.finish = turn, make, peak, mix, finish

    def batch(self, ahead):
        return 3 * self.lap + (self.u + ahead)

    def buf(self, ahead):
        return (self.u + ahead) % 3

    def use(self, ahead):
        return self.lap + (self.u + ahead) // 3

    def items(self):
        order = [("peak", p, j) for p in range(PAIRS) for j in range(NCH)]
        peaks = [order[PEAKS_BY[kt]:PEAKS_BY[kt + 1]] for kt in range(KT)]
        if not self.mix:
            out = [("total", 0, 0), ("project", 0, 0)] if self.finish else []
            if self.make:
                out += [item for kt in range(KT) for item in MADE.get(kt, [])]
                out += [("stat", n, 0) for n in range(KT)]
            if self.peak:
                out += order
            if self.turn:
                out += [item for kt in range(KT) for item in TURNS.get(kt, [])]
            if self.peak:
                out += [("shift", 0, 0), ("shift", 1, 0)]
            return out
        out = []
        for kt in range(KT):
            out.append(("score", kt, 0))
            if self.finish:
                out += {0: [("total", 0, 0)], 5: [("project", 0, 0)]}.get(kt, [])
            made = MADE.get(kt, []) if self.make else []
            found = peaks[kt] if self.peak else []
            both = []
            for n in range(max(len(made), len(found))):
                both += (found[n:n + 1] + made[n:n + 1]) if kt > 1 else (made[n:n + 1] + found[n:n + 1])
            if self.turn:
                both += TURNS.get(kt, [])
            if self.make and STATS_FROM <= kt < STATS_FROM + KT // 2:
                both += [("stat", 2 * (kt - STATS_FROM) + n, 0) for n in range(2)]
            if kt:
                both.insert(MIX_EARLY if kt < KT // 2 else MIX_LATE, ("mix", kt - 1, 0))
            out += both
        if self.peak:
            out += [("shift", 0, 0), ("shift", 1, 0)]
        out.append(("mix", KT - 1, 0))
        return out

    def slots(self):
        n, out = 0, []
        for kind, a, b in self.items():
            if kind in LOOSE:
                out.append((kind, a, b, 0, 0))
            else:
                at = self.first + n
                out.append((kind, a, b, at % RING, at // RING + self.laps))
                n += 1
        return out

    def last_turn(self):
        before = Step(0, 0, 0, 0, True, self.peak, self.mix, self.finish, False)
        kinds = [kind for kind, _, _ in before.items() if kind not in LOOSE]
        at = self.first - 1 - kinds[::-1].index("turn")
        return at % RING, at // RING + self.laps + 1

    def width(self):
        return sum(kind not in LOOSE for kind, _, _ in self.items())


def run_steps(eng, nb, body):
    first = 0
    for s in range(-3, 3):
        step = Step(s // 3, s % 3, first, 0, True, s >= -2, s >= -1, s >= 0, s >= 1)
        body(step)
        first += step.width()
    steady = Step(1, 0, 0, 0, True, True, True, True, True).width()
    with eng.Fori(1, (nb - 2) // 3) as lap:
        for u in range(3):
            body(Step(lap, u, first + (u - 3) * steady, lap * steady, True, True, True, True, True))
    first += (nb - 5) * steady
    for s in (nb - 2, nb - 1, nb):
        step = Step(s // 3, s % 3, first, 0, False, False, s == nb - 2, s < nb, True)
        body(step)
        first += step.width()


def rows_of(kt):
    return P if kt < KT - 1 else LAST


def setup(nc, m, early):
    mask = early.enter_context(nc.sbuf_tensor("mask", [m.nb, CTX], I32))
    keep = early.enter_context(nc.sbuf_tensor("keep", [m.nb, CTX], BF16))
    fill = early.enter_context(nc.sbuf_tensor("fill", [m.nb, 3, CTX], BF16))
    with ExitStack() as ctx:
        x_loaded = ctx.enter_context(nc.semaphore("x_loaded"))
        mask_loaded = ctx.enter_context(nc.semaphore("mask_loaded"))
        made = ctx.enter_context(nc.semaphore("masks_made"))
        block = ctx.enter_context(nc.Block())

        @block.sync
        def _(sp):
            sp.dma_start(mask[:, :], m.mask_dram).then_inc(mask_loaded, 16)
            sp.dma_start(m.x[:, :, :], m.x_dram.rearrange("b s d -> (b s) d").rearrange(
                "(n p) d -> p n d", p=TOK)).then_inc(x_loaded, 16)
            sp.dma_start(m.mats[:, :], m.mats_dram).then_inc(m.weights_loaded, 16)
            sp.dma_start(m.cols[:, :], m.cols_dram).then_inc(m.weights_loaded, 16)
            sp.dma_start(m.rows[:, :], m.rows_dram.partition_broadcast(P)).then_inc(m.weights_loaded, 16)
            sp.dma_start(m.router[:, :], m.router_dram).then_inc(m.weights_loaded, 16)
            sp.dma_start(m.b2e[:, :], m.b2e_dram).then_inc(m.weights_loaded, 16)
            sp.wait_ge(made, 4)
            sp.dma_start(m.keep_dram, keep[:, :]).then_inc(m.masks_saved, 16)
            sp.dma_start(m.fill_dram, fill[:, :, :]).then_inc(m.masks_saved, 16)
            sp.wait_ge(x_loaded, 16)

        @block.vector
        def _(dve):
            dve.wait_ge(mask_loaded, 16)
            nc.vector.tensor_scalar(keep[:, :], mask[:, :], 0.0, None, ALU.not_equal).then_inc(made, 1)
            dve.wait_ge(made, 1)
            for n in range(3):
                nc.vector.tensor_scalar(fill[:, n, :], keep[:, :], 1.0, FILL[n], ALU.subtract, ALU.mult)\
                    .then_inc(made, 1)


WEIGHT_LOADS = 5


def mat(m, name):
    at = MATS.index(name) * P
    return m.mats[:, at:at + P]


def col(m, name):
    at = COLS.index(name)
    return m.cols[:, at:at + 1]


def row(m, name, p=P):
    at = ROW_AT[name]
    return m.rows[0:p, at:at + dict(ROWS)[name]]


def per_token(ap, nt, width=D):
    return ap.unsqueeze(2).to_broadcast([TOK, nt, width])


def per_channel(ap, nt, width=D):
    return ap.unsqueeze(1).to_broadcast([TOK, nt, width])


class Chain:

    def __init__(self, eng, sem):
        self.eng, self.sem, self.n = eng, sem, 0

    def then(self, ins):
        self.n += 1
        ins.then_inc(self.sem, 1)
        self.eng.wait_ge(self.sem, self.n)

    def mark(self, ins):
        self.n += 1
        ins.then_inc(self.sem, 1)
        return self.n


def norm_vector(nc, dve, chain, normal, src, dst, tmp, st, nt, turn):
    for i in range(nt):
        last = nc.vector.bn_stats(tmp[:, i, 0:6], src[:, i, :])
    chain.then(last)
    even, odd, apart, squares = tmp[:, :, 1], tmp[:, :, 4], tmp[:, :, 6], tmp[:, :, 7]
    chain.mark(nc.vector.tensor_tensor(apart, even, odd, ALU.subtract))
    chain.mark(nc.vector.tensor_tensor(squares, tmp[:, :, 2], tmp[:, :, 5], ALU.add))
    chain.then(nc.vector.tensor_tensor(st[:, 0, :], even, odd, ALU.add))
    chain.then(nc.vector.scalar_tensor_tensor(out=apart, in0=apart, scalar=D / 4.0, in1=apart,
                                              op0=ALU.mult, op1=ALU.mult))
    chain.then(nc.vector.tensor_tensor(st[:, 2, :], squares, apart, ALU.add))
    chain.mark(nc.vector.tensor_scalar(st[:, 1, :], st[:, 0, :], 0.5, None, ALU.mult))
    dve.wait_ge(normal, turn + 1)
    chain.then(nc.vector.reciprocal(st[:, 4, :], st[:, 3, :]))
    chain.mark(nc.vector.scalar_tensor_tensor(out=st[:, 5, :], in0=st[:, 1, :], scalar=-1.0, in1=st[:, 4, :],
                                              op0=ALU.mult, op1=ALU.mult))
    own = nt - nt * 3 // 8
    for i in range(own):
        if i == own - 1:
            dve.wait_ge(normal, turn + 2)
        last = nc.vector.tensor_scalar(dst[:, i, :], src[:, i, :], st[:, 1, i:i + 1], st[:, 4, i:i + 1],
                                       ALU.subtract, ALU.mult)
    chain.then(last)


NORM_LINKS = 10
NORM_SUM = 6
NORM_SHIFT = 9


def norm_scalar(nc, act, m, chain_sem, at, normal, src, dst, st, nt):
    act.wait_ge(chain_sem, at + NORM_SUM)
    nc.scalar.activation(st[:, 3, :], st[:, 2, :], ACT.Sqrt, bias=m.eps[0:TOK, 0:1], scale=1.0 / D)\
        .then_inc(normal, 1)
    act.wait_ge(chain_sem, at + NORM_SHIFT)
    for i in range(nt - nt * 3 // 8, nt):
        last = nc.scalar.activation(dst[:, i, :], src[:, i, :], ACT.Identity, bias=st[:, 5, i:i + 1],
                                    scale=st[:, 4, i:i + 1])
    last.then_inc(normal, 1)


class KeyNorms:

    LINKS = 8

    def __init__(self, nc, m, ctx):
        nk = m.nb * KT
        self.nc, self.m = nc, m

        def sb(name, shape):
            return ctx.enter_context(nc.sbuf_tensor("kn_" + name, shape, F32))

        def sem(name):
            return ctx.enter_context(nc.semaphore("kn_" + name))

        self.st = sb("st", [P, nk, 6])
        self.apart, self.var, self.half, self.root = (sb(n, [P, nk]) for n in ("apart", "var", "half", "root"))
        self.norms = sb("norms", [P, m.nb, 2, KT])
        self.loaded, self.links, self.rooted, self.saved = sem("loaded"), sem("links"), sem("rooted"), sem("saved")

    def fetch(self, sp):
        sp.dma_start(self.st[:, :, :].rearrange("p k n -> p (k n)"),
                     self.m.stats_dram.rearrange("p b n -> p (b n)")).then_inc(self.loaded, 16)

    def put_back(self, sp):
        sp.wait_ge(self.links, self.LINKS)
        sp.dma_start(self.m.norms_dram.rearrange("p b n -> p (b n)"),
                     self.norms[:, :, :, :].rearrange("p b n c -> p (b n c)")).then_inc(self.saved, 16)
        sp.wait_ge(self.saved, 16)

    def by_batch(self, ap):
        return ap.rearrange("p (b c) -> p b c", c=KT)

    def vector(self, dve):
        nc, chain, apart, var = self.nc, Chain(dve, self.links), self.apart, self.var
        even, odd = self.st[:, :, 1], self.st[:, :, 4]
        dve.wait_ge(self.loaded, 16)
        chain.then(nc.vector.tensor_scalar(self.half[:, :], odd, 0.5, None, ALU.mult))
        chain.then(nc.vector.tensor_tensor(apart[:, :], even, odd, ALU.subtract))
        chain.then(nc.vector.tensor_tensor(apart[:, :], apart[:, :], apart[:, :], ALU.mult))
        chain.then(nc.vector.tensor_scalar(apart[:, :], apart[:, :], 0.25, None, ALU.mult))
        chain.then(nc.vector.tensor_tensor(var[:, :], self.st[:, :, 2], self.st[:, :, 5], ALU.add))
        chain.mark(nc.vector.scalar_tensor_tensor(out=var[:, :], in0=var[:, :], scalar=1.0 / D, in1=apart[:, :],
                                                  op0=ALU.mult, op1=ALU.add))
        chain.mark(nc.vector.scalar_tensor_tensor(out=self.norms[:, :, 0, :], in0=self.by_batch(even), scalar=0.5,
                                                  in1=self.by_batch(self.half[:, :]), op0=ALU.mult, op1=ALU.add))
        dve.wait_ge(self.rooted, 1)
        chain.mark(nc.vector.reciprocal(self.norms[:, :, 1, :], self.by_batch(self.root[:, :])))

    def scalar(self, act):
        act.wait_ge(self.links, 6)
        self.nc.scalar.activation(self.root[:, :], self.var[:, :], ACT.Sqrt, bias=self.m.eps[:, 0:1])\
            .then_inc(self.rooted, 1)


def queries(nc, m, layer):
    nt, ng = m.nt, m.nt // GT if m.nt >= GT else 1
    gt = min(GT, m.nt)
    gc = gt * TOK
    L = str(layer)
    norms = 1 + layer
    cols = nt * TOK
    with ExitStack() as ctx:
        def sb(name, shape, dt):
            return ctx.enter_context(nc.sbuf_tensor(f"q{L}_{name}", shape, dt))

        def sem(name):
            return ctx.enter_context(nc.semaphore(f"q{L}_{name}"))

        z = sb("z", [TOK, nt, D], F32)
        sq = sb("sq", [TOK, nt, D], F32)
        st = sb("st", [TOK, 6, nt], F32)
        zT = sb("zT", [P, cols], F32)
        qf = sb("qf", [P, cols], F32)
        rest = sb("rest", [P, cols], F32)
        part = sb("part", [P, 3, cols], BF16)
        block_q = sb("block_q", [P, 3, m.nb, PQ], BF16)
        wq = sb("wq", [P, P], F32)
        bq = sb("bq", [P, 1], F32)
        bvb = sb("bvb", [P, TOK], F32)
        turned = [ctx.enter_context(nc.psum_tensor(f"q{L}_turned{g}", [P, 512], F32)) for g in range(ng)]
        qps = ctx.enter_context(nc.psum_tensor(f"q{L}_qps", [P, 2, 512], F32))
        small = ctx.enter_context(nc.psum_tensor(f"q{L}_small", [P, 512], F32))
        normed, roots, turns, turns_out = sem("normed"), sem("roots"), sem("turns"), sem("turns_out")
        folded, biases = sem("folded"), sem("biases")
        projected, steps, blocks, saved = sem("projected"), sem("steps"), sem("blocks"), sem("saved")
        eps_set = sem("eps_set")
        key_norms = KeyNorms(nc, m, ctx) if layer else None
        block = ctx.enter_context(nc.Block())
        last_norm = NORM_LINKS * norms

        @block.vector
        def _(dve):
            if layer == 0:
                nc.vector.memset(m.eps[:, :], EPS).then_inc(eps_set, 1)
            chain = Chain(dve, normed)
            src = m.x
            for n in range(norms):
                norm_vector(nc, dve, chain, roots, src[:, :, :], z[:, :, :], sq[:, :, :], st, nt, 2 * n)
                src = z
            if layer == 0:
                dve.wait_ge(m.weights_loaded, 16 * WEIGHT_LOADS)
                nc.vector.tensor_copy(wq[:, :], mat(m, "wq0")).then_inc(folded, 1)
                nc.vector.tensor_copy(m.wk[0][:, :], mat(m, "wk0")).then_inc(folded, 1)
                nc.vector.tensor_copy(m.wv[0][:, :], mat(m, "wv0")).then_inc(folded, 1)
                nc.vector.tensor_copy(bq[:, :], col(m, "bq0")).then_inc(folded, 1)
                nc.vector.tensor_copy(m.bk[0][:, :], col(m, "bk0")).then_inc(folded, 1)
                nc.vector.tensor_copy(bvb[:, :], col(m, "bv0").to_broadcast([P, TOK])).then_inc(folded, 1)
            else:
                nc.vector.tensor_scalar(wq[:, :], mat(m, "wq1"), col(m, "g_x"), None, ALU.mult).then_inc(folded, 1)
                nc.vector.tensor_scalar(m.wk[1][:, :], mat(m, "wk1"), col(m, "g_kv"), None, ALU.mult).then_inc(folded, 1)
                nc.vector.tensor_scalar(m.wv[1][:, :], mat(m, "wv1"), col(m, "g_kv"), None, ALU.mult).then_inc(folded, 1)
                dve.wait_ge(biases, 1)
                nc.vector.tensor_copy(bq[:, :], small[:, 0:1]).then_inc(folded, 1)
                nc.vector.tensor_copy(m.bk[1][:, :], small[:, 1:2]).then_inc(folded, 1)
                nc.vector.tensor_copy(bvb[:, :], small[:, 2:3].to_broadcast([P, TOK])).then_inc(folded, 1)
            dve.wait_ge(biases, 2)
            nc.vector.tensor_tensor(m.yb[layer][:, :], small[0:TOK, 128:256], row(m, "bo" + L, TOK), ALU.add)\
                .then_inc(folded, 1)
            done = Chain(dve, steps)
            for g in range(ng):
                dve.wait_ge(projected, g + 1)
                dve.wait_ge(folded, 4)
                nc.vector.tensor_scalar(qf[:, g * gc:(g + 1) * gc], qps[:, g % 2, 0:gc], bq[:, 0:1], SCALE,
                                        ALU.add, ALU.mult).then_inc(steps, 1)
            done.n = ng
            dve.wait_ge(steps, ng)
            done.then(nc.vector.tensor_copy(part[:, 0, :], qf[:, :]))
            done.then(nc.vector.tensor_tensor(rest[:, :], qf[:, :], part[:, 0, :], ALU.subtract))
            done.then(nc.vector.tensor_copy(part[:, 1, :], rest[:, :]))
            done.then(nc.vector.tensor_tensor(part[:, 2, :], rest[:, :], part[:, 1, :], ALU.subtract))
            for n in range(3):
                for h, name in enumerate(("even", "odd")):
                    nc.vector.tensor_scalar(
                        block_q[:, n, :, h * S:(h + 1) * S], part[:, n, :].rearrange("p (b q) -> p b q", q=S),
                        col(m, name), None, ALU.mult).then_inc(blocks, 1)
            if layer:
                key_norms.vector(dve)

        @block.scalar
        def _(act):
            if layer == 0:
                act.wait_ge(eps_set, 1)
            for n in range(norms):
                norm_scalar(nc, act, m, normed, NORM_LINKS * n, roots, z if n else m.x, z, st, nt)
            if layer == 0:
                act.wait_ge(m.weights_loaded, 16 * WEIGHT_LOADS)
                nc.scalar.activation(m.identb[:, :], mat(m, "ident"), ACT.Copy)
                nc.scalar.activation(m.gates[:, :], m.rows[:, ROW_AT["gates"]:ROW_AT["gates"] + 4], ACT.Tanh)
            for g in range(ng):
                act.wait_ge(turns, g + 1)
                nc.scalar.activation(zT[:, g * gc:(g + 1) * gc], turned[g][:, 0:gc], ACT.Copy)\
                    .then_inc(turns_out, 1)
            if layer:
                key_norms.scalar(act)

        @block.tensor
        def _(pe):
            if layer == 1:
                for n, (w, b) in enumerate((("wq1", "b_x"), ("wk1", "b_kv"), ("wv1", "b_kv"))):
                    last = nc.tensor.matmul(small[:, n:n + 1], mat(m, w), col(m, b), start=True, stop=True)
                last.then_inc(biases, 1)
            else:
                pe.wait_ge(m.weights_loaded, 16 * WEIGHT_LOADS)
                pe.sem_inc(biases, 1)
            pe.wait_ge(folded, 6)
            nc.tensor.matmul(small[0:TOK, 128:256], bvb[:, :], mat(m, "wo" + L), start=True, stop=True)\
                .then_inc(biases, 1)
            pe.wait_ge(normed, last_norm)
            for g in range(ng):
                for i in range(gt):
                    last = nc.tensor.transpose(turned[g][:, i * TOK:(i + 1) * TOK], z[:, g * gt + i, :],
                                               mat(m, "ident")[0:TOK, 0:TOK])
                last.then_inc(turns, 1)
            for g in range(ng):
                pe.wait_ge(turns_out, g + 1)
                if g >= 2:
                    pe.wait_ge(steps, g - 1)
                nc.tensor.matmul(qps[:, g % 2, 0:gc], wq[:, :], zT[:, g * gc:(g + 1) * gc], start=True, stop=True)\
                    .then_inc(projected, 1)

        @block.sync
        def _(sp):
            if layer:
                key_norms.fetch(sp)
            for n in range(3):
                sp.wait_ge(blocks, 2 * n + 2)
                sp.dma_start(m.q_dram[n].rearrange("r p b c -> p r (b c)"),
                             block_q[:, n, :, :].rearrange("p b c -> p (b c)")).then_inc(saved, 16)
            if layer:
                key_norms.put_back(sp)
            sp.wait_ge(saved, 16 * 3)
            if layer == 0:
                sp.wait_ge(m.masks_saved, 32)


def attention(nc, m, layer):
    nb = m.nb
    raw_loads = 2 if layer == 0 else 3
    rows_a = SPLIT if layer == 0 else FILLED
    loads = 6 if layer == 0 else 7
    L = str(layer)
    with ExitStack() as ctx:
        def sb(name, shape, dt):
            return ctx.enter_context(nc.sbuf_tensor(f"a{L}_{name}", shape, dt))

        def sem(name):
            return ctx.enter_context(nc.semaphore(f"a{L}_{name}"))

        ones = sb("ones", [STACK, CTX], BF16)
        kstack = sb("kstack", [STACK, 3, PAIRS, CTX], BF16)
        qstack = sb("qstack", [STACK, 3, PAIRS, PQ], BF16)
        raw = sb("raw", [P, 3, KT, D], F32)
        stats = sb("stats", [P, KT, 6], F32) if layer == 0 else None
        norms = sb("norms", [P, 3, 2, KT], F32) if layer else None
        rawT = sb("rawT", [P, CTX], F32)
        kf = sb("kf", [P, CTX], F32)
        rest = sb("rest", [P, CTX], F32)
        part = sb("part", [P, 3, CTX], BF16)
        keep = sb("keep", [P, CTX], BF16) if layer else None
        vals = sb("vals", [P, 3, KT, PAIRS, VW], F32)
        probs = sb("probs", [P, 2, 2, GC], F32)
        mixed_sb = sb("mixed_sb", [P, 2 * PQ], F32)
        inverse = sb("inverse", [P, 2 * PQ], F32)
        heads = sb("heads", [P, 2, 2, S], F32)
        out_sb = sb("out_sb", [S, D], F32)
        peaks = sb("peaks", [PQ, PAIRS, NCH], F32)
        low = sb("low", [PQ, 3, PAIRS], F32)
        shift = sb("shift", [PQ, PAIRS, 6], BF16)
        scores = [ctx.enter_context(nc.psum_tensor(f"a{L}_scores{i}", [P, 2, 512], F32)) for i in range(2)]
        ring = [ctx.enter_context(nc.psum_tensor(f"a{L}_ring{i}", [P, 512], F32)) for i in range(RING)]
        mix_ps = ctx.enter_context(nc.psum_tensor(f"a{L}_mix", [P, 512], F32))

        ones_made, ones_spread, shift_set = sem("ones_made"), sem("ones_spread"), sem("shift_set")
        ready = sem("ready")
        raw_loaded = [sem(f"raw_loaded{i}") for i in range(3)]
        stats_made, stats_saved = sem("stats_made"), sem("stats_saved")
        centred, normed = sem("centred"), sem("normed")
        keep_loaded = sem("keep_loaded")
        filled = [sem(f"ring_filled{i}") for i in range(RING)]
        drained = [sem(f"ring_drained{i}") for i in range(RING)]
        high_made, rest_made, mid_made, low_made = sem("high_made"), sem("rest_made"), sem("mid_made"), sem("low_made")
        part_saved = [sem(f"part_saved{i}") for i in range(3)]
        stack_loaded = [sem(f"stack_loaded{i}") for i in range(3)]
        scored, exped, mixed, mix_read = sem("scored"), sem("exped"), sem("mixed"), sem("mix_read")
        shift_steps, normalised, out_saved = sem("shift_steps"), sem("normalised"), sem("out_saved")
        READY = 6
        SHIFTS = 6
        block = ctx.enter_context(nc.Block())

        @block.sync
        def _(sp):
            def load_context(k, batch):
                sp.dma_start(raw[:, k, 0:KT - 1, :], m.ctx_dram[batch, 0:(KT - 1) * P, :].rearrange(
                    "(c p) d -> p c d", p=P)).then_inc(raw_loaded[k], 16)
                sp.dma_start(raw[0:LAST, k, KT - 1, :], m.ctx_dram[batch, (KT - 1) * P:CTX, :])\
                    .then_inc(raw_loaded[k], 16)
                if layer:
                    sp.dma_start(norms[:, k, :, :].rearrange("p n c -> p (n c)"), m.norms_dram[:, batch, :])\
                        .then_inc(raw_loaded[k], 16)

            sp.wait_ge(ready, 1)
            load_context(0, 0)
            sp.wait_ge(ones_made, 1)
            for k in range(3):
                sp.dma_start(kstack[SPLIT:STACK, k, :, :],
                             ones[SPLIT:STACK, :].unsqueeze(1).to_broadcast([STACK - SPLIT, PAIRS, CTX]))\
                    .then_inc(ones_spread, 16)
            sp.wait_ge(ready, READY - 1)
            sp.wait_ge(ones_spread, 48)
            sp.sem_inc(ready, 1)

            def step(s):
                if not s.make:
                    return
                load_context(s.buf(3), s.batch(3) % nb)
                if layer:
                    if s.peak:
                        sp.wait_ge(high_made, NCH * s.batch(2))
                    sp.dma_start(keep[:, :], m.keep_dram[s.batch(2)].partition_broadcast(P)).then_inc(keep_loaded, 16)
                k, batch = s.buf(2), s.batch(2)
                if s.mix:
                    sp.wait_ge(scored, 12 * s.batch(0))
                at = 0
                for n in (3, 2, 1):
                    sp.dma_start(qstack[at:at + n * PR, k, :, :],
                                 m.q_dram[0:n, :, :, batch, :].rearrange("t r p c -> (t r) p c"))\
                        .then_inc(stack_loaded[k], 16)
                    at += n * PR
                if layer:
                    sp.dma_start(kstack[SPLIT:FILLED, k, :, :],
                                 m.fill_dram[batch].unsqueeze(1).to_broadcast([3, PAIRS, CTX]))\
                        .then_inc(stack_loaded[k], 16)
                def save(n, made):
                    sp.wait_ge(made, NCH * (batch + 1))
                    sp.dma_start(m.k_dram[k, n].rearrange("r p n -> p r n"), part[:, n, :])\
                        .then_inc(part_saved[n], 16)

                def stack(n):
                    at, rows = PARTS_K.index(n) * PR, PARTS_K.count(n)
                    sp.wait_ge(part_saved[n], 16 * (batch + 1))
                    sp.dma_start(kstack[at:at + rows * PR, k, :, :],
                                 m.k_dram[k, n].unsqueeze(0).to_broadcast([rows, PR, PAIRS, CTX]))\
                        .then_inc(stack_loaded[k], 16)

                save(0, high_made)
                save(1, mid_made)
                stack(0)
                save(2, low_made)
                stack(1)
                stack(2)
                if layer == 0:
                    sp.wait_ge(stats_made, batch + 1)
                    sp.dma_start(m.stats_dram[:, batch, :], stats[:, :, :].rearrange("p c n -> p (c n)"))\
                        .then_inc(stats_saved, 16)

            run_steps(sp, nb, step)
            for k in range(3):
                sp.wait_ge(stack_loaded[k], 16 * loads * len(range(k, nb, 3)))
                sp.wait_ge(raw_loaded[k], 16 * raw_loads * len(range(k, nb + 1, 3)))
            if layer == 0:
                sp.wait_ge(stats_saved, 16 * nb)

        @block.scalar
        def _(act):
            act.wait_ge(ready, READY)
            act.sem_inc(exped, 2)

            def step(s):
                for kind, a, j, bank, before in s.slots():
                    if kind == "score":
                        rows, n = rows_of(a), 12 * s.batch(0) + a + 1
                        act.wait_ge(scored, n)
                        act.wait_ge(mixed, n)
                        nc.scalar.activation(probs[0:rows, a % 2, :, :], scores[a % 2][0:rows, :, 0:GC], ACT.Exp)\
                            .then_inc(exped, 1)
                    elif kind == "turn":
                        act.wait_ge(filled[bank], before + 1)
                        width = min(512, CTX - 512 * a)
                        nc.scalar.activation(rawT[:, 512 * a:512 * a + width], ring[bank][:, 0:width], ACT.Copy)\
                            .then_inc(drained[bank], 1)
                    elif kind == "key":
                        if layer == 0:
                            act.wait_ge(filled[bank], before + 1)
                            if s.peak:
                                act.wait_ge(rest_made, NCH * s.batch(1) + a + 1)
                            nc.scalar.activation(kf[:, CH * a:CH * (a + 1)], ring[bank][:, 0:CH], ACT.Identity,
                                                 bias=m.bk[0][:, 0:1]).then_inc(drained[bank], 1)
                        act.wait_ge(drained[bank], before + 1)
                        if s.peak:
                            act.wait_ge(part_saved[0], 16 * s.batch(2))
                            act.wait_ge(rest_made, NCH * s.batch(1) + a + 1)
                        nc.scalar.activation(part[:, 0, CH * a:CH * (a + 1)], kf[:, CH * a:CH * (a + 1)], ACT.Copy)\
                            .then_inc(high_made, 1)
                    elif kind == "value":
                        act.wait_ge(filled[bank], before + 1)
                        tiles = ring[bank][:, :].rearrange("p (c h e) -> p c h e", c=4, h=PAIRS)
                        k = s.buf(2)
                        if a < NCH - 1:
                            nc.scalar.activation(vals[:, k, 4 * a:4 * a + 4, :, 0:PR], tiles, ACT.Copy)\
                                .then_inc(drained[bank], 1)
                        else:
                            nc.scalar.activation(vals[:, k, 4 * a:4 * a + 3, :, 0:PR], tiles[:, 0:3], ACT.Copy)
                            nc.scalar.activation(vals[0:LAST, k, KT - 1, :, 0:PR], tiles[0:LAST, 3], ACT.Copy)\
                                .then_inc(drained[bank], 1)
                    elif kind == "mix" and a == KT - 1:
                        act.wait_ge(mixed, 12 * s.batch(1) + 2)
                        nc.scalar.activation(mixed_sb[:, :], mix_ps[:, 0:2 * PQ], ACT.Copy).then_inc(mix_read, 1)
                    elif kind == "project":
                        act.wait_ge(filled[bank], before + 1)
                        act.wait_ge(out_saved, 16 * s.batch(-1))
                        nc.scalar.activation(out_sb[:, :], ring[bank][0:S, 0:D], ACT.Copy)\
                            .then_inc(drained[bank], 1)
                        act.wait_ge(drained[bank], before + 1)
                        act.dma_start(m.y_dram[s.batch(-1)], out_sb[:, :]).then_inc(out_saved, 16)

            run_steps(act, nb, step)
            act.wait_ge(out_saved, 16 * nb)

        @block.vector
        def _(dve):
            nc.vector.memset(raw[:, :, KT - 1, :], 0.0).then_inc(ready, 1)
            nc.vector.memset(ones[SPLIT:STACK, :], 1.0).then_inc(ones_made, 1)
            nc.vector.memset(qstack[SPLIT:STACK, :, :, :], 1.0).then_inc(ready, 1)
            nc.vector.memset(vals[:, :, :, :, PR:VW], 1.0).then_inc(ready, 1)
            nc.vector.memset(shift[:, :, :], 1.0).then_inc(shift_set, 1)
            nc.vector.memset(mix_ps[:, :], 0.0).then_inc(ready, 1)
            if layer == 0:
                dve.wait_ge(shift_set, 1)
                nc.vector.memset(shift[:, :, 0:3], 0.0).then_inc(ready, 1)
            else:
                nc.vector.memset(low[:, :, :], 0.0).then_inc(ready, 1)
            dve.wait_ge(ready, READY)

            def mids(s, chunks):
                batch = s.batch(2)
                for a in chunks:
                    dve.wait_ge(rest_made, NCH * batch + a + 1)
                    if s.peak:
                        dve.wait_ge(part_saved[1], 16 * batch)
                        dve.wait_ge(low_made, NCH * s.batch(1) + a + 1)
                    nc.vector.tensor_copy(part[:, 1, CH * a:CH * (a + 1)], rest[:, CH * a:CH * (a + 1)])\
                        .then_inc(mid_made, 1)

            def step(s):
                for kind, a, j, bank, before in s.slots():
                    if kind == "peak":
                        dve.wait_ge(filled[bank], before + 1)
                        nc.vector.tensor_reduce(peaks[:, a, j:j + 1], ring[bank][0:PQ, 0:CH], AX.X, ALU.max)\
                            .then_inc(drained[bank], 1)
                        if (a, j) == (PAIRS - 1, NCH - 1):
                            n = SHIFTS * s.batch(1)
                            dve.wait_ge(drained[bank], before + 1)
                            nc.vector.tensor_reduce(low[:, 0, :], peaks[:, :, :], AX.X, ALU.max, negate=True)\
                                .then_inc(shift_steps, 1)
                            dve.wait_ge(shift_steps, n + 1)
                            nc.vector.tensor_copy(shift[:, :, 3], low[:, 0, :]).then_inc(shift_steps, 1)
                            dve.wait_ge(shift_steps, n + 2)
                            nc.vector.tensor_tensor(low[:, 1, :], low[:, 0, :], shift[:, :, 3], ALU.subtract)\
                                .then_inc(shift_steps, 1)
                            dve.wait_ge(shift_steps, n + 3)
                            nc.vector.tensor_copy(shift[:, :, 4], low[:, 1, :]).then_inc(shift_steps, 1)
                            dve.wait_ge(shift_steps, n + 4)
                            nc.vector.tensor_tensor(low[:, 2, :], low[:, 1, :], shift[:, :, 4], ALU.subtract)\
                                .then_inc(shift_steps, 1)
                            dve.wait_ge(shift_steps, n + 5)
                            nc.vector.tensor_copy(shift[:, :, 5], low[:, 2, :]).then_inc(shift_steps, 1)
                    elif kind == "shift":
                        dve.wait_ge(filled[bank], before + 1)
                        nc.vector.tensor_copy(qstack[SPLIT:STACK, s.buf(1), 4 * a:4 * a + 4, :],
                                              ring[bank][SPLIT:STACK, 0:GC].rearrange("r (p c) -> r p c", p=4))\
                            .then_inc(drained[bank], 1)
                    elif kind == "key" and layer:
                        dve.wait_ge(filled[bank], before + 1)
                        dve.wait_ge(keep_loaded, 16 * (s.batch(2) + 1))
                        if s.peak:
                            dve.wait_ge(rest_made, NCH * s.batch(1) + a + 1)
                        nc.vector.scalar_tensor_tensor(
                            out=kf[:, CH * a:CH * (a + 1)], in0=ring[bank][:, 0:CH], scalar=m.bk[1][:, 0:1],
                            in1=keep[:, CH * a:CH * (a + 1)], op0=ALU.add, op1=ALU.mult)\
                            .then_inc(drained[bank], 1)
                    elif kind == "mid":
                        mids(s, [a])
                    elif kind == "stat" and layer == 0:
                        if a == 0:
                            dve.wait_ge(raw_loaded[s.buf(2)], 32 * (s.use(2) + 1))
                            if s.peak:
                                dve.wait_ge(stats_saved, 16 * s.batch(2))
                        last = nc.vector.bn_stats(stats[:, a, :], raw[:, s.buf(2), a, :])
                        if a == KT - 1:
                            last.then_inc(stats_made, 1)
                    elif kind == "total":
                        dve.wait_ge(filled[bank], before + 1)
                        nc.vector.reciprocal(inverse[:, :], ring[bank][:, 0:2 * PQ]).then_inc(drained[bank], 1)
                        dve.wait_ge(drained[bank], before + 1)
                        nc.vector.tensor_tensor(heads[:, :, :, :].rearrange("p r x q -> p (r x q)"),
                                                mixed_sb[:, :], inverse[:, :], ALU.mult).then_inc(normalised, 1)

            run_steps(dve, nb, step)

        @block.gpsimd
        def _(pool):
            def normalise(k, batch, use):
                def per_key(n):
                    return norms[:, k, n, :].unsqueeze(2).to_broadcast([P, KT, D])

                pool.wait_ge(raw_loaded[k], 16 * raw_loads * (use + 1))
                nc.gpsimd.tensor_tensor(raw[:, k, :, :], raw[:, k, :, :], per_key(0), ALU.subtract)\
                    .then_inc(centred, 1)
                pool.wait_ge(centred, batch + 1)
                nc.gpsimd.tensor_tensor(raw[:, k, :, :], raw[:, k, :, :], per_key(1), ALU.mult)\
                    .then_inc(normed, 1)

            pool.wait_ge(ready, READY)
            if layer:
                normalise(0, 0, 0)

            def step(s):
                if not s.make:
                    return
                batch = s.batch(2)
                for a in range(NCH):
                    pool.wait_ge(high_made, NCH * batch + a + 1)
                    if s.peak:
                        pool.wait_ge(low_made, NCH * s.batch(1) + a + 1)
                    nc.gpsimd.tensor_tensor(rest[:, CH * a:CH * (a + 1)], kf[:, CH * a:CH * (a + 1)],
                                            part[:, 0, CH * a:CH * (a + 1)], ALU.subtract).then_inc(rest_made, 1)
                for a in range(NCH):
                    pool.wait_ge(mid_made, NCH * batch + a + 1)
                    if s.peak:
                        pool.wait_ge(part_saved[2], 16 * batch)
                    nc.gpsimd.tensor_tensor(part[:, 2, CH * a:CH * (a + 1)], rest[:, CH * a:CH * (a + 1)],
                                            part[:, 1, CH * a:CH * (a + 1)], ALU.subtract).then_inc(low_made, 1)
                if layer:
                    normalise(s.buf(3), s.batch(3), s.use(3))

            run_steps(pool, nb, step)

        @block.tensor
        def _(pe):
            pe.wait_ge(ready, READY)
            pe.sem_inc(mixed, 2)
            ident = mat(m, "ident")

            def step(s):
                shifts = []
                for kind, a, j, bank, before in s.slots():
                    if kind not in LOOSE:
                        pe.wait_ge(drained[bank], before)
                    if kind == "score":
                        rows, k = rows_of(a), s.buf(0)
                        pe.wait_ge(exped, 12 * s.batch(0) + a + 1)
                        for p in range(PAIRS):
                            last = nc.tensor.matmul(
                                scores[a % 2][0:rows, p // 4, (p % 4) * PQ:(p % 4 + 1) * PQ],
                                kstack[:, k, p, P * a:P * a + rows], qstack[:, k, p, :], start=True, stop=True)
                        last.then_inc(scored, 1)
                    elif kind == "mix":
                        rows, k = rows_of(a), s.buf(0)
                        pe.wait_ge(exped, 12 * s.batch(0) + a + 3)
                        if a == 0:
                            pe.wait_ge(mix_read, s.batch(0))
                        for p in range(PAIRS):
                            r, q = p // 4, p % 4
                            last = nc.tensor.matmul(
                                mix_ps[32 * q:32 * q + VW, r * PQ:(r + 1) * PQ], vals[0:rows, k, a, p, :],
                                probs[0:rows, a % 2, r, q * PQ:(q + 1) * PQ],
                                start=(a == 0 and r == 0), stop=(a == KT - 1), skip_group_check=True)
                        last.then_inc(mixed, 1)
                    elif kind == "peak":
                        k = s.buf(1)
                        if (a, j) == (0, 0):
                            pe.wait_ge(stack_loaded[k], 16 * loads * (s.use(1) + 1))
                        nc.tensor.matmul(ring[bank][0:PQ, 0:CH], qstack[0:rows_a, k, a, :],
                                         kstack[0:rows_a, k, a, CH * j:CH * (j + 1)], start=True, stop=True)\
                            .then_inc(filled[bank], 1)
                    elif kind == "shift":
                        pe.wait_ge(shift_steps, SHIFTS * (s.batch(1) + 1))
                        for p in range(4):
                            last = nc.tensor.matmul(ring[bank][SPLIT:STACK, p * PQ:(p + 1) * PQ],
                                                    shift[:, 4 * a + p, :], m.identb[0:PQ, 0:PQ],
                                                    start=True, stop=True)
                        last.then_inc(filled[bank], 1)
                        shifts.append((bank, before + 1))
                    elif kind == "turn":
                        k = s.buf(3)
                        if a == 0:
                            if layer:
                                pe.wait_ge(normed, s.batch(3) + 1)
                            else:
                                pe.wait_ge(raw_loaded[k], 32 * (s.use(3) + 1))
                        for c in range(4 * a, 4 * a + 4):
                            rows = rows_of(c)
                            last = nc.tensor.transpose(ring[bank][:, P * (c - 4 * a):P * (c - 4 * a) + rows],
                                                       raw[0:rows, k, c, :], ident[0:rows, 0:rows])
                        last.then_inc(filled[bank], 1)
                    elif kind == "key":
                        if a == 0:
                            last_bank, count = s.last_turn()
                            pe.wait_ge(drained[last_bank], count)
                        nc.tensor.matmul(ring[bank][:, 0:CH], m.wk[layer][:, :], rawT[:, CH * a:CH * (a + 1)],
                                         start=True, stop=True).then_inc(filled[bank], 1)
                    elif kind == "value":
                        for c in range(4 * a, 4 * a + 4):
                            rows = rows_of(c)
                            last = nc.tensor.matmul(ring[bank][0:rows, P * (c - 4 * a):P * (c - 4 * a + 1)],
                                                    rawT[:, P * c:P * c + rows], m.wv[layer][:, :],
                                                    start=True, stop=True)
                        last.then_inc(filled[bank], 1)
                    elif kind == "total":
                        pe.wait_ge(mix_read, s.batch(0))
                        nc.tensor.matmul(ring[bank][:, 0:2 * PQ], mat(m, "pick"), mixed_sb[:, :],
                                         start=True, stop=True).then_inc(filled[bank], 1)
                    elif kind == "project":
                        pe.wait_ge(normalised, s.batch(0))
                        for n in range(4):
                            last = nc.tensor.matmul(ring[bank][0:S, 0:D], heads[:, n // 2, n % 2, :],
                                                    mat(m, f"woh{layer}{'abcd'[n]}"), start=(n == 0), stop=(n == 3))
                        last.then_inc(filled[bank], 1)
                for bank, n in shifts:
                    pe.wait_ge(drained[bank], n)

            run_steps(pe, nb, step)


def ffn_ternary(nc, m):
    nt = m.nt
    gt = min(GT, nt)
    ng = nt // gt
    gc = gt * TOK
    cols = nt * TOK
    with ExitStack() as ctx:
        def sb(name, shape, dt):
            return ctx.enter_context(nc.sbuf_tensor("t_" + name, shape, dt))

        def sem(name):
            return ctx.enter_context(nc.semaphore("t_" + name))

        y = sb("y", [TOK, nt, D], F32)
        z = sb("z", [TOK, nt, D], F32)
        sq = sb("sq", [TOK, nt, D], F32)
        st = sb("st", [TOK, 12, nt], F32)
        qz = sb("qz", [TOK, nt, D], BF16)
        qzT = sb("qzT", [P, cols], BF16)
        w1 = sb("w1", [P, F0], BF16)
        w2 = sb("w2", [P, F0], BF16)
        wr = sb("wr", [P, F0], F32)
        wst = sb("wst", [P, 8], F32)
        ones = sb("ones", [P, P], F32)
        h = sb("h", [TOK, nt, F0], F32)
        hq = sb("hq", [TOK, 2, F0], F32)
        hb = sb("hb", [TOK, 2, F0], BF16)
        hT = sb("hT", [P, 2, FT, TOK], BF16)
        junk = sb("junk", [TOK, F0], F32)
        less_magic = sb("less_magic", [TOK, 1], F32)
        sums = ctx.enter_context(nc.psum_tensor("t_sums", [P, 512], F32))
        turned = [ctx.enter_context(nc.psum_tensor(f"t_turned{i}", [P, 1024], BF16)) for i in range(2)]
        hps = [ctx.enter_context(nc.psum_tensor(f"t_hps{i}", [TOK, F0], F32)) for i in range(2)]
        ops = [ctx.enter_context(nc.psum_tensor(f"t_ops{i}", [TOK, 512], F32)) for i in range(2)]
        y_loaded, chain_sem, roots = sem("y_loaded"), sem("chain"), sem("roots")
        wsum, wready, zturned, zcopied = sem("wsum"), sem("wready"), sem("zturned"), sem("zcopied")
        hid, hid_read, gelus, squares = sem("hid"), sem("hid_read"), sem("gelus"), sem("squares")
        quant, hturned, hcopied, outs, outs_read = sem("quant"), sem("hturned"), sem("hcopied"), sem("outs"), sem("outs_read")
        tok_quant, rounded = sem("tok_quant"), sem("rounded")
        block = ctx.enter_context(nc.Block())

        @block.sync
        def _(sp):
            sp.dma_start(y[:, :, :], m.y_dram.rearrange("b s d -> (b s) d").rearrange("(n p) d -> p n d", p=TOK))\
                .then_inc(y_loaded, 16)

        @block.vector
        def _(dve):
            def out_tile(i):
                dve.wait_ge(outs, i + 1)
                nc.vector.scalar_tensor_tensor(out=y[:, i, :], in0=ops[i % 2][:, 0:D], scalar=st[:, 7, i:i + 1],
                                               in1=row(m, "b2", TOK), op0=ALU.mult, op1=ALU.add).then_inc(outs_read, 1)

            chain = Chain(dve, chain_sem)
            nc.vector.memset(ones[:, :], 1.0).then_inc(wready, 1)
            nc.vector.memset(less_magic[:, :], -MAGIC).then_inc(wready, 1)
            for n, (a, b) in enumerate((("fa", "fd"), ("ga", "gd"))):
                at = MATS.index(a) * P
                nc.vector.tensor_reduce(wst[:, n:n + 1], m.mats[:, at:at + F0], AX.X, ALU.add,
                                        apply_absolute_value=True).then_inc(wready, 1)
            dve.wait_ge(wsum, 1)
            chain.then(nc.vector.tensor_scalar(wst[:, 2:4], sums[:, 0:2], 1.0 / (D * F0), 1e-5, ALU.mult, ALU.max))
            chain.then(nc.vector.reciprocal(wst[:, 4:6], wst[:, 2:4]))
            for n, (w, a) in enumerate(((w1, "fa"), (w2, "ga"))):
                at = MATS.index(a) * P
                chain.then(nc.vector.tensor_scalar(wr[:, :], m.mats[:, at:at + F0], wst[:, 4 + n:5 + n], 1.0,
                                                   ALU.mult, ALU.min))
                chain.then(nc.vector.tensor_scalar(wr[:, :], wr[:, :], -1.0, MAGIC, ALU.max, ALU.add))
                chain.then(nc.vector.tensor_scalar(w[:, :], wr[:, :], MAGIC, None, ALU.subtract))
            dve.wait_ge(y_loaded, 16)
            chain.then(nc.vector.tensor_tensor(y[:, :, :], y[:, :, :], per_channel(m.yb[0][:, :], nt), ALU.add))
            chain.then(nc.vector.scalar_tensor_tensor(out=m.x[:, :, :], in0=y[:, :, :], scalar=m.gates[0:TOK, 0:1],
                                                      in1=m.x[:, :, :], op0=ALU.mult, op1=ALU.add))
            norm_vector(nc, dve, chain, roots, m.x[:, :, :], z[:, :, :], sq[:, :, :], st, nt, 0)
            chain.then(nc.vector.tensor_tensor(sq[:, :, :], z[:, :, :], z[:, :, :], ALU.mult))
            chain.then(nc.vector.tensor_reduce(st[:, 2, :], sq[:, :, :], AX.X, ALU.add))
            dve.wait_ge(roots, 3)
            chain.then(nc.vector.reciprocal(st[:, 4, :], st[:, 3, :]))
            chain.then(nc.vector.tensor_tensor(z[:, :, :], z[:, :, :], per_token(st[:, 4, :], nt), ALU.mult))
            chain.then(nc.vector.tensor_reduce(st[:, 5, :], z[:, :, :], AX.X, ALU.max, apply_absolute_value=True))
            chain.then(nc.vector.tensor_scalar(st[:, 5, :], st[:, 5, :], 1e-5, 1.0 / 127.0, ALU.max, ALU.mult))
            chain.then(nc.vector.reciprocal(st[:, 6, :], st[:, 5, :]))
            chain.then(nc.vector.tensor_tensor(z[:, :, :], z[:, :, :], per_token(st[:, 6, :], nt), ALU.mult))
            chain.then(nc.vector.tensor_scalar(z[:, :, :], z[:, :, :], 127.0, -128.0, ALU.min, ALU.max))
            chain.then(nc.vector.tensor_scalar(z[:, :, :], z[:, :, :], MAGIC, MAGIC, ALU.add, ALU.subtract))
            nc.vector.tensor_copy(qz[:, :, :], z[:, :, :]).then_inc(tok_quant, 1)
            chain.then(nc.vector.tensor_scalar(st[:, 7, :], st[:, 5, :], wst[0:TOK, 2:3], None, ALU.mult))
            for g in range(ng):
                dve.wait_ge(zturned, g + 1)
                nc.vector.tensor_copy(qzT[:, g * gc:(g + 1) * gc], turned[g % 2][:, 0:gc]).then_inc(zcopied, 1)
            for i in range(nt):
                dve.wait_ge(hid, i + 1)
                nc.vector.scalar_tensor_tensor(out=h[:, i, :], in0=hps[i % 2][:, :], scalar=st[:, 7, i:i + 1],
                                               in1=row(m, "b1", TOK), op0=ALU.mult, op1=ALU.add).then_inc(hid_read, 1)
            for i in range(nt):
                dve.wait_ge(gelus, i + 1)
                last = nc.vector.tensor_reduce(st[:, 8, i:i + 1], h[:, i, :], AX.X, ALU.max,
                                               apply_absolute_value=True)
            chain.then(last)
            dve.wait_ge(roots, 4)
            chain.then(nc.vector.reciprocal(st[:, 4, :], st[:, 3, :]))
            chain.then(nc.vector.tensor_tensor(st[:, 8, :], st[:, 8, :], st[:, 4, :], ALU.mult))
            chain.then(nc.vector.tensor_scalar(st[:, 5, :], st[:, 8, :], 1e-5, 1.0 / 127.0, ALU.max, ALU.mult))
            chain.then(nc.vector.reciprocal(st[:, 6, :], st[:, 5, :]))
            chain.then(nc.vector.tensor_tensor(st[:, 6, :], st[:, 6, :], st[:, 4, :], ALU.mult))
            chain.then(nc.vector.tensor_scalar(st[:, 7, :], st[:, 5, :], wst[0:TOK, 3:4], None, ALU.mult))
            for i in range(nt):
                u = i % 2
                if i >= 2:
                    dve.wait_ge(quant, i - 1)
                chain.then(nc.vector.tensor_scalar(hq[:, u, :], h[:, i, :], st[:, 6, i:i + 1], 127.0, ALU.mult, ALU.min))
                nc.vector.tensor_scalar(hq[:, u, :], hq[:, u, :], -128.0, MAGIC, ALU.max, ALU.add).then_inc(rounded, 1)
                if i >= 2:
                    out_tile(i - 2)
            out_tile(nt - 2)
            out_tile(nt - 1)
            dve.wait_ge(outs_read, nt)
            chain.then(nc.vector.scalar_tensor_tensor(out=m.x[:, :, :], in0=y[:, :, :], scalar=m.gates[0:TOK, 2:3],
                                                      in1=m.x[:, :, :], op0=ALU.mult, op1=ALU.add))

        links_before = 2 + 6 + 2

        @block.scalar
        def _(act):
            norm_scalar(nc, act, m, chain_sem, links_before, roots, m.x, z, st, nt)
            act.wait_ge(chain_sem, links_before + NORM_LINKS + 2)
            nc.scalar.activation(st[:, 3, :], st[:, 2, :], ACT.Sqrt, bias=m.eps[0:TOK, 0:1], scale=1.0 / D)\
                .then_inc(roots, 1)
            for i in range(nt):
                act.wait_ge(hid_read, i + 1)
                nc.scalar.activation(h[:, i, :], h[:, i, :], ACT.Gelu).then_inc(gelus, 1)
            act.wait_ge(gelus, nt)
            for i in range(nt):
                nc.scalar.activation(junk[:, :], h[:, i, :], ACT.Square, accum_out=st[:, 9, i:i + 1])\
                    .then_inc(squares, 1)
                act.wait_ge(squares, i + 1)
            nc.scalar.activation(st[:, 3, :], st[:, 9, :], ACT.Sqrt, bias=m.eps[0:TOK, 0:1], scale=1.0 / F0)\
                .then_inc(roots, 1)

            def turned_tile(i):
                act.wait_ge(hturned, i + 1)
                if i >= 2:
                    act.wait_ge(outs, i - 1)
                nc.scalar.activation(hT[:, i % 2, :, :].rearrange("p f t -> p (f t)"), turned[i % 2][:, 0:FT * TOK],
                                     ACT.Copy).then_inc(hcopied, 1)

            act.wait_ge(wready, 4)
            for i in range(nt):
                act.wait_ge(rounded, i + 1)
                if i >= 2:
                    act.wait_ge(hturned, i - 1)
                nc.scalar.activation(hb[:, i % 2, :], hq[:, i % 2, :], ACT.Identity, bias=less_magic[:, 0:1])\
                    .then_inc(quant, 1)
                if i:
                    turned_tile(i - 1)
            turned_tile(nt - 1)

        @block.tensor
        def _(pe):
            def second(i):
                pe.wait_ge(hcopied, i + 1)
                if i >= 2:
                    pe.wait_ge(outs_read, i - 1)
                for f in range(FT):
                    last = nc.tensor.matmul(ops[i % 2][:, 0:D], hT[:, i % 2, f, :], w2[:, f * P:(f + 1) * P],
                                            start=(f == 0), stop=(f == FT - 1))
                last.then_inc(outs, 1)

            pe.wait_ge(wready, 4)
            nc.tensor.matmul(sums[:, 0:2], ones[:, :], wst[:, 0:2], start=True, stop=True).then_inc(wsum, 1)
            pe.wait_ge(tok_quant, 1)
            for g in range(ng):
                if g >= 2:
                    pe.wait_ge(zcopied, g - 1)
                for i in range(gt):
                    last = nc.tensor.transpose(turned[g % 2][:, i * TOK:(i + 1) * TOK], qz[:, g * gt + i, :],
                                               m.identb[0:TOK, 0:TOK])
                last.then_inc(zturned, 1)
            pe.wait_ge(chain_sem, 8)
            for i in range(nt):
                pe.wait_ge(zcopied, i // gt + 1)
                if i >= 2:
                    pe.wait_ge(hid_read, i - 1)
                nc.tensor.matmul(hps[i % 2][:, :], qzT[:, i * TOK:(i + 1) * TOK], w1[:, :], start=True, stop=True)\
                    .then_inc(hid, 1)
            for i in range(nt):
                pe.wait_ge(quant, i + 1)
                pe.wait_ge(zcopied, ng)
                if i >= 2:
                    pe.wait_ge(hcopied, i - 1)
                for f in range(FT):
                    last = nc.tensor.transpose(turned[i % 2][:, f * TOK:(f + 1) * TOK], hb[:, i % 2, f * P:(f + 1) * P],
                                               m.identb[0:TOK, 0:TOK])
                last.then_inc(hturned, 1)
                if i:
                    second(i - 1)
            second(nt - 1)


def ffn_experts(nc, m):
    nt = m.nt
    gt = min(GT, nt)
    ng = nt // gt
    gc = gt * TOK
    cols = nt * TOK
    PER = FT * ng
    HB = 4
    AHEAD = 2
    with ExitStack() as ctx:
        def sb(name, shape, dt):
            return ctx.enter_context(nc.sbuf_tensor("e_" + name, shape, dt))

        def sem(name):
            return ctx.enter_context(nc.semaphore("e_" + name))

        y = sb("y", [TOK, nt, D], F32)
        n1 = sb("n1", [TOK, nt, D], F32)
        sq = sb("sq", [TOK, nt, D], F32)
        st = sb("st", [TOK, 6, nt], F32)
        x1 = sb("x1", [TOK, nt, D], F32)
        nT = sb("nT", [P, cols], F32)
        pr = sb("pr", [TOK, 6, nt, E], F32)
        top = sb("top", [TOK, 3, nt], F32)
        order = sb("order", [TOK, E], F32)
        shifts = sb("shifts", [TOK, D], F32)
        ind = sb("ind", [E, cols], F32)
        w1 = sb("w1", [P, 2, F0], F32)
        w2 = sb("w2", [P, 2, F0], F32)
        b1 = sb("b1", [P, 2, FT], F32)
        comb = sb("comb", [P, 2, cols], F32)
        hid = sb("hid", [P, HB, GC], F32)
        hw = sb("hw", [P, HB, GC], F32)
        oT = sb("oT", [P, cols], F32)
        acc = [ctx.enter_context(nc.psum_tensor(f"e_acc{g}", [P, 512], F32)) for g in range(ng)]
        ps = [ctx.enter_context(nc.psum_tensor(f"e_ps{i}", [P, 512], F32)) for i in range(HB)]
        pl = ps[HB - 1]
        y_loaded, chain_sem, roots = sem("y_loaded"), sem("chain"), sem("roots")
        turned, copied, mixed, mixed_read = sem("turned"), sem("copied"), sem("mixed"), sem("mixed_read")
        routed, chosen, comb_saved, comb_turned = sem("routed"), sem("chosen"), sem("comb_saved"), sem("comb_turned")
        comb_copied = sem("comb_copied")
        loaded = [sem("loaded0"), sem("loaded1")]
        hidden, silus, weighted, added = sem("hidden"), sem("silus"), sem("weighted"), sem("added")
        acc_read, back, outed, out_saved = sem("acc_read"), sem("back"), sem("outed"), sem("out_saved")
        ex = sem("ex")
        block = ctx.enter_context(nc.Block())

        @block.sync
        def _(sp):
            sp.dma_start(y[:, :, :], m.y_dram.rearrange("b s d -> (b s) d").rearrange("(n p) d -> p n d", p=TOK))\
                .then_inc(y_loaded, 16)
            def weights(e, u):
                sp.dma_start(w1[:, u, :], m.w1_dram[e]).then_inc(loaded[u], 16)
                sp.dma_start(w2[:, u, :], m.w2_dram[e]).then_inc(loaded[u], 16)
                sp.dma_start(b1[:, u, :], m.b1_dram[e]).then_inc(loaded[u], 16)

            def shares(e, u):
                sp.dma_start(comb[:, u, :], m.comb_dram[e].partition_broadcast(P)).then_inc(loaded[u], 16)

            weights(0, 0)
            weights(1, 1)
            sp.wait_ge(comb_copied, ng)
            sp.dma_start(m.comb_dram, ind[:, :]).then_inc(comb_saved, 16)
            sp.wait_ge(comb_saved, 16)
            shares(0, 0)
            shares(1, 1)
            with sp.Fori(1, E // 2) as lap:
                for u in range(2):
                    sp.wait_ge(added, 2 * PER * lap + PER * u)
                    weights(2 * lap + u, u)
                    shares(2 * lap + u, u)
            sp.wait_ge(outed, ng + 1)
            sp.dma_start(m.out_dram.rearrange("b s d -> (b s) d").rearrange("(n p) d -> p n d", p=TOK), m.x[:, :, :])\
                .then_inc(out_saved, 16)
            sp.wait_ge(out_saved, 16)

        @block.vector
        def _(dve):
            chain = Chain(dve, chain_sem)
            for e in range(E):
                last = nc.vector.memset(order[:, e:e + 1], float(E - e))
            dve.wait_ge(y_loaded, 16)
            chain.then(nc.vector.tensor_tensor(y[:, :, :], y[:, :, :], per_channel(m.yb[1][:, :], nt), ALU.add))
            chain.then(nc.vector.scalar_tensor_tensor(out=m.x[:, :, :], in0=y[:, :, :], scalar=m.gates[0:TOK, 1:2],
                                                      in1=m.x[:, :, :], op0=ALU.mult, op1=ALU.add))
            norm_vector(nc, dve, chain, roots, m.x[:, :, :], x1[:, :, :], sq[:, :, :], st, nt, 0)
            norm_vector(nc, dve, chain, roots, x1[:, :, :], n1[:, :, :], sq[:, :, :], st, nt, 2)
            chain.mark(nc.vector.tensor_tensor(sq[:, :, :], n1[:, :, :], per_channel(row(m, "g1", TOK), nt), ALU.mult))
            chain.then(nc.vector.tensor_tensor(shifts[:, :], row(m, "be1", TOK), row(m, "mix_b", TOK), ALU.add))
            chain.then(nc.vector.tensor_tensor(x1[:, :, :], x1[:, :, :], sq[:, :, :], ALU.add))
            chain.then(nc.vector.tensor_tensor(x1[:, :, :], x1[:, :, :], per_channel(shifts[:, :], nt), ALU.add))
            for g in range(ng):
                dve.wait_ge(mixed, g + 1)
                nc.vector.tensor_tensor(x1[:, g * gt:(g + 1) * gt, :], x1[:, g * gt:(g + 1) * gt, :],
                                        acc[g][0:TOK, 0:gt * D].rearrange("p (i d) -> p i d", i=gt), ALU.add)\
                    .then_inc(mixed_read, 1)
            dve.wait_ge(mixed_read, ng)
            norm_vector(nc, dve, chain, roots, x1[:, :, :], n1[:, :, :], sq[:, :, :], st, nt, 4)
            dve.wait_ge(routed, 1)
            logits = pl[0:TOK, 0:nt * E].rearrange("p (i e) -> p i e", e=E)

            def spread(ap):
                return per_token(ap, nt, E)

            chain.then(nc.vector.tensor_reduce(top[:, 0, :], logits, AX.X, ALU.max))
            nc.vector.tensor_tensor(pr[:, 0, :, :], logits, spread(top[:, 0, :]), ALU.subtract).then_inc(ex, 1)
            dve.wait_ge(ex, 2)
            chain.then(nc.vector.tensor_reduce(top[:, 1, :], pr[:, 1, :, :], AX.X, ALU.add))
            chain.then(nc.vector.reciprocal(top[:, 2, :], top[:, 1, :]))
            chain.then(nc.vector.tensor_tensor(pr[:, 0, :, :], pr[:, 1, :, :], spread(top[:, 2, :]), ALU.mult))
            chain.then(nc.vector.tensor_copy(pr[:, 5, :, :], pr[:, 0, :, :]))
            for n in (3, 4):
                chain.then(nc.vector.tensor_reduce(top[:, 0, :], pr[:, 5, :, :], AX.X, ALU.max))
                chain.then(nc.vector.tensor_tensor(pr[:, 2, :, :], pr[:, 5, :, :], spread(top[:, 0, :]), ALU.is_equal))
                chain.then(nc.vector.tensor_tensor(pr[:, 2, :, :], pr[:, 2, :, :],
                                                   order[:, :].unsqueeze(1).to_broadcast([TOK, nt, E]), ALU.mult))
                chain.then(nc.vector.tensor_reduce(top[:, 1, :], pr[:, 2, :, :], AX.X, ALU.max))
                chain.then(nc.vector.tensor_tensor(pr[:, n, :, :], pr[:, 2, :, :], spread(top[:, 1, :]), ALU.is_equal))
                if n == 3:
                    chain.then(nc.vector.scalar_tensor_tensor(
                        out=pr[:, 5, :, :], in0=pr[:, 3, :, :], scalar=-2.0, in1=pr[:, 5, :, :],
                        op0=ALU.mult, op1=ALU.add))
            chain.then(nc.vector.tensor_tensor(pr[:, 3, :, :], pr[:, 3, :, :], pr[:, 4, :, :], ALU.add))
            nc.vector.tensor_tensor(pr[:, 2, :, :], pr[:, 3, :, :], pr[:, 0, :, :], ALU.mult).then_inc(chosen, 1)
            dve.sem_inc(weighted, HB)
            with dve.Fori(0, E // 2) as lap:
                for u in range(2):
                    dve.wait_ge(loaded[u], 64 * lap + 64)
                    for f in range(FT):
                        for g in range(ng):
                            n = PER * u + f * ng + g
                            at = 2 * PER * lap + n
                            dve.wait_ge(silus, at + 1 + HB)
                            dve.wait_ge(added, at + 1 - HB + PER)
                            nc.vector.tensor_tensor(hw[:, n % HB, 0:gc], hid[:, n % HB, 0:gc],
                                                    comb[:, u, g * gc:(g + 1) * gc], ALU.mult).then_inc(weighted, 1)
            for g in range(ng):
                dve.wait_ge(back, g + 1)
                nc.vector.tensor_tensor(x1[:, g * gt:(g + 1) * gt, :], x1[:, g * gt:(g + 1) * gt, :],
                                        ps[g % 2][0:TOK, 0:gt * D].rearrange("p (i d) -> p i d", i=gt), ALU.add)\
                    .then_inc(outed, 1)
            dve.wait_ge(outed, ng)
            nc.vector.scalar_tensor_tensor(out=m.x[:, :, :], in0=x1[:, :, :], scalar=m.gates[0:TOK, 3:4],
                                           in1=m.x[:, :, :], op0=ALU.mult, op1=ALU.add).then_inc(outed, 1)

        first_norm = 2
        second_norm = first_norm + 2 * NORM_LINKS + 4

        @block.scalar
        def _(act):
            norm_scalar(nc, act, m, chain_sem, first_norm, roots, m.x, x1, st, nt)
            norm_scalar(nc, act, m, chain_sem, first_norm + NORM_LINKS, roots, x1, n1, st, nt)
            for g in range(ng):
                act.wait_ge(turned, g + 1)
                nc.scalar.activation(nT[:, g * gc:(g + 1) * gc], ps[g % 2][:, 0:gc], ACT.Identity,
                                     bias=col(m, "be1"), scale=col(m, "g1")).then_inc(copied, 1)
            norm_scalar(nc, act, m, chain_sem, second_norm, roots, x1, n1, st, nt)
            for g in range(ng):
                act.wait_ge(turned, ng + g + 1)
                nc.scalar.activation(nT[:, g * gc:(g + 1) * gc], ps[g % 2][:, 0:gc], ACT.Identity,
                                     bias=col(m, "be2"), scale=col(m, "g2")).then_inc(copied, 1)
            act.wait_ge(ex, 1)
            nc.scalar.activation(pr[:, 1, :, :], pr[:, 0, :, :], ACT.Exp).then_inc(ex, 1)
            for g in range(ng):
                act.wait_ge(comb_turned, g + 1)
                nc.scalar.activation(ind[:, g * gc:(g + 1) * gc], ps[g % 2][0:E, 0:gc], ACT.Copy).then_inc(comb_copied, 1)
            act.sem_inc(silus, HB)
            with act.Fori(0, E // 2) as lap:
                for u in range(2):
                    act.wait_ge(loaded[u], 64 * lap + 64)
                    for f in range(FT):
                        for g in range(ng):
                            n = PER * u + f * ng + g
                            at = 2 * PER * lap + n
                            act.wait_ge(hidden, at + 1)
                            act.wait_ge(weighted, at + 1)
                            nc.scalar.activation(hid[:, n % HB, 0:gc], ps[n % HB][:, 0:gc], ACT.Silu,
                                                 bias=b1[:, u, f:f + 1]).then_inc(silus, 1)
            act.wait_ge(added, PER + E * PER)
            for g in range(ng):
                nc.scalar.activation(oT[:, g * gc:(g + 1) * gc], acc[g][:, 0:gc], ACT.Copy).then_inc(acc_read, 1)

        @block.tensor
        def _(pe):
            ident = mat(m, "ident")

            def turn(base):
                for g in range(ng):
                    if g >= 2:
                        pe.wait_ge(copied, base + g - 1)
                    for i in range(gt):
                        last = nc.tensor.transpose(ps[g % 2][:, i * TOK:(i + 1) * TOK], n1[:, g * gt + i, :],
                                                   ident[0:TOK, 0:TOK])
                    last.then_inc(turned, 1)

            pe.wait_ge(chain_sem, first_norm + 2 * NORM_LINKS)
            turn(0)
            for g in range(ng):
                pe.wait_ge(copied, g + 1)
                for i in range(gt):
                    at = (g * gt + i) * TOK
                    last = nc.tensor.matmul(acc[g][0:TOK, i * D:(i + 1) * D], nT[:, at:at + TOK], mat(m, "mix"),
                                            start=True, stop=True)
                last.then_inc(mixed, 1)
            pe.wait_ge(chain_sem, second_norm + NORM_LINKS)
            pe.wait_ge(copied, ng)
            turn(ng)
            pe.wait_ge(copied, 2 * ng)
            for i in range(nt):
                last = nc.tensor.matmul(pl[0:TOK, i * E:(i + 1) * E], nT[:, i * TOK:(i + 1) * TOK], m.router[:, :],
                                        start=True, stop=True)
            last.then_inc(routed, 1)
            pe.wait_ge(chosen, 1)
            for g in range(ng):
                if g >= 2:
                    pe.wait_ge(comb_copied, g - 1)
                for i in range(gt):
                    last = nc.tensor.transpose(ps[g % 2][0:E, i * TOK:(i + 1) * TOK], pr[:, 2, g * gt + i, :],
                                               ident[0:TOK, 0:TOK])
                last.then_inc(comb_turned, 1)
            pe.wait_ge(comb_copied, ng)
            pe.wait_ge(mixed_read, ng)
            for g in range(ng):
                nc.tensor.matmul(acc[g][:, 0:gc], m.b2e[:, :], ind[:, g * gc:(g + 1) * gc], start=True, stop=False,
                                 skip_group_check=True)

            pe.sem_inc(added, PER)

            def first(lap, n):
                u, f, g = n // PER, (n // ng) % FT, n % ng
                if n == PER * u:
                    pe.wait_ge(loaded[u], 64 * lap + 64)
                pe.wait_ge(silus, 2 * PER * lap + n + 1)
                nc.tensor.matmul(ps[n % HB][:, 0:gc], w1[:, u, f * P:(f + 1) * P], nT[:, g * gc:(g + 1) * gc],
                                 start=True, stop=True).then_inc(hidden, 1)

            def second(lap, n):
                u, f, g = n // PER, (n // ng) % FT, n % ng
                pe.wait_ge(weighted, 2 * PER * lap + n + 1 + HB)
                nc.tensor.matmul(acc[g][:, 0:gc], w2[:, u, f * P:(f + 1) * P], hw[:, n % HB, 0:gc],
                                 start=False, stop=True, skip_group_check=True).then_inc(added, 1)

            def two_experts(lap, more):
                for n in range(2 * PER):
                    if n + AHEAD < 2 * PER:
                        first(lap, n + AHEAD)
                    elif more:
                        first(lap + 1, n + AHEAD - 2 * PER)
                    second(lap, n)

            for n in range(AHEAD):
                first(0, n)
            with pe.Fori(0, E // 2 - 1) as lap:
                two_experts(lap, True)
            two_experts(E // 2 - 1, False)
            for g in range(ng):
                pe.wait_ge(acc_read, g + 1)
                if g >= 2:
                    pe.wait_ge(outed, g - 1)
                for i in range(gt):
                    at = (g * gt + i) * TOK
                    last = nc.tensor.transpose(ps[g % 2][0:TOK, i * D:(i + 1) * D], oT[:, at:at + TOK], ident)
                last.then_inc(back, 1)


def program(nc, nb, x_dram, ctx_dram, mask_dram, mats_dram, cols_dram, rows_dram, router_dram, b2e_dram,
            w1_dram, w2_dram, b1_dram, out_dram):
    nt = nb // 2
    with ExitStack() as ctx:
        def sb(name, shape, dt):
            return ctx.enter_context(nc.sbuf_tensor(name, shape, dt))

        def dram(name, shape, dt):
            return nc.dram_tensor(name, shape, dt, kind="Internal").ap()

        m = Shared()
        m.nb = nb
        m.nt = nt
        m.x_dram = x_dram
        m.ctx_dram = ctx_dram
        m.mask_dram = mask_dram
        m.mats_dram = mats_dram
        m.cols_dram = cols_dram
        m.rows_dram = rows_dram
        m.router_dram = router_dram
        m.b2e_dram = b2e_dram
        m.w1_dram = w1_dram
        m.w2_dram = w2_dram
        m.b1_dram = b1_dram
        m.out_dram = out_dram
        m.stats_dram = dram("stats_scratch", [P, nb, KT * 6], F32)
        m.norms_dram = dram("norms_scratch", [P, nb, 2 * KT], F32)
        m.keep_dram = dram("keep_scratch", [nb, CTX], BF16)
        m.fill_dram = dram("fill_scratch", [nb, 3, CTX], BF16)
        m.q_dram = dram("q_scratch", [3, PR, PAIRS, nb, PQ], BF16)
        m.k_dram = dram("k_scratch", [3, 3, PR, PAIRS, CTX], BF16)
        m.y_dram = dram("y_scratch", [nb, S, D], F32)
        m.comb_dram = dram("comb_scratch", [E, nb * S], F32)
        m.x = sb("x", [TOK, nt, D], F32)
        m.mats = sb("mats", [P, len(MATS) * P], F32)
        m.cols = sb("cols", [P, len(COLS)], F32)
        m.rows = sb("rows", [P, ROW_W], F32)
        m.router = sb("router", [P, E], F32)
        m.b2e = sb("b2e", [E, D], F32)
        m.identb = sb("identb", [P, P], BF16)
        m.gates = sb("gates", [P, 4], F32)
        m.eps = sb("eps", [P, 1], F32)
        m.wk = [sb("wk_0", [P, P], F32), sb("wk_1", [P, P], F32)]
        m.wv = [sb("wv_0", [P, P], F32), sb("wv_1", [P, P], F32)]
        m.bk = [sb("bk_0", [P, 1], F32), sb("bk_1", [P, 1], F32)]
        m.yb = [sb("yb_0", [TOK, D], F32), sb("yb_1", [TOK, D], F32)]
        m.weights_loaded = ctx.enter_context(nc.semaphore("weights_loaded"))
        m.masks_saved = ctx.enter_context(nc.semaphore("masks_saved"))
        with ExitStack() as early:
            setup(nc, m, early)
            queries(nc, m, 0)
        attention(nc, m, 0)
        ffn_ternary(nc, m)
        queries(nc, m, 1)
        attention(nc, m, 1)
        ffn_experts(nc, m)


def layouts(inputs):
    import numpy as np

    a = {k: np.asarray(v) for k, v in inputs.items()}
    f = np.float32
    mats = {
        "wq0": a["L0_xattn_Wq"].T, "wk0": a["L0_xattn_Wk"].T, "wv0": a["L0_xattn_Wv"].T, "wo0": a["L0_xattn_Wo"].T,
        "wq1": a["L1_xattn_w_q"], "wk1": a["L1_xattn_w_kv"][:, :D], "wv1": a["L1_xattn_w_kv"][:, D:],
        "wo1": a["L1_xattn_w_proj"], "mix": a["L1_ffn_mix_w"], "ident": np.eye(P, dtype=f),
    }
    pick = np.zeros((P, P), f)
    for i in range(P):
        pick[i // 32 * 32 + PR, i] = 1.0
    mats["pick"] = pick
    for layer in range(2):
        wo = mats[f"wo{layer}"]
        for n in range(4):
            r, odd = n // 2, n % 2
            w = np.zeros((P, P), f)
            for q in range(4):
                h = 2 * (4 * r + q) + odd
                w[32 * q + HD * odd:32 * q + HD * odd + HD] = wo[h * HD:(h + 1) * HD]
            mats[f"woh{layer}{'abcd'[n]}"] = w
    w1 = a["L0_ffn_w1"].T
    w2 = a["L0_ffn_w2"].T
    for n in range(4):
        mats["f" + "abcd"[n]] = w1[:, n * P:(n + 1) * P]
        mats["g" + "abcd"[n]] = w2[n * P:(n + 1) * P, :]
    parity = (np.arange(P) // HD) % 2
    cols = {
        "g1": a["L1_ffn_g1"], "be1": a["L1_ffn_be1"], "bq0": a["L0_xattn_bq"], "bk0": a["L0_xattn_bk"], "bv0": a["L0_xattn_bv"], "g_x": a["L1_xattn_g_x"],
        "b_x": a["L1_xattn_b_x"], "g_kv": a["L1_xattn_g_kv"], "b_kv": a["L1_xattn_b_kv"], "g2": a["L1_ffn_g2"],
        "be2": a["L1_ffn_be2"], "even": (1 - parity).astype(f), "odd": parity.astype(f),
    }
    rows = {
        "bo0": a["L0_xattn_bo"], "b2": a["L0_ffn_b2"], "b1": a["L0_ffn_b1"], "bo1": a["L1_xattn_b_proj"],
        "g1": a["L1_ffn_g1"], "be1": a["L1_ffn_be1"], "mix_b": a["L1_ffn_mix_b"],
        "gates": np.concatenate([a["g_xattn"], a["g_ffn"]]),
    }
    out = {
        "x": a["x"], "ctx": a["ctx_1024"], "mask": a["mask_BxS2_ik0"],
        "mats": np.concatenate([mats[k] for k in MATS], axis=1),
        "cols": np.stack([cols[k] for k in COLS], axis=1),
        "rows": np.concatenate([rows[k] for k, _ in ROWS]),
        "router": a["L1_ffn_router_w"], "b2e": a["L1_ffn_b2"],
        "w1": a["L1_ffn_w1"],
        "w2": a["L1_ffn_w2"].reshape(E, FT, P, D).transpose(0, 2, 1, 3).reshape(E, P, FT * D),
        "b1": a["L1_ffn_b1"].reshape(E, FT, P).transpose(0, 2, 1),
    }
    return {k: np.ascontiguousarray(v) for k, v in out.items()}


def kernel(**inputs):
    import concourse.bacc as bacc
    from concourse.bass_utils import run_bass_kernel_spmd

    arrays = layouts(inputs)
    nb = arrays["x"].shape[0]
    nc = bacc.Bacc("TRN2", target_bir_lowering=False, num_devices=1)
    args = {f"{k}_dram": nc.dram_tensor(f"in_{k}", v.shape, mybir.dt.from_np(v.dtype), kind="ExternalInput").ap()
            for k, v in arrays.items()}
    out = nc.dram_tensor("out_x", (nb, S, D), F32, kind="ExternalOutput").ap()
    program(nc, nb, out_dram=out, **args)
    r = run_bass_kernel_spmd(nc, [{f"in_{k}": v for k, v in arrays.items()}], core_ids=[0])
    return r.results[0]["out_x"]
```
